# Optimizing a Trainium2 kernel written in Bass

```python
import numpy as np
import jax
import jax.numpy as jnp

def _softmax(x, axis=-1):
    return jax.nn.softmax(x, axis=axis)

def _gelu(x):
    return jax.nn.gelu(x, approximate=True)

def _silu(x):
    return jax.nn.silu(x)

def _sigmoid(x):
    return jax.nn.sigmoid(x)

def _layernorm(x, axis=-1, eps=1e-05):
    m = jnp.mean(x, axis=axis, keepdims=True)
    v = jnp.var(x, axis=axis, keepdims=True)
    return (x - m) / jnp.sqrt(v + eps)

def _scatter_add(tgt, idx, src, axis=0):
    return tgt.at[idx].add(src)

def _segment_sum(src, seg, n):
    return jax.ops.segment_sum(src, seg, n)
kernel_name = 'mk_hybrid_d1_jaxref_r8_c4e386'

def setup_inputs(seed: int=0):
    np.random.seed(seed)
    _w = jnp.asarray

    def _L0_attn_a_setup():
        import jax, jax.numpy as jnp
        import numpy as np
        import math
        N_HEAD = 16
        DEG = 2
        EPS = 1e-07
        key = jax.random.key(seed)
        k1, k2 = jax.random.split(key)
        B, T, C = (2, 256, 128)
        x = jax.random.normal(k1, (B, T, C), dtype=jnp.float32)
        W = jax.random.normal(k2, (3 * C + N_HEAD, C), dtype=jnp.float32) * (1.0 / math.sqrt(C))
        return {'x': x, 'W': W}
    _L0_attn_a_in = _L0_attn_a_setup()

    def _L0_attn_b_setup():
        import jax, jax.numpy as jnp
        import numpy as np
        B, N, D, H = (2, 256, 128, 16)
        HD = D // H

        def l2norm(x, eps=1e-12):
            n = jnp.sqrt(jnp.sum(x * x, axis=-1, keepdims=True))
            return x / jnp.maximum(n, eps)

        def dplr_delta_rule(q, k, v, a, gk):
            qm, km, vm, am, gm = (jnp.moveaxis(t, 1, 0) for t in (q, k, v, a, gk))

            def step(S, inp):
                qt, kt, vt, at, gkt = inp
                Sp = S * jnp.exp(gkt)[..., None]
                u = jnp.einsum('bhk,bhkv->bhv', at, Sp) + vt
                S = Sp + jnp.einsum('bhk,bhv->bhkv', kt, u)
                o = jnp.einsum('bhk,bhkv->bhv', qt, S)
                return (S, o)
            S0 = jnp.zeros((q.shape[0], q.shape[2], q.shape[3], v.shape[3]), q.dtype)
            _, o = jax.lax.scan(step, S0, (qm, km, vm, am, gm))
            return jnp.moveaxis(o, 0, 1)

        def _forward(x, Wq, Wk, Wv, Wgamma, Wf, Wg1, Wg2, Wo, norm_w):
            b, n, d = x.shape
            silu = jax.nn.silu
            q = silu(x @ Wq)
            k = silu(x @ Wk)
            v = silu(x @ Wv)
            log_f = jax.nn.log_sigmoid(x @ Wf)
            gamma = -jax.nn.sigmoid(x @ Wgamma)
            q = q.reshape(b, n, H, HD)
            k = l2norm(k.reshape(b, n, H, HD))
            v = v.reshape(b, n, H, HD)
            gk = jnp.broadcast_to(log_f[..., None], (b, n, H, HD))
            a = k * gamma[..., None] * jnp.exp(gk)
            out = dplr_delta_rule(q, k, v, a, gk)
            out = out.reshape(b, n, d)
            gate = jax.nn.sigmoid(x @ Wg1 @ Wg2)
            out = out * gate
            mu = jnp.mean(out, axis=-1, keepdims=True)
            var = jnp.mean(jnp.square(out - mu), axis=-1, keepdims=True)
            out = (out - mu) * jax.lax.rsqrt(var + 1e-05) * norm_w
            return out @ Wo
        key = jax.random.key(seed)
        ks = jax.random.split(key, 10)
        s = 0.02
        return {'x': jax.random.normal(ks[0], (B, N, D), jnp.float32), 'Wq': jax.random.normal(ks[1], (D, D), jnp.float32) * s, 'Wk': jax.random.normal(ks[2], (D, D), jnp.float32) * s, 'Wv': jax.random.normal(ks[3], (D, D), jnp.float32) * s, 'Wgamma': jax.random.normal(ks[4], (D, H), jnp.float32) * s, 'Wf': jax.random.normal(ks[5], (D, H), jnp.float32) * s, 'Wg1': jax.random.normal(ks[6], (D, HD), jnp.float32) * s, 'Wg2': jax.random.normal(ks[7], (HD, D), jnp.float32) * s, 'Wo': jax.random.normal(ks[8], (D, D), jnp.float32) * s, 'norm_w': jnp.ones((D,), jnp.float32)}
    _L0_attn_b_in = _L0_attn_b_setup()

    def _L0_ffn_setup():
        import jax, jax.numpy as jnp
        import numpy as np
        E, D, F, GATE_DIM = (8, 128, 512, 16)
        B, T = (2, 256)
        key = jax.random.key(seed)
        ks = jax.random.split(key, 7)
        s = 0.02
        return {'hidden_states': jax.random.normal(ks[0], (B, T, D), dtype=jnp.float32), 'w_red': jax.random.normal(ks[1], (D, GATE_DIM), dtype=jnp.float32) * s, 'wg': jax.random.normal(ks[2], (E, GATE_DIM), dtype=jnp.float32), 'w1': jax.random.normal(ks[3], (E, D, F), dtype=jnp.float32) * s, 'b1': jax.random.normal(ks[4], (E, F), dtype=jnp.float32) * s, 'w2': jax.random.normal(ks[5], (E, F, D), dtype=jnp.float32) * s, 'b2': jax.random.normal(ks[6], (E, D), dtype=jnp.float32) * s}
    _L0_ffn_in = _L0_ffn_setup()
    _d = {'L0_attn_a_x': _L0_attn_a_in['x'], 'L0_attn_a_W': _L0_attn_a_in['W'], 'L0_attn_b_Wq': _L0_attn_b_in['Wq'], 'L0_attn_b_Wk': _L0_attn_b_in['Wk'], 'L0_attn_b_Wv': _L0_attn_b_in['Wv'], 'L0_attn_b_Wgamma': _L0_attn_b_in['Wgamma'], 'L0_attn_b_Wf': _L0_attn_b_in['Wf'], 'L0_attn_b_Wg1': _L0_attn_b_in['Wg1'], 'L0_attn_b_Wg2': _L0_attn_b_in['Wg2'], 'L0_attn_b_Wo': _L0_attn_b_in['Wo'], 'L0_attn_b_norm_w': _L0_attn_b_in['norm_w'], 'L0_ffn_w_red': _L0_ffn_in['w_red'], 'L0_ffn_wg': _L0_ffn_in['wg'], 'L0_ffn_w1': _L0_ffn_in['w1'], 'L0_ffn_b1': _L0_ffn_in['b1'], 'L0_ffn_w2': _L0_ffn_in['w2'], 'L0_ffn_b2': _L0_ffn_in['b2']}
    _x0 = _d['L0_attn_a_x']
    _d['L0_attn_a_x'] = jax.random.normal(jax.random.fold_in(jax.random.key(seed), 1), (8, 512, 128), dtype=_x0.dtype)
    del _x0
    return _d

def reference(L0_attn_a_x, L0_attn_a_W, L0_attn_b_Wq, L0_attn_b_Wk, L0_attn_b_Wv, L0_attn_b_Wgamma, L0_attn_b_Wf, L0_attn_b_Wg1, L0_attn_b_Wg2, L0_attn_b_Wo, L0_attn_b_norm_w, L0_ffn_w_red, L0_ffn_wg, L0_ffn_w1, L0_ffn_b1, L0_ffn_w2, L0_ffn_b2):

    def _L0_attn_a_ref(x, W):
        import jax, jax.numpy as jnp
        import numpy as np
        import math
        N_HEAD = 16
        DEG = 2
        EPS = 1e-07
        B, T, C = x.shape
        nh = N_HEAD
        hs = C // nh
        scale = 1.0 / math.sqrt(hs)
        qkvgr = jnp.einsum('btc,oc->bto', x, W)
        q, k, v = (qkvgr[..., :C], qkvgr[..., C:2 * C], qkvgr[..., 2 * C:3 * C])
        log_g = jax.nn.log_sigmoid(qkvgr[..., 3 * C:].astype(jnp.float32))
        log_G = jnp.cumsum(log_g, axis=1).transpose(0, 2, 1)

        def heads(a):
            return a.reshape(B, T, nh, hs).transpose(0, 2, 1, 3)
        Q, K, V = (heads(q), heads(k), heads(v))
        S = jnp.einsum('bhtd,bhsd->bhts', Q, K)
        Tm = DEG * jnp.log(jnp.abs(S) + EPS) + jnp.log(jnp.float32(scale))
        Z = Tm + log_G[..., :, None] - log_G[..., None, :]
        mask = jnp.tril(jnp.ones((T, T), dtype=bool))
        Z = jnp.where(mask, Z, -jnp.inf)
        Z_rowmax = jax.lax.stop_gradient(jnp.max(Z, axis=-1, keepdims=True))
        P = jnp.exp(Z - Z_rowmax)
        norm = jnp.sum(P, axis=-1)
        O = jnp.einsum('bhts,bhsd->bhtd', P, V)
        y = O / norm[..., None]
        return y.transpose(0, 2, 1, 3).reshape(B, T, C)

    def _L0_attn_b_ref(x, Wq, Wk, Wv, Wgamma, Wf, Wg1, Wg2, Wo, norm_w):
        import jax, jax.numpy as jnp
        import numpy as np
        B, N, D, H = (2, 256, 128, 16)
        HD = D // H

        def l2norm(x, eps=1e-12):
            n = jnp.sqrt(jnp.sum(x * x, axis=-1, keepdims=True))
            return x / jnp.maximum(n, eps)

        def dplr_delta_rule(q, k, v, a, gk):
            qm, km, vm, am, gm = (jnp.moveaxis(t, 1, 0) for t in (q, k, v, a, gk))

            def step(S, inp):
                qt, kt, vt, at, gkt = inp
                Sp = S * jnp.exp(gkt)[..., None]
                u = jnp.einsum('bhk,bhkv->bhv', at, Sp) + vt
                S = Sp + jnp.einsum('bhk,bhv->bhkv', kt, u)
                o = jnp.einsum('bhk,bhkv->bhv', qt, S)
                return (S, o)
            S0 = jnp.zeros((q.shape[0], q.shape[2], q.shape[3], v.shape[3]), q.dtype)
            _, o = jax.lax.scan(step, S0, (qm, km, vm, am, gm))
            return jnp.moveaxis(o, 0, 1)

        def _forward(x, Wq, Wk, Wv, Wgamma, Wf, Wg1, Wg2, Wo, norm_w):
            b, n, d = x.shape
            silu = jax.nn.silu
            q = silu(x @ Wq)
            k = silu(x @ Wk)
            v = silu(x @ Wv)
            log_f = jax.nn.log_sigmoid(x @ Wf)
            gamma = -jax.nn.sigmoid(x @ Wgamma)
            q = q.reshape(b, n, H, HD)
            k = l2norm(k.reshape(b, n, H, HD))
            v = v.reshape(b, n, H, HD)
            gk = jnp.broadcast_to(log_f[..., None], (b, n, H, HD))
            a = k * gamma[..., None] * jnp.exp(gk)
            out = dplr_delta_rule(q, k, v, a, gk)
            out = out.reshape(b, n, d)
            gate = jax.nn.sigmoid(x @ Wg1 @ Wg2)
            out = out * gate
            mu = jnp.mean(out, axis=-1, keepdims=True)
            var = jnp.mean(jnp.square(out - mu), axis=-1, keepdims=True)
            out = (out - mu) * jax.lax.rsqrt(var + 1e-05) * norm_w
            return out @ Wo
        return _forward(x, Wq, Wk, Wv, Wgamma, Wf, Wg1, Wg2, Wo, norm_w)

    def _L0_ffn_ref(hidden_states, w_red, wg, w1, b1, w2, b2):
        import jax, jax.numpy as jnp
        import numpy as np
        E, D, F, GATE_DIM = (8, 128, 512, 16)
        B, T = (2, 256)
        b, t, c = hidden_states.shape
        x = hidden_states.reshape(-1, c)
        red = x @ w_red
        wg_n = wg / jnp.maximum(jnp.linalg.norm(wg, axis=1, keepdims=True), 0.0001)
        logits = red @ wg_n.T
        gates = jax.nn.softmax(logits, axis=1)
        idx = jnp.argmax(gates, axis=1)
        scores = jnp.take_along_axis(gates, idx[:, None], axis=1)
        h = jax.nn.gelu(jnp.einsum('td,edf->etf', x, w1) + b1[:, None, :], approximate=False)
        y = jnp.einsum('etf,efd->etd', h, w2) + b2[:, None, :]
        out = jnp.take_along_axis(y, idx[None, :, None], axis=0)[0]
        out = out * scores
        return out.reshape(b, t, c)
    x = L0_attn_a_x
    x = x + _L0_attn_a_ref(_layernorm(x, axis=-1), L0_attn_a_W)
    x = x + _L0_ffn_ref(_layernorm(x, axis=-1), L0_ffn_w_red, L0_ffn_wg, L0_ffn_w1, L0_ffn_b1, L0_ffn_w2, L0_ffn_b2)
    x = x + _L0_attn_b_ref(_layernorm(x, axis=-1), L0_attn_b_Wq, L0_attn_b_Wk, L0_attn_b_Wv, L0_attn_b_Wgamma, L0_attn_b_Wf, L0_attn_b_Wg1, L0_attn_b_Wg2, L0_attn_b_Wo, L0_attn_b_norm_w)
    x = x + _L0_ffn_ref(_layernorm(x, axis=-1), L0_ffn_w_red, L0_ffn_wg, L0_ffn_w1, L0_ffn_b1, L0_ffn_w2, L0_ffn_b2)
    return x

_drawn_inputs = setup_inputs


def setup_inputs(seed=0):
    import zlib

    import numpy as np

    out = dict(_drawn_inputs(seed))
    spreads = {'L0_attn_b_norm_w': (1.0, 0.2)}
    factors = {'L0_attn_b_Wgamma': 24.235,
     'L0_attn_b_Wf': 5.057,
     'L0_attn_b_Wg1': 8.0,
     'L0_attn_b_Wg2': 8.0,
     'L0_ffn_w_red': 3.95,
     'L0_ffn_wg': 3.946,
     'L0_ffn_w1': 4.036,
     'L0_ffn_b1': 8.0,
     'L0_ffn_w2': 3.947,
     'L0_ffn_b2': 8.0}
    for name, (base, spread) in spreads.items():
        noise = np.random.default_rng([zlib.crc32(name.encode()), seed]).standard_normal(out[name].shape)
        drawn = base * np.exp(spread * noise) if base else spread * noise
        out[name] = jnp.asarray(drawn.astype(out[name].dtype))
    for name, factor in factors.items():
        out[name] = (out[name] * factor).astype(out[name].dtype)
    return out
```

```python
from contextlib import ExitStack

import concourse.bass as bass
from concourse import mybir

F32 = mybir.dt.float32
BF16 = mybir.dt.bfloat16
I32 = mybir.dt.int32
ALU = mybir.AluOpType
ACT = mybir.ActivationFunctionType
AX = mybir.AxisListType
RMAX = bass.bass_isa.ReduceOp.max

P = 128
B, T, C = 8, 512, 128
H, HD = 16, 8
TT = T // P
NT = B * TT
EPS_LN = 1e-5

NP = H // 2
L = 64
NM = T // L
NU = 2 * NM * 2
EPS_A = 1e-7
NPARTS = 8
Q_PART = [0, 0, 1, 1, 0, 2, 1, 2]
K_PART = [0, 1, 0, 1, 2, 0, 2, 1]
OFF_FIRST = [sum(NM - 1 - j for j in range(m)) for m in range(NM)]
N_OFF = NM * (NM - 1) // 2

E, F, GD = 8, 512, 16
NF = F // P
ST = 256
NS = (B * T + E * (ST - 1)) // ST
NC2 = ST // P
SLOT_TILES = [(NS + 1) // 2, NS // 2]
EPS_G = 1e-4

CH = 8
NCH = T // CH
EPS_K = 1e-12


def attention(nc, x, xin, W):
    with ExitStack() as ctx:
        def sb(name, shape, dt=F32):
            return ctx.enter_context(nc.sbuf_tensor("a_" + name, shape, dt))

        def psum(name, shape):
            return ctx.enter_context(nc.psum_tensor("a_" + name, shape, F32))

        def sem(name):
            return ctx.enter_context(nc.semaphore(name))

        scratch = nc.dram_tensor("parts_scratch", [2, 2, 3, P, T], BF16, kind="Internal").ap()

        wn = sb("wn", [P, 4, C])
        wT = sb("wT", [P, 3, C])
        wvg = sb("wvg", [P, 2, 72])
        wgT = sb("wgT", [P, H])
        sq = sb("sq", [P, C])
        wss = sb("wss", [P, 2])
        wmx = sb("wmx", [P, 2])
        guard = sb("guard", [P, 4])
        eps_a = sb("eps_a", [P, 1])
        ident = sb("ident", [P, P])
        ident_b = sb("ident_b", [P, P], BF16)
        upto = sb("upto", [P, P])
        after = sb("after", [P, P])
        same = sb("same", [P, P])
        tri = sb("tri", [P, L])
        never = sb("never", [P, L], BF16)
        restart = sb("restart", [P, NP, NM])
        zeros = sb("zeros", [P, 18])
        stats = sb("stats", [P, NT, 6])
        mv = sb("mv", [P, NT, 2])
        rstd = sb("rstd", [P, 4, NT])
        xn = sb("xn", [P, TT, C])
        xnT = sb("xnT", [P, T])
        parts = sb("parts", [P, 2, 3, T], BF16)
        rest = sb("rest", [P, 2, T])
        qf = sb("qf", [P, 2, NP, T], BF16)
        kc = sb("kc", [P, NP, T], BF16)
        kf = sb("kf", [P, 2, NP, NM, 2, L], BF16)
        vd = sb("vd", [P, 2, NM, NP, 18])
        vo = sb("vo", [P, N_OFF, NP, 18])
        gates = sb("gates", [P, P])
        g_low = sb("g_low", [P, P])
        g_abs = sb("g_abs", [P, P])
        logg = sb("logg", [P, P])
        g_cum = sb("g_cum", [P, P])
        b_tot = sb("b_tot", [P, NP, NM])
        b_cum = sb("b_cum", [P, NP, NM])
        tail = sb("tail", [P, NP, NM])
        reach = sb("reach", [P, NP, NM, NM])
        e_tok = sb("e_tok", [P, 2, TT * H])
        ramp = sb("ramp", [P, 2, NP, L])
        decay = sb("decay", [P, 2, NM, NP, L])
        mag = sb("mag", [P, 2, 2 * T])
        pw = sb("pw", [P, 4, 2 * T])
        pdg = sb("pdg", [P, 4, 2, L])
        off_sb = sb("off_sb", [P, T])
        dia_sb = sb("dia_sb", [P, T])
        acc = sb("acc", [P, TT * 4, 2, 9])
        rnorm = sb("rnorm", [P, TT * 4, 2])
        y = sb("y", [P, TT * 4, 2, HD])

        pS = psum("pS", [P, 4, T])
        pOff = psum("pOff", [P, T])
        pDia = psum("pDia", [P, T])
        M0 = psum("M0", [P, T])
        M1 = psum("M1", [P, T])

        names = """x_in w_in consts guard_step w_scaled w_T w_sb stat_done rstd_step rstd_ready
        xn_done xnT_ps xnT_sb qk_ps split_hi split_rest split_mid split_lo parts_out feat_q feat_k
        v_ps v_sb gate_sb tok_ps g_step logg_done cum_ps cum_sb reach_step reach_exp vo_done ramp_done decay_ps decay_sb
        s_ps mag_done sq_done pdg_done pv_done pv_half off_done dia_done fin_ps fin_step fin_done fin_num 
        c_step vd_zero kx_done kf_zero vo_zero w_misc""".split()
        s = {n: sem("a_" + n) for n in names}
        block = ctx.enter_context(nc.Block())

        def vo_at(j, i):
            return OFF_FIRST[j] + i - j - 1

        def width(m):
            return T - L * m

        def unit(n):
            hf, r = divmod(n, 2 * NM)
            m, qh = divmod(r, 2)
            return hf, m, qh

        AHEAD_S, AHEAD_MAG, AHEAD_PW = 2, 2, 4
        TURN, QK, VALUES, SUMS, FIN0, DECAY, EXPAND = 3, 5, 8, 12, 17, 20, 22

        @block.sync
        def _(sp):
            for k in range(B):
                sp.dma_start(x[:, TT * k:TT * (k + 1), :],
                             xin[k].rearrange("(i p) c -> p i c", p=P)).then_inc(s["x_in"], 16)

            def features(bb, k):
                sp.wait_ge(s["split_hi"], 2 * bb + 2)
                sp.wait_ge(s["split_mid"], 2 * bb + 2)
                sp.wait_ge(s["split_lo"], 2 * bb + 2)
                for t in range(2):
                    for c in range(3):
                        sp.dma_start(scratch[k, t, c], parts[:, t, c, :]).then_inc(s["parts_out"], 16)
                sp.wait_ge(s["parts_out"], 96 * bb + 96)
                sp.wait_ge(s["kx_done"], 2 * bb)
                for par in range(2):
                    for c in range(NPARTS):
                        row = 64 * par + HD * c
                        src = [scratch[k, t, part].rearrange("(p x d) t -> x d p t", x=2, d=HD)[par]
                               for t, part in ((0, Q_PART[c]), (1, K_PART[c]))]
                        sp.dma_start(qf[row:row + HD, k, :, :], src[0]).then_inc(s["feat_q"], 16)
                        sp.dma_start(kc[row:row + HD, :, :], src[1]).then_inc(s["feat_k"], 16)

            features(0, 0)

            def batch(b, k, last=False):
                if not last:
                    sp.wait_ge(s["s_ps"], NU * b)
                    features(b + 1, 1 - k)

            batch(0, 0)
            with sp.Fori(1, B - 2, 2) as b:
                batch(b, 1)
                batch(b + 1, 0)

        @block.gpsimd
        def _(pool):
            st = 0

            def step(ins):
                nonlocal st
                st += 1
                ins.then_inc(s["c_step"], 1)
                pool.wait_ge(s["c_step"], st)

            for t, val in ((ident, 0.0), (ident_b, 0.0), (upto, 0.0), (after, 0.0), (same, 0.0), (tri, 1.0),
                           (never, 0.0), (zeros, 0.0)):
                step(pool.memset(t[:, :], val))
            step(pool.memset(restart[:, :, :], 1.0))
            pool.wait_ge(s["c_step"], st)
            step(pool.memset(restart[:, :, 0:1], 0.0))
            for t in (ident, ident_b):
                step(pool.affine_select(out=t[:, :], in_=t[:, :], compare_op=ALU.not_equal, fill=1.0,
                                        base=0, pattern=[[-1, P]], channel_multiplier=1))
            for h in range(2):
                for t in (upto, after, same):
                    step(pool.memset(t[L * h:L * h + L, L * h:L * h + L], 1.0))
            pool.wait_ge(s["c_step"], st)
            for h in range(2):
                lo, hi = L * h, L * h + L
                step(pool.affine_select(out=upto[lo:hi, lo:hi], in_=upto[lo:hi, lo:hi], compare_op=ALU.is_ge,
                                        fill=0.0, base=0, pattern=[[1, L]], channel_multiplier=-1))
                step(pool.affine_select(out=after[lo:hi, lo:hi], in_=after[lo:hi, lo:hi], compare_op=ALU.is_ge,
                                        fill=0.0, base=-1, pattern=[[-1, L]], channel_multiplier=1))
                step(pool.affine_select(out=tri[lo:hi, :], in_=tri[lo:hi, :], compare_op=ALU.is_ge,
                                        fill=0.0, base=0, pattern=[[1, L]], channel_multiplier=-1))
                step(pool.affine_select(out=never[lo:hi, :], in_=never[lo:hi, :], compare_op=ALU.is_ge,
                                        fill=-1e30, base=0, pattern=[[1, L]], channel_multiplier=-1))
            pool.wait_ge(s["c_step"], st)
            pool.memset(guard[:, 3:4], 0.0).then_inc(s["consts"], 1)
            for k in range(2):
                pool.memset(kf[:, k, :, :, :, :].rearrange("p a m x t -> p (a m x t)").bitcast(F32), 0.0)\
                    .then_inc(s["kf_zero"], 1)
            pool.wait_ge(s["guard_step"], 2)
            pool.partition_all_reduce(wmx[:, :], wss[:, :], P, RMAX).then_inc(s["guard_step"], 1)

            def ramps(bb, m, first=False):
                pool.wait_ge(s["logg_done"], bb + 1)
                if not (first and m < 2):
                    pool.wait_ge(s["decay_ps"], NM * bb + m - 1)
                pool.tensor_tensor(ramp[:, m % 2, :, :],
                                   tri[:, :].unsqueeze(1).broadcast_to([P, NP, L]),
                                   logg[:, 0:64].rearrange("p (a m) -> p a m", m=NM)[:, :, m:m + 1]
                                   .broadcast_to([P, NP, L]), ALU.mult).then_inc(s["ramp_done"], 1)

            def values_off(bb, k, j, first=False):
                if first:
                    pool.wait_ge(s["vd_zero"], 2)
                if j == 0:
                    pool.wait_ge(s["reach_exp"], bb + 1)
                    pool.wait_ge(s["v_sb"], 4 * bb + 4)
                if not first:
                    pool.wait_ge(s["pv_done"], NU * (bb - 1) + 2 * NM + 2 * j + 2 + AHEAD_PW)
                n = NM - 1 - j
                pool.tensor_tensor(
                    vo[:, vo_at(j, j + 1):vo_at(j, j + 1) + n, :, :],
                    vd[:, k, j, :, :].unsqueeze(1).broadcast_to([P, n, NP, 18]),
                    reach[:, :, j, j:NM - 1].rearrange("p a i -> p i a").unsqueeze(3)
                    .broadcast_to([P, n, NP, 18]), ALU.mult).then_inc(s["vo_done"], 1)

            def diagonal(b, n, k):
                hf, m, qh = unit(n)
                sl = n % 4
                pool.wait_ge(s["sq_done"], NU * b + n + 1 + AHEAD_MAG)
                pool.wait_ge(s["decay_sb"], NM * b + m + 1)
                pool.wait_ge(s["pv_done"], NU * b + n + 1)
                pool.tensor_tensor(pdg[:, sl, :, :],
                                   pw[:, sl, 0:2 * width(m)].rearrange("p (l t) -> p l t", l=2)[:, :, 0:L],
                                   decay[:, k, m, 4 * qh + hf:4 * qh + hf + 3:2, :], ALU.mult)\
                    .then_inc(s["pdg_done"], 1)

            for m in range(NM):
                ramps(0, m, first=True)
            for j in range(NM - 1):
                values_off(0, 0, j, first=True)

            def batch(b, k, last=False):
                for n in range(NU):
                    diagonal(b, n, k)
                    if last:
                        continue
                    if DECAY - 2 <= n < DECAY - 2 + NM:
                        ramps(b + 1, n - DECAY + 2)
                    if n >= 2 * NM + 3 and n % 2 == 1 and (n - 2 * NM - 3) // 2 < NM - 1:
                        values_off(b + 1, 1 - k, (n - 2 * NM - 3) // 2)
            batch(0, 0)
            with pool.Fori(1, B - 2, 2) as b:
                batch(b, 1)
                batch(b + 1, 0)
            batch(B - 1, 1, last=True)

        @block.scalar
        def _(act):
            act.dma_start(wn[:, 0:3, :], W[0:3 * C, :].rearrange("(j p) c -> p j c", p=P)).then_inc(s["w_in"], 16)
            act.dma_start(wn[0:H, 3, :], W[3 * C:3 * C + H, :]).then_inc(s["w_in"], 16)
            act.wait_ge(s["w_in"], 32)
            act.activation(sq[:, :], wn[:, 0, :], ACT.Square, accum_out=wss[:, 0:1]).then_inc(s["guard_step"], 1)
            act.activation(dia_sb[:, 0:C], wn[:, 1, :], ACT.Square, accum_out=wss[:, 1:2]).then_inc(s["guard_step"], 1)
            act.wait_ge(s["guard_step"], 7)
            act.activation(guard[:, 1:2], guard[:, 0:1], ACT.Sqrt).then_inc(s["guard_step"], 1)
            act.wait_ge(s["rstd_step"], 1)
            act.activation(rstd[:, 2, :], rstd[:, 1, :], ACT.Sqrt).then_inc(s["rstd_step"], 1)

            def turned(bb):
                act.wait_ge(s["xnT_ps"], bb + 1)
                act.wait_ge(s["v_ps"], bb)
                act.activation(xnT[:, :], M0[:, :], ACT.Copy).then_inc(s["xnT_sb"], 1)

            def split_high(bb, t):
                act.wait_ge(s["qk_ps"], 2 * bb + t + 1)
                act.wait_ge(s["parts_out"], 96 * bb)
                act.activation(parts[:, t, 0, :], (M0, M1)[t][:, :], ACT.Copy).then_inc(s["split_hi"], 1)

            def split_mid(bb, t):
                act.wait_ge(s["split_rest"], 2 * bb + t + 1)
                act.activation(parts[:, t, 1, :], rest[:, t, :], ACT.Copy).then_inc(s["split_mid"], 1)

            def values(bb, k, first=False):
                act.wait_ge(s["gate_sb"], 4 * bb + 3)
                if first:
                    act.wait_ge(s["vd_zero"], 2)
                else:
                    act.wait_ge(s["pv_done"], NU * (bb - 1) + AHEAD_PW)
                    act.wait_ge(s["vo_done"], 7 * (bb - 1))
                for q, M in enumerate((M0, M1)):
                    for par in range(2):
                        lo, hi = L * par, L * par + L
                        act.activation(
                            vd[lo:hi, k, 4 * q:4 * q + 4, :, 9 * par:9 * par + HD],
                            M[lo:hi, 0:288].rearrange("p (m c) -> p m c", c=72)[:, :, 0:64]
                            .rearrange("p m (a d) -> p m a d", d=HD), ACT.Copy).then_inc(s["v_sb"], 1)

            def gate_logs(bb):
                act.wait_ge(s["g_step"], 3 * bb + 1)
                act.activation(g_abs[:, :], g_abs[:, :], ACT.Exp).then_inc(s["g_step"], 1)
                act.wait_ge(s["g_step"], 3 * bb + 2)
                act.activation(g_abs[:, :], g_abs[:, :], ACT.Ln, bias=1.0).then_inc(s["g_step"], 1)

            def reaches(bb, k, first=False):
                act.wait_ge(s["cum_sb"], 6 * bb + 2)
                if not first:
                    act.wait_ge(s["fin_done"], 2 * (bb - 1))
                act.activation(e_tok[:, k, :], M0[:, 64:128], ACT.Exp).then_inc(s["tok_ps"], 1)
                act.wait_ge(s["reach_step"], bb + 1)
                act.activation(reach[:, :, :, :].rearrange("p a j i -> p (a j i)"),
                               reach[:, :, :, :].rearrange("p a j i -> p (a j i)"), ACT.Exp)\
                    .then_inc(s["reach_exp"], 1)

            def decays(bb, k, m, first=False):
                act.wait_ge(s["decay_ps"], NM * bb + m + 1)
                if not first and m == 0:
                    act.wait_ge(s["pdg_done"], NU * (bb - 1))
                act.activation(decay[:, k, m, :, :].rearrange("p a t -> p (a t)"), (M0, M1)[m % 2][:, :],
                               ACT.Exp).then_inc(s["decay_sb"], 1)

            def square(b, n):
                hf, m, qh = unit(n)
                N = 2 * width(m)
                act.wait_ge(s["mag_done"], NU * b + n + 1 + AHEAD_S)
                act.wait_ge(s["pv_done"], NU * b + n + 1)
                act.activation(pw[:, n % 4, 0:N], mag[:, n % 2, 0:N], ACT.Square, bias=eps_a[:, 0:1])\
                    .then_inc(s["sq_done"], 1)

            def off_copy(b, hf):
                act.wait_ge(s["pv_done"], NU * b + 2 * NM * (hf + 1) + AHEAD_PW)
                act.wait_ge(s["fin_ps"], 2 * b + hf)
                act.activation(off_sb[:, :], pOff[:, :], ACT.Copy).then_inc(s["off_done"], 1)

            def batch(b, k, last=False):
                for n in range(NU):
                    square(b, n)
                    if n == 2 * NM + 1:
                        off_copy(b, 0)
                    if last:
                        continue
                    if n == TURN:
                        turned(b + 1)
                    if n == QK + 1:
                        split_high(b + 1, 0)
                        split_high(b + 1, 1)
                    if n == QK + 2:
                        split_mid(b + 1, 0)
                        split_mid(b + 1, 1)
                    if n == VALUES + 1:
                        values(b + 1, 1 - k)
                    if n == VALUES + 2:
                        gate_logs(b + 1)
                    if n == SUMS + 1:
                        reaches(b + 1, 1 - k)
                    if DECAY <= n < DECAY + NM:
                        decays(b + 1, 1 - k, n - DECAY)
                off_copy(b, 1)

            act.sem_inc(s["sq_done"], AHEAD_MAG)
            turned(0)
            split_high(0, 0)
            split_high(0, 1)
            split_mid(0, 0)
            split_mid(0, 1)
            values(0, 0, first=True)
            gate_logs(0)
            reaches(0, 0, first=True)
            for m in range(NM):
                decays(0, 0, m, first=True)
            batch(0, 0)
            with act.Fori(1, B - 2, 2) as b:
                batch(b, 1)
                batch(b + 1, 0)
            batch(B - 1, 1, last=True)

        @block.vector
        def _(dve):
            dve.sem_inc(s["mag_done"], AHEAD_S)
            dve.memset(vd[:, :, :, :, :].rearrange("p k m a c -> p (k m a c)"), 0.0).then_inc(s["w_misc"], 1)
            dve.memset(vo[:, :, :, :].rearrange("p n a c -> p (n a c)"), 0.0).then_inc(s["vo_zero"], 1)
            dve.memset(pOff[:, :], 0.0).then_inc(s["w_misc"], 1)
            dve.memset(pDia[:, :], 0.0).then_inc(s["w_misc"], 1)
            dve.wait_ge(s["w_misc"], 3)
            for par in range(2):
                lo, hi = L * par, L * par + L
                dve.memset(vd[lo:hi, :, :, :, 9 * par + HD:9 * par + HD + 1]
                           .rearrange("p k m a c -> p (k m a) c"), 1.0).then_inc(s["vd_zero"], 1)
            dve.wait_ge(s["guard_step"], 3)
            dve.tensor_scalar(wss[:, :], wmx[:, :], 1e-30, None, ALU.max).then_inc(s["guard_step"], 1)
            dve.wait_ge(s["guard_step"], 4)
            dve.reciprocal(wmx[:, :], wss[:, :]).then_inc(s["guard_step"], 1)
            dve.wait_ge(s["guard_step"], 5)
            dve.tensor_tensor(guard[:, 2:3], wmx[:, 0:1], wmx[:, 1:2], ALU.mult).then_inc(s["guard_step"], 1)
            dve.wait_ge(s["guard_step"], 6)
            dve.tensor_scalar(guard[:, 0:1], guard[:, 2:3], 1e30 / (HD * HD * C * C), 1.0, ALU.mult, ALU.min)\
                .then_inc(s["guard_step"], 1)
            dve.wait_ge(s["guard_step"], 8)
            dve.tensor_scalar(eps_a[:, :], guard[:, 1:2], EPS_A, None, ALU.mult).then_inc(s["w_scaled"], 1)
            dve.tensor_scalar(wn[:, 0, :], wn[:, 0, :], guard[:, 1:2], None, ALU.mult).then_inc(s["w_scaled"], 1)
            dve.wait_ge(s["w_T"], 1)
            dve.tensor_copy(wT[:, :, :].rearrange("p j o -> p (j o)"), M0[:, 0:384]).then_inc(s["w_sb"], 1)
            dve.tensor_copy(wgT[:, :], M0[:, 384:400]).then_inc(s["w_sb"], 1)
            for par in range(2):
                dve.tensor_copy(wvg[:, par, 0:64].rearrange("p (a d) -> p a d", d=HD),
                                M0[:, 256:384].rearrange("p (a x d) -> p x a d", x=2, d=HD)[:, par])\
                    .then_inc(s["w_sb"], 1)
                dve.tensor_copy(wvg[:, par, 64:72],
                                M0[:, 384:400].rearrange("p (a x) -> p x a", x=2)[:, par]).then_inc(s["w_sb"], 1)
            for k in range(B):
                dve.wait_ge(s["x_in"], 16 * B)
                for i in range(TT):
                    dve.bn_stats(stats[:, TT * k + i, :], x[:, TT * k + i, :]).then_inc(s["stat_done"], 1)
            for k in range(B):
                for i in range(TT):
                    dve.wait_ge(s["stat_done"], TT * k + i + 1)
                    dve.bn_aggr(mv[:, TT * k + i, :], stats[:, TT * k + i, :]).then_inc(s["stat_done"], 1)
            dve.wait_ge(s["stat_done"], 2 * NT)
            dve.tensor_scalar(rstd[:, 1, :], mv[:, :, 1], EPS_LN, None, ALU.add).then_inc(s["rstd_step"], 1)
            dve.wait_ge(s["rstd_step"], 2)
            dve.reciprocal(rstd[:, 3, :], rstd[:, 2, :]).then_inc(s["rstd_step"], 1)
            dve.wait_ge(s["rstd_step"], 3)
            dve.tensor_tensor(rstd[:, 2, :], rstd[:, 3, :], rstd[:, 3, :], ALU.mult).then_inc(s["rstd_step"], 1)
            dve.wait_ge(s["rstd_step"], 4)
            dve.tensor_tensor(rstd[:, 2, :], rstd[:, 2, :], rstd[:, 1, :], ALU.mult).then_inc(s["rstd_step"], 1)
            dve.wait_ge(s["rstd_step"], 5)
            dve.tensor_scalar(rstd[:, 2, :], rstd[:, 2, :], -0.5, 1.5, ALU.mult, ALU.add)\
                .then_inc(s["rstd_step"], 1)
            dve.wait_ge(s["rstd_step"], 6)
            dve.tensor_tensor(rstd[:, 0, :], rstd[:, 2, :], rstd[:, 3, :], ALU.mult).then_inc(s["rstd_ready"], 1)

            def normalize(bb, first=False):
                dve.wait_ge(s["rstd_ready"], 1)
                if not first:
                    dve.wait_ge(s["xnT_ps"], bb)
                for i in range(TT):
                    j = TT * bb + i
                    dve.tensor_scalar(xn[:, i, :], x[:, bass.ds(j, 1), :].rearrange("p a c -> p (a c)"),
                                       mv[:, bass.ds(j, 1), 0:1].rearrange("p a c -> p (a c)"),
                                       rstd[:, 0, bass.ds(j, 1)], ALU.subtract, ALU.mult).then_inc(s["xn_done"], 1)

            def split_rest(bb, t, first=False):
                dve.wait_ge(s["split_hi"], 2 * bb + t + 1)
                if not first:
                    dve.wait_ge(s["split_mid"], 2 * (bb - 1) + t + 1)
                dve.tensor_tensor(rest[:, t, :], (M0, M1)[t][:, :], parts[:, t, 0, :], ALU.subtract)\
                    .then_inc(s["split_rest"], 1)

            def split_low(bb, t):
                dve.wait_ge(s["split_mid"], 2 * bb + t + 1)
                dve.wait_ge(s["parts_out"], 96 * bb)
                dve.tensor_tensor(parts[:, t, 2, :], rest[:, t, :], parts[:, t, 1, :], ALU.subtract)\
                    .then_inc(s["split_lo"], 1)

            def gate_prep(bb):
                dve.wait_ge(s["v_ps"], bb + 1)
                for q, M in enumerate((M0, M1)):
                    dve.tensor_copy(gates[:, 0:64].rearrange("p (a m) -> p m a", m=NM)[:, 4 * q:4 * q + 4, :],
                                    M[:, 0:288].rearrange("p (m c) -> p m c", c=72)[:, :, 64:72])\
                        .then_inc(s["gate_sb"], 1)
                dve.tensor_copy(gates[:, 64:128], M0[:, 288:352]).then_inc(s["gate_sb"], 1)
                dve.wait_ge(s["gate_sb"], 4 * bb + 3)
                dve.tensor_scalar(g_low[:, :], gates[:, :], 0.0, None, ALU.min).then_inc(s["gate_sb"], 1)
                dve.wait_ge(s["gate_sb"], 4 * bb + 4)
                dve.scalar_tensor_tensor(g_abs[:, :], g_low[:, :], 2.0, gates[:, :], ALU.mult, ALU.subtract)\
                    .then_inc(s["g_step"], 1)

            def gate_log(bb):
                dve.wait_ge(s["g_step"], 3 * bb + 3)
                dve.wait_ge(s["ramp_done"], NM * bb)
                dve.tensor_tensor(logg[:, :], g_low[:, :], g_abs[:, :], ALU.subtract).then_inc(s["logg_done"], 1)

            def sums(bb):
                dve.wait_ge(s["cum_ps"], bb + 1)
                dve.tensor_copy(b_tot[:, :, :].rearrange("p a m -> p (a m)"), M0[:, 128:192])\
                    .then_inc(s["cum_sb"], 1)
                dve.wait_ge(s["cum_sb"], 6 * bb + 1)
                dve.tensor_tensor(tail[:, :, :].rearrange("p a m -> p (a m)"),
                                  b_tot[:, :, :].rearrange("p a m -> p (a m)"), M0[:, 0:64], ALU.subtract)\
                    .then_inc(s["cum_sb"], 1)
                dve.tensor_tensor_scan(b_cum[:, :, :].rearrange("p a m -> p (a m)"),
                                       restart[:, :, :].rearrange("p a m -> p (a m)"),
                                       b_tot[:, :, :].rearrange("p a m -> p (a m)"), 0.0, ALU.mult, ALU.add)\
                    .then_inc(s["cum_sb"], 1)
                dve.wait_ge(s["cum_sb"], 6 * bb + 3)
                dve.tensor_tensor(tail[:, :, :], tail[:, :, :], b_cum[:, :, :], ALU.subtract)\
                    .then_inc(s["cum_sb"], 1)
                dve.wait_ge(s["cum_sb"], 6 * bb + 4)
                dve.wait_ge(s["vo_done"], 7 * bb)
                dve.tensor_tensor(reach[:, :, :, :], b_cum[:, :, :].unsqueeze(2).broadcast_to([P, NP, NM, NM]),
                                  tail[:, :, :].unsqueeze(3).broadcast_to([P, NP, NM, NM]), ALU.add)\
                    .then_inc(s["cum_sb"], 1)
                dve.wait_ge(s["cum_sb"], 6 * bb + 5)
                dve.tensor_scalar(reach[:, :, :, :].rearrange("p a j i -> p (a j i)"),
                                  reach[:, :, :, :].rearrange("p a j i -> p (a j i)"), 0.0, None, ALU.min)\
                    .then_inc(s["cum_sb"], 1)
                dve.wait_ge(s["cum_sb"], 6 * bb + 6)
                dve.sem_inc(s["reach_step"], 1)

            def expand(bb, k, first=False):
                dve.wait_ge(s["feat_k"], 256 * bb + 256)
                if first:
                    dve.wait_ge(s["kf_zero"], 2)
                else:
                    dve.wait_ge(s["s_ps"], NU * (bb - 1))
                for par in range(2):
                    lo, hi = L * par, L * par + L
                    dve.tensor_copy(kf[lo:hi, k, :, :, par, :].rearrange("p a m t -> p (a m) t"),
                                    kc[lo:hi, :, :].rearrange("p a (m t) -> p (a m) t", t=L))\
                        .then_inc(s["kx_done"], 1)

            def magnitude(b, n):
                hf, m, qh = unit(n)
                N = width(m)
                dve.wait_ge(s["s_ps"], NU * b + n + 1)
                dve.wait_ge(s["sq_done"], NU * b + n + 1)
                dve.tensor_scalar(mag[:, n % 2, 0:2 * N].bitcast(I32).rearrange("p (l t) -> p l t", l=2),
                                  pS[:, 2 * (n % 2):2 * (n % 2) + 2, 0:N].bitcast(I32),
                                  0x7fffffff, None, ALU.bitwise_and).then_inc(s["mag_done"], 1)

            def dia_copy(b, hf):
                dve.wait_ge(s["pv_done"], NU * b + 2 * NM * (hf + 1) + AHEAD_PW)
                dve.wait_ge(s["fin_ps"], 2 * b + hf)
                dve.tensor_copy(dia_sb[:, :], pDia[:, :]).then_inc(s["dia_done"], 1)

            def finish(b, k, hf):
                dve.wait_ge(s["fin_ps"], 2 * b + hf + 1)
                dve.wait_ge(s["tok_ps"], b + 1)
                step = 5 * (2 * b + hf)
                view = [M[:, :].rearrange("p (a c) -> p a c", c=32)[:, :, 0:18]
                        .rearrange("p a (x d) -> p a x d", x=2) for M in (M0, M1)]
                et = e_tok[:, k, :].rearrange("p (a x) -> p a x", x=4)[:, :, 2 * hf:2 * hf + 2].unsqueeze(3)\
                    .broadcast_to([P, 16, 2, 9])
                dve.tensor_tensor(acc[:, :, :, :], view[0], et, ALU.mult).then_inc(s["fin_step"], 1)
                dve.wait_ge(s["fin_step"], step + 1)
                dve.tensor_tensor(acc[:, :, :, :], view[1], acc[:, :, :, :], ALU.add).then_inc(s["fin_step"], 1)
                dve.wait_ge(s["fin_step"], step + 2)
                dve.reciprocal(rnorm[:, :, :], acc[:, :, :, HD]).then_inc(s["fin_step"], 1)
                dve.wait_ge(s["fin_step"], step + 3)
                dve.tensor_tensor(y[:, :, :, :], acc[:, :, :, 0:HD],
                                  rnorm[:, :, :].unsqueeze(3).broadcast_to([P, 16, 2, HD]), ALU.mult)\
                    .then_inc(s["fin_step"], 1)
                dve.wait_ge(s["fin_step"], step + 4)
                xs = x[:, bass.ds(TT * b, TT), :].rearrange("p i (a c) -> p (i a) c", c=32)[:, :, 16 * hf:16 * hf + 16]
                dve.tensor_tensor(xs, xs, y[:, :, :, :].rearrange("p a x d -> p a (x d)"), ALU.add)\
                    .then_inc(s["fin_step"], 1)
                dve.wait_ge(s["fin_step"], step + 5)
                dve.sem_inc(s["fin_done"], 1)

            normalize(0, first=True)
            split_rest(0, 0, first=True)
            split_rest(0, 1, first=True)
            split_low(0, 0)
            split_low(0, 1)
            gate_prep(0)
            gate_log(0)
            sums(0)
            expand(0, 0, first=True)
            magnitude(0, 0)
            magnitude(0, 1)

            def batch(b, k, last=False):
                for n in range(NU):
                    if n + 2 < NU:
                        magnitude(b, n + 2)
                    elif not last:
                        magnitude(b + 1, n + 2 - NU)
                    if n == 2 * NM - 1:
                        dia_copy(b, 0)
                    if n == FIN0 + 1:
                        finish(b, k, 0)
                    if last:
                        continue
                    if n == TURN - 2:
                        normalize(b + 1)
                    if n == QK + 1:
                        split_rest(b + 1, 0)
                        split_rest(b + 1, 1)
                    if n == QK + 3:
                        split_low(b + 1, 0)
                        split_low(b + 1, 1)
                    if n == VALUES + 1:
                        gate_prep(b + 1)
                    if n == VALUES + 3:
                        gate_log(b + 1)
                    if n == SUMS + 1:
                        sums(b + 1)
                    if n == EXPAND:
                        expand(b + 1, 1 - k)
                dia_copy(b, 1)
                finish(b, k, 1)

            batch(0, 0)
            with dve.Fori(1, B - 2, 2) as b:
                batch(b, 1)
                batch(b + 1, 0)
            batch(B - 1, 1, last=True)

        @block.tensor
        def _(pe):
            pe.sem_inc(s["pv_done"], AHEAD_PW)
            pe.wait_ge(s["consts"], 1)
            pe.wait_ge(s["w_scaled"], 2)
            for j in range(3):
                pe.transpose(M0[:, P * j:P * j + P], wn[:, j, :], ident[:, :])
            pe.transpose(M0[:, 384:400], wn[0:H, 3, :], ident[0:H, 0:H]).then_inc(s["w_T"], 1)
            pe.wait_ge(s["w_sb"], 6)

            def turn(bb, first=False):
                pe.wait_ge(s["xn_done"], TT * bb + TT)
                if not first:
                    pe.wait_ge(s["fin_done"], 2 * (bb - 1))
                for i in range(TT):
                    ins = pe.transpose(M0[:, P * i:P * i + P], xn[:, i, :], ident[:, :])
                ins.then_inc(s["xnT_ps"], 1)

            def project(bb):
                pe.wait_ge(s["xnT_sb"], bb + 1)
                for t, M in enumerate((M0, M1)):
                    pe.matmul(M[:, :], wT[:, t, :], xnT[:, :], start=True, stop=True).then_inc(s["qk_ps"], 1)

            def values(bb):
                pe.wait_ge(s["split_hi"], 2 * bb + 2)
                pe.wait_ge(s["split_rest"], 2 * bb + 2)
                for m in range(NM):
                    for par in range(2):
                        pe.matmul((M0, M1)[m // 4][L * par:L * par + L, 72 * (m % 4):72 * (m % 4) + 72],
                                  xnT[:, L * m:L * m + L], wvg[:, par, :], start=True, stop=True)
                for i in range(TT):
                    ins = pe.matmul(M0[:, 288 + H * i:288 + H * i + H], xnT[:, P * i:P * i + P], wgT[:, :],
                                    start=True, stop=True)
                ins.then_inc(s["v_ps"], 1)

            def sums(bb):
                pe.wait_ge(s["logg_done"], bb + 1)
                pe.wait_ge(s["v_sb"], 4 * bb + 4)
                pe.matmul(M0[:, 0:128], upto[:, :], logg[:, :], start=True, stop=True)
                pe.matmul(M0[:, 128:192], same[:, :], logg[:, 0:64], start=True, stop=True)\
                    .then_inc(s["cum_ps"], 1)

            def decay_sums(bb, m, first=False):
                pe.wait_ge(s["ramp_done"], NM * bb + m + 1)
                if m >= 2:
                    pe.wait_ge(s["decay_sb"], NM * bb + m - 1)
                elif first:
                    pe.wait_ge(s["cum_sb"], 6)
                    pe.wait_ge(s["tok_ps"], 1)
                else:
                    pe.wait_ge(s["fin_done"], 2 * (bb - 1) + 1)
                M = (M0, M1)[m % 2]
                pe.matmul(M[:, :], after[:, :], ramp[:, m % 2, :, :].rearrange("p a t -> p (a t)"),
                          start=True, stop=False)
                pe.matmul(M[:, :].rearrange("p (a t) -> p a t", t=L), ident_b[:, :],
                          never[:, :].unsqueeze(1).broadcast_to([P, NP, L]), start=False, stop=True)\
                    .then_inc(s["decay_ps"], 1)

            def scores(b, k, n):
                hf, m, qh = unit(n)
                if n == 0:
                    pe.wait_ge(s["feat_q"], 256 * b + 256)
                    pe.wait_ge(s["kx_done"], 2 * b + 2)
                pe.wait_ge(s["mag_done"], NU * b + n + 1)
                for l in range(2):
                    p = 4 * qh + 2 * l + hf
                    ins = pe.matmul(pS[:, 2 * (n % 2) + l, 0:width(m)], kf[:, k, p, m, :, :].rearrange("p x t -> p (x t)"),
                                    qf[:, k, p, L * m:T], start=True, stop=True)
                ins.then_inc(s["s_ps"], 1)

            def attend(b, k, n):
                hf, m, qh = unit(n)
                if n % (2 * NM) == 0:
                    pe.wait_ge(s["off_done"], 2 * b + hf)
                    pe.wait_ge(s["dia_done"], 2 * b + hf)
                if n == 0:
                    pe.wait_ge(s["w_misc"], 3)
                pe.wait_ge(s["pdg_done"], NU * b + n + 1)
                if hf == 0 and qh == 0 and m < NM - 1:
                    pe.wait_ge(s["vo_done"], 7 * b + m + 1)
                for l in range(2):
                    Q = 2 * qh + l
                    p = 2 * Q + hf
                    lo, hi = 32 * Q, 32 * Q + 18
                    w = pw[:, n % 4, 0:2 * width(m)].rearrange("p (l t) -> p l t", l=2)[:, l, :]
                    if m == 0:
                        pe.matmul(pOff[lo:hi, 0:L], zeros[:, :], pdg[:, n % 4, l, :], start=True, stop=False,
                                  skip_group_check=True)
                    for i in range(m + 1, NM):
                        pe.matmul(pOff[lo:hi, L * i:L * i + L], vo[:, vo_at(m, i), p, :],
                                  w[:, L * (i - m):L * (i - m) + L], start=False, stop=(m == NM - 2),
                                  skip_group_check=True)
                    ins = pe.matmul(pDia[lo:hi, L * m:L * m + L], vd[:, k, m, p, :], pdg[:, n % 4, l, :],
                                    start=(m == 0), stop=(m == NM - 1), skip_group_check=True)
                ins.then_inc(s["pv_done"], 1)

            def turn_back(b, hf, last=False):
                pe.wait_ge(s["off_done"], 2 * b + hf + 1)
                pe.wait_ge(s["dia_done"], 2 * b + hf + 1)
                if hf == 0:
                    if not isinstance(b, int) or b < B - 1:
                        pe.wait_ge(s["cum_sb"], 6 * (b + 1) + 6)
                        pe.wait_ge(s["tok_ps"], b + 2)
                elif last:
                    pe.wait_ge(s["fin_done"], 2 * b + 1)
                else:
                    pe.wait_ge(s["decay_sb"], NM * (b + 2))
                for src, M in ((off_sb, M0), (dia_sb, M1)):
                    for i in range(TT):
                        ins = pe.transpose(M[:, P * i:P * i + P], src[:, P * i:P * i + P], ident[:, :])
                ins.then_inc(s["fin_ps"], 1)

            turn(0, first=True)
            project(0)
            values(0)
            sums(0)
            for m in range(NM):
                decay_sums(0, m, first=True)
            scores(0, 0, 0)
            scores(0, 0, 1)

            def batch(b, k, last=False):
                for n in range(NU):
                    if n == FIN0:
                        turn_back(b, 0)
                    if not last:
                        if n == TURN:
                            turn(b + 1)
                        if n == QK:
                            project(b + 1)
                        if n == VALUES:
                            values(b + 1)
                        if n == SUMS:
                            sums(b + 1)
                        if DECAY <= n < DECAY + NM:
                            decay_sums(b + 1, n - DECAY)
                    if n + 2 < NU:
                        scores(b, k, n + 2)
                    elif not last:
                        scores(b + 1, 1 - k, n + 2 - NU)
                    attend(b, k, n)
                turn_back(b, 1, last)

            batch(0, 0)
            with pe.Fori(1, B - 2, 2) as b:
                batch(b, 1)
                batch(b + 1, 0)
            batch(B - 1, 1, last=True)


def experts(nc, x, xs_dram, ys_dram, s, keep, f, w_red, wg, w1, b1, w2, b2, out):
    with ExitStack() as ctx:
        def sb(name, shape, dt=F32):
            return ctx.enter_context(nc.sbuf_tensor(f"f{f}_" + name, shape, dt))

        def psum(name, shape):
            return ctx.enter_context(nc.psum_tensor(f"f{f}_" + name, shape, F32))

        def sem(name):
            return ctx.enter_context(nc.semaphore(name))

        xs_in, ws_in, ys_out = s["xs_in"], s["ws_in"], s["ys_out"]
        ident = keep["ident"]
        before = keep["before"]
        ones = keep["ones"]
        zero = keep["zero"]
        pref = keep["pref"]
        restart_e = keep["restart_e"]
        tile_at = keep["tile_at"]
        k_at = keep["k_at"]
        stats = sb("stats", [P, NT, 6])
        mv = sb("mv", [P, NT, 2])
        rstd = sb("rstd", [P, 4, NT])
        xa = sb("xa", [P, NT, C])
        rT = sb("rT", [P, 2, T])
        red = sb("red", [GD, 2, T])
        wred_sb = keep["wred_sb"]
        wg_sb = sb("wg_sb", [E, GD])
        wg_sq = sb("wg_sq", [E, GD])
        wg_n = sb("wg_n", [E, 4])
        wgT_s = keep["wgT_s"]
        b_in = sb("b_in", [E * NF + E, P])
        b1T = keep["b1T"]
        b2T = keep["b2T"]
        lg = sb("lg", [P, NT, E])
        lgx = sb("lgx", [P, NT, E])
        hit = sb("hit", [P, NT, E])
        top = sb("top", [P, NT])
        first = sb("first", [P, NT])
        score = sb("score", [P, NT])
        lsum = sb("lsum", [P, NT])
        oh = sb("oh", [P, E, NT])
        tot = sb("tot", [P, E, NT])
        cinc = sb("cinc", [P, E, NT])
        p_at = sb("p_at", [P, E, NT])
        more = sb("more", [P, E, NT * P // ST])
        n_til = sb("n_til", [P, E])
        ends = sb("ends", [P, E])
        base = sb("base", [P, E])
        pos_f = sb("pos_f", [P, NT])
        pos = sb("pos", [P, NT], I32)
        past = sb("past", [P, NS, E])
        texp_f = sb("texp_f", [P, NS])
        texp = sb("texp", [P, NS], I32)
        one8 = keep["one8"]
        xs = sb("xs", [P, 2, NC2, C])
        w1s = sb("w1s", [P, 2, F])
        w2s = sb("w2s", [P, 2, NF, C])
        b1s = sb("b1s", [P, 2, NF])
        b2s = sb("b2s", [P, 2, 1])
        xsT = sb("xsT", [P, 2, ST])
        hs = sb("hs", [P, 2, NF, ST])
        ysT = sb("ysT", [P, 2, ST])
        yo = sb("yo", [P, 2, NC2, C])
        bA = psum("bA", [P, T])
        bB = psum("bB", [P, T])
        bH = psum("bH", [P, 4, T])
        bY = psum("bY", [P, T])
        bO = psum("bO", [P, T])
        block = ctx.enter_context(nc.Block())

        @block.sync
        def _(sp):
            if f == 0:
                sp.dma_start(wred_sb[:, :], w_red).then_inc(s["fw_in"], 16)
                sp.dma_start(wg_sb[:, :], wg).then_inc(s["fw_in"], 16)
                sp.dma_start(b_in[0:E * NF, :], b1.rearrange("e (k p) -> (e k) p", p=P)).then_inc(s["fw_in"], 16)
                sp.dma_start(b_in[E * NF:E * NF + E, :], b2).then_inc(s["fw_in"], 16)
                sp.wait_ge(s["f_consts"], 1)
                for k in range(NS * ST // 1024 + 1):
                    n = min(1024, NS * ST - 1024 * k)
                    sp.dma_start(xs_dram[1024 * k:1024 * k + n, :].rearrange("(p a) c -> p (a c)", p=P),
                                 zero[:, 0:n // P * C]).then_inc(s["zero_done"], 16)

                sp.wait_ge(s["wgT_sb"], 3)

            def ffn(f):
                sp.wait_ge(s["texp_done"], f + 1)
                sp.wait_ge(s["scat_done"], 16 * NT * (f + 1))

                def tile(r, k):
                    j = 2 * r + k
                    g = NS * f + j
                    e = sp.value_load(texp[0:1, bass.ds(j, 1)], min_val=0, max_val=E - 1)
                    late = f > 0 or not isinstance(r, int) or r > 0
                    if late:
                        sp.wait_ge(s["x_ps"], g - 1)
                    sp.dma_start(xs[:, k, :, :], xs_dram[bass.ds(j * ST, ST), :]
                                 .rearrange("(a p) c -> p a c", p=P)).then_inc(xs_in[k], 16)
                    if late:
                        sp.wait_ge(s["h_sb"], g - 1)
                    sp.dma_start(w1s[:, k, :], w1[bass.ds(e, 1), :, :].rearrange("e p f -> p (e f)"))\
                        .then_inc(ws_in[k], 16)
                    sp.dma_start(b1s[:, k, :], b1T[:, bass.ds(e, 1), :].rearrange("p e k -> p (e k)"))\
                        .then_inc(ws_in[k], 16)
                    if late:
                        sp.wait_ge(s["y_sb"], g - 1)
                    sp.dma_start(w2s[:, k, :, :], w2[bass.ds(e, 1), :, :].rearrange("e (k p) d -> p (e k) d", p=P))\
                        .then_inc(ws_in[k], 16)
                    sp.dma_start(b2s[:, k, :], b2T[:, bass.ds(e, 1)]).then_inc(ws_in[k], 16)

                tile(0, 0)
                tile(0, 1)
                with sp.Fori(1, NS // 2) as r:
                    tile(r, 0)
                    tile(r, 1)
                tile(NS // 2, 0)

            ffn(f)
            if f == 1:
                sp.wait_ge(s["add_done"], 2 * NT)
                for k in range(B):
                    sp.dma_start(out[k].rearrange("(i p) c -> p i c", p=P),
                                 x[:, TT * k:TT * (k + 1), :]).then_inc(s["x_out"], 16)
                sp.wait_ge(s["x_out"], 16 * B)

        @block.gpsimd
        def _(pool):
            st = 0

            def step(ins):
                nonlocal st
                st += 1
                ins.then_inc(s["fc_step"], 1)
                pool.wait_ge(s["fc_step"], st)

            if f == 0:
                step(pool.memset(ident[:, :], 0.0))
                step(pool.memset(zero[:, :], 0.0))
                step(pool.memset(before[:, :], 1.0))
                step(pool.memset(ones[:, :], 1.0))
                step(pool.memset(one8[:, :], 1.0))
                step(pool.memset(restart_e[:, :, :], 1.0))
                step(pool.memset(restart_e[:, :, 0:1], 0.0))
                step(pool.affine_select(out=ident[:, :], in_=ident[:, :], compare_op=ALU.not_equal, fill=1.0,
                                        base=0, pattern=[[-1, P]], channel_multiplier=1))
                step(pool.affine_select(out=before[:, :], in_=before[:, :], compare_op=ALU.is_ge, fill=0.0,
                                        base=-1, pattern=[[1, P]], channel_multiplier=-1))
                step(pool.iota(pref[:, :], [[-1, E]], base=E, channel_multiplier=0,
                               allow_small_or_imprecise_dtypes=True))
                step(pool.iota(tile_at[:, :], [[1, NS]], base=0, channel_multiplier=0,
                               allow_small_or_imprecise_dtypes=True))
                step(pool.iota(k_at[:, :], [[ST, NT * P // ST]], base=0, channel_multiplier=0,
                               allow_small_or_imprecise_dtypes=True))
                pool.memset(zero[:, 0:1], 0.0).then_inc(s["f_consts"], 1)

            def ffn(f):
                pool.wait_ge(s["zero_done"], 16 * (NS * ST // 1024 + 1))
                pool.wait_ge(s["pos_done"], f + 1)
                for i in range(NT):
                    pool.indirect_dma_start(xs_dram[:, :], bass.IndirectOffsetOnAxis(ap=pos[:, i:i + 1], axis=0),
                                            xa[:, i, :], None).then_inc(s["scat_done"], 16)

                def store(r, k):
                    j = 2 * r + k
                    pool.wait_ge(s["o_sb"], NS * f + j + 1)
                    pool.dma_start(ys_dram[bass.ds(j * ST, ST), :].rearrange("(a p) c -> p a c", p=P),
                                   yo[:, k, :, :]).then_inc(ys_out[k], 16)

                with pool.Fori(0, NS // 2) as r:
                    store(r, 0)
                    store(r, 1)
                store(NS // 2, 0)
                for k in range(2):
                    pool.wait_ge(ys_out[k], 16 * SLOT_TILES[k] * (f + 1))
                pool.wait_ge(s["scat_done"], 16 * NT * (f + 1))
                for i in range(NT):
                    pool.indirect_dma_start(xa[:, i, :], None, ys_dram[:, :],
                                            bass.IndirectOffsetOnAxis(ap=pos[:, i:i + 1], axis=0))\
                        .then_inc(s["gat_done"], 16)

            ffn(f)

        @block.scalar
        def _(act):
            if f == 0:
                act.wait_ge(s["wg_step"], 1)
                act.activation(wg_n[:, 1:2], wg_n[:, 0:1], ACT.Sqrt).then_inc(s["wg_step"], 1)

            def ffn(f):
                act.wait_ge(s["rstd_step"], 6 * f + 1)
                act.activation(rstd[:, 2, :], rstd[:, 1, :], ACT.Sqrt).then_inc(s["rstd_step"], 1)
                for g in range(B):
                    q = B * f + g
                    act.wait_ge(s["rT_ps"], q + 1)
                    if q >= 2:
                        act.wait_ge(s["red_ps"], q - 1)
                    act.activation(rT[:, g % 2, :], bA[:, :], ACT.Copy).then_inc(s["rT_sb"], 1)
                act.wait_ge(s["lg_step"], 4 * f + 3)
                act.activation(lgx[:, :, :].rearrange("p i e -> p (i e)"),
                               lgx[:, :, :].rearrange("p i e -> p (i e)"), ACT.Exp).then_inc(s["lg_exp"], 1)

                def x_copy(r, k, late=True):
                    g = NS * f + 2 * r + k
                    act.wait_ge(s["x_ps"], g + 1)
                    if late:
                        act.wait_ge(s["h_ps"], g - 1)
                    act.activation(xsT[:, k, :], bA[:, 0:ST], ACT.Copy).then_inc(s["x_sb"], 1)

                def gelu(r, k, late=True):
                    g = NS * f + 2 * r + k
                    act.wait_ge(s["h_ps"], g + 1)
                    act.wait_ge(ws_in[k], 64 * (SLOT_TILES[k] * f + r + 1))
                    if late:
                        act.wait_ge(s["y_ps"], g - 1)
                    for q in range(NF):
                        ins = act.activation(hs[:, k, q, :], bH[:, 2 * k + q // 2, ST * (q % 2):ST * (q % 2) + ST],
                                             ACT.Gelu, bias=b1s[:, k, q:q + 1])
                    ins.then_inc(s["h_sb"], 1)

                x_copy(0, 0, late=f > 0)
                x_copy(0, 1, late=f > 0)
                gelu(0, 0, late=f > 0)
                x_copy(1, 0)
                gelu(0, 1, late=f > 0)
                with act.Fori(1, NS // 2) as r:
                    x_copy(r, 1)
                    gelu(r, 0)
                    x_copy(r + 1, 0)
                    gelu(r, 1)
                gelu(NS // 2, 0)

            ffn(f)

        @block.vector
        def _(dve):
            if f == 0:
                dve.wait_ge(s["fw_in"], 64)
                dve.tensor_tensor_reduce(wg_sq[:, :], wg_sb[:, :], wg_sb[:, :], 1.0, 0.0, ALU.mult, ALU.add,
                                         wg_n[:, 0:1]).then_inc(s["wg_step"], 1)
                dve.wait_ge(s["wg_step"], 2)
                dve.tensor_scalar(wg_n[:, 2:3], wg_n[:, 1:2], EPS_G, None, ALU.max).then_inc(s["wg_step"], 1)
                dve.wait_ge(s["wg_step"], 3)
                dve.reciprocal(wg_n[:, 3:4], wg_n[:, 2:3]).then_inc(s["wg_step"], 1)
                dve.wait_ge(s["wg_step"], 4)
                dve.tensor_scalar(wg_sq[:, :], wg_sb[:, :], wg_n[:, 3:4], None, ALU.mult).then_inc(s["wg_step"], 1)
                dve.wait_ge(s["wgT_ps"], 1)
                dve.tensor_copy(wgT_s[:, :], bB[0:GD, 0:E]).then_inc(s["wgT_sb"], 1)
                dve.tensor_copy(b1T[:, :, :].rearrange("p e k -> p (e k)"), bB[:, 64:64 + E * NF]).then_inc(s["wgT_sb"], 1)
                dve.tensor_copy(b2T[:, :], bB[:, 64 + E * NF:64 + E * NF + E]).then_inc(s["wgT_sb"], 1)

            def layernorm(f):
                n0 = 2 * NT * f
                for i in range(NT):
                    dve.bn_stats(stats[:, i, :], x[:, i, :]).then_inc(s["stat_done"], 1)
                for i in range(NT):
                    dve.wait_ge(s["stat_done"], n0 + i + 1)
                    dve.bn_aggr(mv[:, i, :], stats[:, i, :]).then_inc(s["stat_done"], 1)
                dve.wait_ge(s["stat_done"], n0 + 2 * NT)
                dve.tensor_scalar(rstd[:, 1, :], mv[:, :, 1], EPS_LN, None, ALU.add).then_inc(s["rstd_step"], 1)
                dve.wait_ge(s["rstd_step"], 6 * f + 2)
                dve.reciprocal(rstd[:, 3, :], rstd[:, 2, :]).then_inc(s["rstd_step"], 1)
                dve.wait_ge(s["rstd_step"], 6 * f + 3)
                dve.tensor_tensor(rstd[:, 2, :], rstd[:, 3, :], rstd[:, 3, :], ALU.mult).then_inc(s["rstd_step"], 1)
                dve.wait_ge(s["rstd_step"], 6 * f + 4)
                dve.tensor_tensor(rstd[:, 2, :], rstd[:, 2, :], rstd[:, 1, :], ALU.mult).then_inc(s["rstd_step"], 1)
                dve.wait_ge(s["rstd_step"], 6 * f + 5)
                dve.tensor_scalar(rstd[:, 2, :], rstd[:, 2, :], -0.5, 1.5, ALU.mult, ALU.add)\
                    .then_inc(s["rstd_step"], 1)
                dve.wait_ge(s["rstd_step"], 6 * f + 6)
                dve.tensor_tensor(rstd[:, 0, :], rstd[:, 2, :], rstd[:, 3, :], ALU.mult).then_inc(s["rstd_ready"], 1)

            def ffn(f):
                layernorm(f)
                dve.wait_ge(s["rstd_ready"], f + 1)
                for i in range(NT):
                    dve.tensor_scalar(xa[:, i, :], x[:, i, :], mv[:, i, 0:1], rstd[:, 0, i:i + 1],
                                      ALU.subtract, ALU.mult).then_inc(s["xnf_done"], 1)
                for g in range(B):
                    q = B * f + g
                    dve.wait_ge(s["red_ps"], q + 1)
                    if q >= 2:
                        dve.wait_ge(s["lg_ps"], q - 1)
                    dve.tensor_copy(red[:, g % 2, :], bB[0:GD, :]).then_inc(s["red_sb"], 1)
                dve.wait_ge(s["lg_ps"], B * (f + 1))
                dve.tensor_copy(lg[:, :, :].rearrange("p i e -> p (i e)"), bY[:, 0:NT * E]).then_inc(s["lg_step"], 1)
                dve.wait_ge(s["lg_step"], 4 * f + 1)
                dve.tensor_reduce(top[:, :], lg[:, :, :], AX.X, ALU.max).then_inc(s["lg_step"], 1)
                dve.wait_ge(s["lg_step"], 4 * f + 2)
                tb = top[:, :].unsqueeze(2).broadcast_to([P, NT, E])
                dve.tensor_tensor(lgx[:, :, :], lg[:, :, :], tb, ALU.subtract).then_inc(s["lg_step"], 1)
                dve.tensor_tensor(hit[:, :, :], lg[:, :, :], tb, ALU.is_equal).then_inc(s["lg_step"], 1)
                dve.wait_ge(s["lg_step"], 4 * f + 4)
                n0 = 5 * f
                dve.tensor_tensor(hit[:, :, :], hit[:, :, :], pref[:, :].unsqueeze(1).broadcast_to([P, NT, E]),
                                  ALU.mult).then_inc(s["oh_done"], 1)
                dve.wait_ge(s["oh_done"], n0 + 1)
                dve.tensor_reduce(first[:, :], hit[:, :, :], AX.X, ALU.max).then_inc(s["oh_done"], 1)
                dve.wait_ge(s["oh_done"], n0 + 2)
                dve.tensor_tensor(oh[:, :, :], pref[:, :].unsqueeze(2).broadcast_to([P, E, NT]),
                                  first[:, :].unsqueeze(1).broadcast_to([P, E, NT]), ALU.is_equal)\
                    .then_inc(s["oh_done"], 1)
                dve.wait_ge(s["lg_exp"], f + 1)
                dve.tensor_reduce(lsum[:, :], lgx[:, :, :], AX.X, ALU.add).then_inc(s["oh_done"], 1)
                dve.wait_ge(s["oh_done"], n0 + 4)
                dve.reciprocal(score[:, :], lsum[:, :]).then_inc(s["oh_done"], 1)
                dve.wait_ge(s["rank_ps"], f + 1)
                at = 12 * f

                def step(ins):
                    nonlocal at
                    at += 1
                    ins.then_inc(s["pos_step"], 1)
                    dve.wait_ge(s["pos_step"], at)

                flat = [t[:, :, :].rearrange("p e i -> p (e i)") for t in (tot, cinc, restart_e)]
                step(dve.tensor_copy(flat[0], bA[:, 256:512]))
                step(dve.tensor_tensor_scan(flat[1], flat[2], flat[0], 0.0, ALU.mult, ALU.add))
                nk = NT * P // ST
                step(dve.tensor_tensor(more[:, :, :], cinc[:, :, NT - 1:NT].broadcast_to([P, E, nk]),
                                       k_at[:, :].unsqueeze(1).broadcast_to([P, E, nk]), ALU.is_gt))
                step(dve.tensor_reduce(n_til[:, :], more[:, :, :], AX.X, ALU.add))
                step(dve.tensor_tensor_scan(ends[:, :], one8[:, :], n_til[:, :], 0.0, ALU.mult, ALU.add))
                step(dve.tensor_tensor(base[:, :], ends[:, :], n_til[:, :], ALU.subtract))
                step(dve.tensor_tensor(p_at[:, :, :], cinc[:, :, :], tot[:, :, :], ALU.subtract))
                step(dve.scalar_tensor_tensor(p_at[:, :, :], base[:, :].unsqueeze(2).broadcast_to([P, E, NT]),
                                              float(ST), p_at[:, :, :], ALU.mult, ALU.add))
                pf = p_at[:, :, :].rearrange("p e i -> p (e i)")
                step(dve.tensor_tensor(pf, bA[:, 0:256], pf, ALU.add))
                step(dve.tensor_tensor(p_at[:, :, :], p_at[:, :, :], oh[:, :, :], ALU.mult))
                step(dve.tensor_reduce(pos_f[:, :], p_at[:, :, :].rearrange("p e i -> p i e"), AX.X, ALU.add))
                dve.tensor_copy(pos[:, :], pos_f[:, :]).then_inc(s["pos_done"], 1)
                step(dve.tensor_tensor(past[:, :, :], tile_at[:, :].unsqueeze(2).broadcast_to([P, NS, E]),
                                       ends[:, :].unsqueeze(1).broadcast_to([P, NS, E]), ALU.is_ge))
                dve.tensor_reduce(texp_f[:, :], past[:, :, :], AX.X, ALU.add).then_inc(s["lg_sum"], 1)
                dve.wait_ge(s["lg_sum"], f + 1)
                dve.tensor_scalar(texp[:, :], texp_f[:, :], float(E - 1), None, ALU.min)\
                    .then_inc(s["texp_done"], 1)

                def y_bias(r, k, late=True):
                    g = NS * f + 2 * r + k
                    dve.wait_ge(s["y_ps"], g + 1)
                    dve.wait_ge(ws_in[k], 64 * (SLOT_TILES[k] * f + r + 1))
                    if late:
                        dve.wait_ge(s["o_ps"], g - 1)
                    dve.tensor_scalar(ysT[:, k, :], bY[:, 0:ST], b2s[:, k, 0:1], None, ALU.add)\
                        .then_inc(s["y_sb"], 1)

                def y_out(r, k, late=True):
                    g = NS * f + 2 * r + k
                    dve.wait_ge(s["o_ps"], g + 1)
                    if late:
                        dve.wait_ge(ys_out[k], 16 * (SLOT_TILES[k] * f + r))
                    dve.tensor_copy(yo[:, k, :, :].rearrange("p a c -> p (a c)"), bO[:, 0:ST])\
                        .then_inc(s["o_sb"], 1)

                y_bias(0, 0, late=f > 0)
                y_out(0, 0, late=f > 0)
                y_bias(0, 1, late=f > 0)
                y_out(0, 1, late=f > 0)
                with dve.Fori(1, NS // 2) as r:
                    for k in range(2):
                        y_bias(r, k)
                        y_out(r, k)
                y_bias(NS // 2, 0)
                y_out(NS // 2, 0)
                for i in range(NT):
                    dve.wait_ge(s["gat_done"], 16 * NT * (f + 1))
                    dve.scalar_tensor_tensor(x[:, i, :], xa[:, i, :], score[:, i:i + 1], x[:, i, :],
                                             ALU.mult, ALU.add).then_inc(s["add_done"], 1)

            ffn(f)

        @block.tensor
        def _(pe):
            if f == 0:
                pe.wait_ge(s["f_consts"], 1)
                pe.wait_ge(s["wg_step"], 5)
                pe.transpose(bB[:, 64:64 + E * NF + E], b_in[:, :], ident[0:E * NF + E, 0:E * NF + E])
                pe.transpose(bB[0:GD, 0:E], wg_sq[:, :], ident[0:E, 0:E]).then_inc(s["wgT_ps"], 1)
                pe.wait_ge(s["wgT_sb"], 3)

            def ffn(f):
                for g in range(B):
                    q = B * f + g
                    pe.wait_ge(s["xnf_done"], NT * f + TT * g + TT)
                    pe.wait_ge(s["rT_sb"], q)
                    for i in range(TT):
                        ins = pe.transpose(bA[:, P * i:P * i + P], xa[:, TT * g + i, :], ident[:, :])
                    ins.then_inc(s["rT_ps"], 1)
                    pe.wait_ge(s["rT_sb"], q + 1)
                    pe.wait_ge(s["red_sb"], q)
                    pe.matmul(bB[0:GD, :], wred_sb[:, :], rT[:, g % 2, :], start=True, stop=True)\
                        .then_inc(s["red_ps"], 1)
                    pe.wait_ge(s["red_sb"], q + 1)
                    for i in range(TT):
                        c = E * (TT * g + i)
                        ins = pe.matmul(bY[:, c:c + E], red[:, g % 2, P * i:P * i + P], wgT_s[:, :],
                                        start=True, stop=True)
                    ins.then_inc(s["lg_ps"], 1)
                pe.wait_ge(s["oh_done"], 5 * f + 3)
                ohf = oh[:, :, :].rearrange("p e i -> p (e i)")
                pe.matmul(bA[:, 0:256], before[:, :], ohf, start=True, stop=True)
                pe.matmul(bA[:, 256:512], ones[:, :], ohf, start=True, stop=True).then_inc(s["rank_ps"], 1)
                pe.wait_ge(s["pos_done"], f + 1)

                def turn_x(r, k):
                    g = NS * f + 2 * r + k
                    pe.wait_ge(xs_in[k], 16 * (SLOT_TILES[k] * f + r + 1))
                    if f > 0 or k > 0 or not isinstance(r, int) or r > 0:
                        pe.wait_ge(s["x_sb"], g)
                    for a in range(NC2):
                        ins = pe.transpose(bA[:, P * a:P * a + P], xs[:, k, a, :], ident[:, :])
                    ins.then_inc(s["x_ps"], 1)

                def up(r, k, late=True):
                    g = NS * f + 2 * r + k
                    pe.wait_ge(ws_in[k], 64 * (SLOT_TILES[k] * f + r + 1))
                    pe.wait_ge(s["x_sb"], g + 1)
                    if late:
                        pe.wait_ge(s["h_sb"], g - 1)
                    for q in range(NF):
                        ins = pe.matmul(bH[:, 2 * k + q // 2, ST * (q % 2):ST * (q % 2) + ST],
                                        w1s[:, k, P * q:P * q + P], xsT[:, k, :], start=True, stop=True)
                    ins.then_inc(s["h_ps"], 1)

                def down(r, k, late=True):
                    g = NS * f + 2 * r + k
                    pe.wait_ge(s["h_sb"], g + 1)
                    if late:
                        pe.wait_ge(s["y_sb"], g)
                    for q in range(NF):
                        ins = pe.matmul(bY[:, 0:ST], w2s[:, k, q, :], hs[:, k, q, :], start=(q == 0),
                                        stop=(q == NF - 1))
                    ins.then_inc(s["y_ps"], 1)

                def turn_y(r, k, late=True):
                    g = NS * f + 2 * r + k
                    pe.wait_ge(s["y_sb"], g + 1)
                    if late:
                        pe.wait_ge(s["o_sb"], g)
                    for a in range(NC2):
                        ins = pe.transpose(bO[:, P * a:P * a + P], ysT[:, k, P * a:P * a + P], ident[:, :])
                    ins.then_inc(s["o_ps"], 1)

                turn_x(0, 0)
                turn_x(0, 1)
                up(0, 0, late=f > 0)
                turn_x(1, 0)
                up(0, 1, late=f > 0)
                down(0, 0, late=f > 0)

                def pair(r, late=True):
                    turn_x(r, 1)
                    up(r, 0)
                    turn_y(r - 1, 0, late)
                    down(r - 1, 1)
                    turn_x(r + 1, 0)
                    up(r, 1)
                    turn_y(r - 1, 1)
                    down(r, 0)

                pair(1, late=f > 0)
                with pe.Fori(2, NS // 2) as r:
                    pair(r)
                up(NS // 2, 0)
                turn_y(NS // 2 - 1, 0)
                down(NS // 2 - 1, 1)
                turn_y(NS // 2 - 1, 1)
                down(NS // 2, 0)
                turn_y(NS // 2, 0)

            ffn(f)


def delta_rule(nc, x, Wq, Wk, Wv, Wgamma, Wf, Wg1, Wg2, Wo, norm_w):
    with ExitStack() as ctx:
        def sb(name, shape, dt=F32):
            return ctx.enter_context(nc.sbuf_tensor("d_" + name, shape, dt))

        def psum(name, shape):
            return ctx.enter_context(nc.psum_tensor("d_" + name, shape, F32))

        def sem(name):
            return ctx.enter_context(nc.semaphore(name))

        head_dram = nc.dram_tensor("head_dram", [3, B, P, T], F32, kind="Internal").ap()
        fg_dram = nc.dram_tensor("fg_dram", [2, B, H, T], F32, kind="Internal").ap()
        o_dram = nc.dram_tensor("o_dram", [B, P, T], F32, kind="Internal").ap()
        s = {}
        for n in """cc_step c_consts stat_done rstd_step rstd_ready cw_in cn_done cT_ps cT_sb
            cq_ps cq_sb cf_ps cf_sb cg1_ps cg1_sb cg2_ps cg2_sb cq_out cf_out bh_in knorm_step knorm_sq kn_done
            fg_sig decay_step kk_step kk_pool qk_mul qk_red w_step u_pool u_done chain po_mul po_done o_red
            o_out gate_sig og_done wo_step cs_ps oy_ps ost_step o_sqrt ost_done""".split():
            s[n] = sem("d_" + n)
        o_in = [sem(f"o_in{k}") for k in range(3)]
        ident = sb("ident", [P, P])
        ones = sb("ones", [P, P])
        stats = sb("stats", [P, NT, 6])
        mv = sb("mv", [P, NT, 2])
        rstd = sb("rstd", [P, 4, NT])
        wqkv = sb("wqkv", [P, 3, C])
        wfg = sb("wfg", [P, 2 * H])
        wg1 = sb("wg1", [P, HD])
        wg2 = sb("wg2", [HD, C])
        wo = sb("wo", [P, C])
        nw = sb("nw", [P, 1])
        wcol = sb("wcol", [P, C])
        act3 = sb("act3", [P, 3, T])
        gate = sb("gate", [P, B, T])
        Q = sb("Q", [P, HD, T])
        K = sb("K", [P, HD, T])
        V = sb("V", [P, HD, T])
        W = sb("W", [P, HD, T])
        O = W
        fg = sb("fg", [P, 2, T])
        alpha = sb("alpha", [P, T])
        beta = sb("beta", [P, T])
        G = sb("G", [P, CH, CH + 1, NCH])
        LL = sb("LL", [P, CH, CH, NCH])
        QQ = sb("QQ", [P, CH, CH, NCH])
        pb_d = sb("pb_d", [P, CH * HD * NCH])
        pb_p = sb("pb_p", [P, CH * HD * NCH])
        cn = pb_d[:, 0:2 * T].rearrange("p (k i c) -> p k i c", k=2, c=C)
        cT = pb_p[:, 0:T]
        fgl = pb_p[0:2 * H, T:2 * T]
        red1 = pb_p[0:HD, 2 * T:3 * T]
        S = sb("S", [P, 4, HD, HD])
        uw = sb("uw", [P, CH, HD])
        sr = sb("sr", [P, HD, HD])
        og = act3
        ost = sb("ost", [P, TT, 6])
        omv = sb("omv", [P, TT, 2])
        ors = sb("ors", [P, 4, TT])
        c0 = psum("c0", [P, T])
        c1 = psum("c1", [P, T])
        c2 = psum("c2", [P, T])
        c3 = psum("c3", [P, T])
        c4 = psum("c4", [P, T])
        c5 = psum("c5", [P, T])
        c6 = psum("c6", [P, T])
        cqkv = (c1, c2, c3)
        block = ctx.enter_context(nc.Block())

        def chunked(t, first=0, n=CH):
            return t[:, :, :].rearrange("p d (c j) -> p j c d", j=CH)[:, first:first + n]

        @block.sync
        def _(sp):
            for i, w in enumerate((Wq, Wk, Wv)):
                sp.dma_start(wqkv[:, i, :], w).then_inc(s["cw_in"], 16)
            sp.dma_start(wfg[:, 0:H], Wf).then_inc(s["cw_in"], 16)
            sp.dma_start(wfg[:, H:2 * H], Wgamma).then_inc(s["cw_in"], 16)
            sp.dma_start(wg1[:, :], Wg1).then_inc(s["cw_in"], 16)
            sp.dma_start(wg2[:, :], Wg2).then_inc(s["cw_in"], 16)
            sp.dma_start(wo[:, :], Wo).then_inc(s["cw_in"], 16)
            sp.dma_start(nw[:, :], norm_w.rearrange("(p a) -> p a", a=1)).then_inc(s["cw_in"], 16)

            def relayout():
                for b in range(B):
                    sp.wait_ge(s["cq_sb"], 3 * b + 3)
                    for i in range(3):
                        sp.dma_start(head_dram[i, b], act3[:, i, :]).then_inc(s["cq_out"], 16)
                    sp.wait_ge(s["cf_sb"], b + 1)
                    for i in range(2):
                        sp.dma_start(fg_dram[i, b], fgl[H * i:H * i + H, :]).then_inc(s["cf_out"], 16)
                sp.wait_ge(s["cf_out"], 32 * B)
                sp.dma_start(fg[:, 0, :], fg_dram[0].rearrange("b h t -> (b h) t")).then_inc(s["bh_in"], 16)
                sp.dma_start(fg[:, 1, :], fg_dram[1].rearrange("b h t -> (b h) t")).then_inc(s["bh_in"], 16)
                sp.wait_ge(s["cq_out"], 48 * B)
                for i, t in ((1, K), (0, Q), (2, V)):
                    sp.dma_start(t[:, :, :].rearrange("p d t -> p (d t)"),
                                 head_dram[i].rearrange("b (h d) t -> (b h) (d t)", d=HD)).then_inc(s["bh_in"], 16)

            def back():
                sp.wait_ge(s["o_red"], NCH)
                for b in range(B):
                    sp.dma_start(o_dram[b].rearrange("(h d) t -> h (d t)", d=HD),
                                 O[H * b:H * b + H, :, :].rearrange("p d t -> p (d t)")).then_inc(s["o_out"], 16)
                sp.wait_ge(s["o_out"], 16 * B)
                for b in range(B):
                    if b >= 3:
                        sp.wait_ge(s["oy_ps"], b - 2)
                    sp.dma_start(og[:, b % 3, :], o_dram[b]).then_inc(o_in[b % 3], 16)

            relayout()
            back()

        @block.gpsimd
        def _(pool):
            st = 0

            def step(ins):
                nonlocal st
                st += 1
                ins.then_inc(s["cc_step"], 1)
                pool.wait_ge(s["cc_step"], st)

            step(pool.memset(ident[:, :], 0.0))
            step(pool.memset(ones[:, :], 1.0))
            step(pool.memset(QQ[:, :, :, :].rearrange("p j i c -> p (j i c)"), 0.0))
            step(pool.memset(G[:, :, :, :].rearrange("p j i c -> p (j i c)"), 1.0))
            step(pool.memset(S[:, 0, :, :].rearrange("p v k -> p (v k)"), 0.0))
            pool.affine_select(out=ident[:, :], in_=ident[:, :], compare_op=ALU.not_equal, fill=1.0,
                               base=0, pattern=[[-1, P]], channel_multiplier=1).then_inc(s["c_consts"], 1)

            def products():
                pool.wait_ge(s["bh_in"], 80)
                pool.wait_ge(s["kn_done"], 1)
                for j in range(CH):
                    n = j + 1
                    if j:
                        pool.wait_ge(s["qk_red"], j)
                    pool.tensor_tensor(pb_p[:, 0:512 * n].rearrange("p (i c d) -> p i c d", c=NCH, d=HD),
                                       chunked(K, 0, n), chunked(Q, j, 1).broadcast_to([P, n, NCH, HD]), ALU.mult)\
                        .then_inc(s["qk_mul"], 1)
                pool.wait_ge(s["kk_step"], 1)
                pool.wait_ge(s["qk_red"], CH)
                n = 0
                for i in range(CH - 1):
                    m = CH - 1 - i
                    t = pb_p[:, 0:512 * m].rearrange("p (j c d) -> p j c d", c=NCH, d=HD)
                    if n:
                        pool.wait_ge(s["u_pool"], n)
                    pool.tensor_tensor(t, LL[:, i + 1:CH, i, :].unsqueeze(3).broadcast_to([P, m, NCH, HD]),
                                       chunked(V, i, 1).broadcast_to([P, m, NCH, HD]), ALU.mult)\
                        .then_inc(s["u_pool"], 1)
                    pool.wait_ge(s["u_pool"], n + 1)
                    pool.tensor_tensor(chunked(V, i + 1, m), chunked(V, i + 1, m), t, ALU.add)\
                        .then_inc(s["u_pool"], 1)
                    n += 2

            def outputs(r, a):
                c = 4 * r + a
                cs = bass.ds(CH * c, CH)
                po = pb_p[:, 2048 * (a % 2):2048 * (a % 2) + 1024].rearrange("p (j v k) -> p j v k", v=HD, k=16)
                fo = pb_p[:, 2048 * (a % 2) + 1024:2048 * (a % 2) + 1536].rearrange("p (j v k) -> p j v k", v=HD, k=8)
                pool.wait_ge(s["chain"], 6 * c + 1)
                if not (isinstance(r, int) and r == 0 and a < 2):
                    pool.wait_ge(s["o_red"], c - 1)
                pool.tensor_tensor(po[:, :, :, 0:8],
                                   Q[:, :, cs].rearrange("p k j -> p j k").unsqueeze(2).broadcast_to([P, CH, HD, HD]),
                                   S[:, a, :, :].unsqueeze(1).broadcast_to([P, CH, HD, HD]), ALU.mult)\
                    .then_inc(s["po_mul"], 1)
                pool.wait_ge(s["chain"], 6 * c + 4)
                pool.tensor_tensor(po[:, :, :, 8:16],
                                   QQ[:, :, :, bass.ds(c, 1)].rearrange("p j i c -> p j (i c)").unsqueeze(2)
                                   .broadcast_to([P, CH, HD, CH]),
                                   V[:, :, cs].unsqueeze(1).broadcast_to([P, CH, HD, CH]), ALU.mult)\
                    .then_inc(s["po_mul"], 1)
                pool.wait_ge(s["po_mul"], 2 * c + 2)
                pool.tensor_tensor(fo, po[:, :, :, 0:8], po[:, :, :, 8:16], ALU.add).then_inc(s["po_done"], 1)

            products()
            for a in range(4):
                outputs(0, a)
            with pool.Fori(1, NCH // 4) as r:
                for a in range(4):
                    outputs(r, a)

        @block.scalar
        def _(act):
            act.wait_ge(s["rstd_step"], 1)
            act.activation(rstd[:, 2, :], rstd[:, 1, :], ACT.Sqrt).then_inc(s["rstd_step"], 1)

            for b in range(B):
                act.wait_ge(s["cT_ps"], b + 1)
                if b:
                    act.wait_ge(s["cg1_ps"], b)
                act.activation(cT[:, :], c0[:, :], ACT.Copy).then_inc(s["cT_sb"], 1)
                if b:
                    act.wait_ge(s["cf_out"], 32 * b)
                    act.wait_ge(s["cq_out"], 48 * b)
                for i in range(3):
                    act.wait_ge(s["cq_ps"], 3 * b + i + 1)
                    act.activation(act3[:, i, :], cqkv[i][:, :], ACT.Silu).then_inc(s["cq_sb"], 1)
                act.wait_ge(s["cf_ps"], b + 1)
                act.activation(fgl[:, :], c4[0:2 * H, :], ACT.Copy).then_inc(s["cf_sb"], 1)
                act.wait_ge(s["cg1_ps"], b + 1)
                act.activation(red1[:, :], c5[0:HD, :], ACT.Copy).then_inc(s["cg1_sb"], 1)
                act.wait_ge(s["cg2_ps"], b + 1)
                act.activation(gate[:, b, :], c6[:, :], ACT.Copy).then_inc(s["cg2_sb"], 1)
            act.wait_ge(s["bh_in"], 80)
            act.wait_ge(s["knorm_step"], 2)
            act.activation(alpha[:, :], beta[:, :], ACT.Sqrt).then_inc(s["knorm_sq"], 1)
            act.activation(fg[:, :, :].rearrange("p a t -> p (a t)"), fg[:, :, :].rearrange("p a t -> p (a t)"),
                           ACT.Sigmoid).then_inc(s["fg_sig"], 1)
            act.wait_ge(s["cg2_sb"], B)
            act.activation(gate[:, :, :].rearrange("p b t -> p (b t)"), gate[:, :, :].rearrange("p b t -> p (b t)"),
                           ACT.Sigmoid).then_inc(s["gate_sig"], 1)
            for b in range(B):
                act.wait_ge(s["ost_step"], 7 * b + 1)
                act.activation(ors[:, 1, :], ors[:, 0, :], ACT.Sqrt).then_inc(s["o_sqrt"], 1)

        @block.vector
        def _(dve):
            for i in range(NT):
                dve.bn_stats(stats[:, i, :], x[:, i, :]).then_inc(s["stat_done"], 1)
            for i in range(NT):
                dve.wait_ge(s["stat_done"], i + 1)
                dve.bn_aggr(mv[:, i, :], stats[:, i, :]).then_inc(s["stat_done"], 1)
            dve.wait_ge(s["stat_done"], 2 * NT)
            dve.tensor_scalar(rstd[:, 1, :], mv[:, :, 1], EPS_LN, None, ALU.add).then_inc(s["rstd_step"], 1)
            dve.wait_ge(s["rstd_step"], 2)
            dve.reciprocal(rstd[:, 3, :], rstd[:, 2, :]).then_inc(s["rstd_step"], 1)
            dve.wait_ge(s["rstd_step"], 3)
            dve.tensor_tensor(rstd[:, 2, :], rstd[:, 3, :], rstd[:, 3, :], ALU.mult).then_inc(s["rstd_step"], 1)
            dve.wait_ge(s["rstd_step"], 4)
            dve.tensor_tensor(rstd[:, 2, :], rstd[:, 2, :], rstd[:, 1, :], ALU.mult).then_inc(s["rstd_step"], 1)
            dve.wait_ge(s["rstd_step"], 5)
            dve.tensor_scalar(rstd[:, 2, :], rstd[:, 2, :], -0.5, 1.5, ALU.mult, ALU.add).then_inc(s["rstd_step"], 1)
            dve.wait_ge(s["rstd_step"], 6)
            dve.tensor_tensor(rstd[:, 0, :], rstd[:, 2, :], rstd[:, 3, :], ALU.mult).then_inc(s["rstd_ready"], 1)
            dve.wait_ge(s["rstd_ready"], 1)
            for b in range(B):
                if b >= 2:
                    dve.wait_ge(s["cT_ps"], b - 1)
                for i in range(TT):
                    j = TT * b + i
                    dve.tensor_scalar(cn[:, b % 2, i, :], x[:, j, :], mv[:, j, 0:1], rstd[:, 0, j:j + 1],
                                      ALU.subtract, ALU.mult).then_inc(s["cn_done"], 1)

            dve.wait_ge(s["bh_in"], 80)
            dve.tensor_tensor(pb_d[:, 0:HD * T].rearrange("p (d t) -> p d t", d=HD), K[:, :, :], K[:, :, :],
                              ALU.mult).then_inc(s["knorm_step"], 1)
            dve.wait_ge(s["knorm_step"], 1)
            dve.tensor_reduce(beta[:, :], pb_d[:, 0:HD * T].rearrange("p (d t) -> p t d", d=HD), AX.X, ALU.add)\
                .then_inc(s["knorm_step"], 1)
            dve.wait_ge(s["knorm_sq"], 1)
            dve.tensor_scalar(beta[:, :], alpha[:, :], EPS_K, None, ALU.max).then_inc(s["knorm_step"], 1)
            dve.wait_ge(s["knorm_step"], 3)
            dve.reciprocal(alpha[:, :], beta[:, :]).then_inc(s["knorm_step"], 1)
            dve.wait_ge(s["knorm_step"], 4)
            dve.tensor_tensor(K[:, :, :], K[:, :, :], alpha[:, :].unsqueeze(1).broadcast_to([P, HD, T]), ALU.mult)\
                .then_inc(s["kn_done"], 1)
            dve.wait_ge(s["fg_sig"], 1)
            dve.wait_ge(s["c_consts"], 1)
            dn = 0

            def dstep(ins):
                nonlocal dn
                dn += 1
                ins.then_inc(s["decay_step"], 1)
                dve.wait_ge(s["decay_step"], dn)

            f, gm = fg[:, 0, :], fg[:, 1, :]
            fj = f.rearrange("p (c j) -> p j c", j=CH)
            dve.wait_ge(s["kn_done"], 1)
            dstep(dve.scalar_tensor_tensor(alpha[:, :], f, -1.0, f, ALU.mult, ALU.mult))
            dstep(dve.tensor_tensor(alpha[:, :], alpha[:, :], gm, ALU.mult))
            dstep(dve.tensor_copy(G[:, 0, 0, :], fj[:, 0, :]))
            for j in range(1, CH):
                dstep(dve.tensor_tensor(G[:, j, 0:j + 1, :], G[:, j - 1, 0:j + 1, :],
                                        fj[:, j:j + 1, :].broadcast_to([P, j + 1, NCH]), ALU.mult))
            aj = alpha[:, :].rearrange("p (c j) -> p j c", j=CH)
            bj = beta[:, :].rearrange("p (c j) -> p j c", j=CH)
            dstep(dve.tensor_copy(beta[:, :], alpha[:, :]))
            dstep(dve.tensor_tensor(bj[:, 1:CH, :], aj[:, 1:CH, :], G[:, 0:CH - 1, 0, :], ALU.mult))
            dstep(dve.tensor_tensor(W[:, :, :], K[:, :, :], beta[:, :].unsqueeze(1).broadcast_to([P, HD, T]),
                                    ALU.mult))

            kn = 0
            for j in range(CH):
                if j:
                    t = pb_d[:, 0:512 * j].rearrange("p (i c d) -> p i c d", c=NCH, d=HD)
                    dve.tensor_tensor(t, chunked(K, 0, j), chunked(K, j, 1).broadcast_to([P, j, NCH, HD]), ALU.mult)\
                        .then_inc(s["kk_pool"], 1)
                    dve.wait_ge(s["kk_pool"], 3 * j - 2)
                    dve.tensor_reduce(LL[:, j, 0:j, :], t, AX.X, ALU.add).then_inc(s["kk_pool"], 1)
                    dve.wait_ge(s["kk_pool"], 3 * j - 1)
                    dve.tensor_tensor(LL[:, j, 0:j, :], LL[:, j, 0:j, :], G[:, j - 1, 1:j + 1, :], ALU.mult)\
                        .then_inc(s["kk_pool"], 1)
                    dve.wait_ge(s["kk_pool"], 3 * j)
                    ins = dve.tensor_tensor(LL[:, j, 0:j, :], LL[:, j, 0:j, :],
                                            aj[:, j:j + 1, :].broadcast_to([P, j, NCH]), ALU.mult)
                    if j == CH - 1:
                        ins.then_inc(s["kk_step"], 1)
                dve.wait_ge(s["qk_mul"], j + 1)
                n = j + 1
                dve.tensor_reduce(QQ[:, j, 0:n, :],
                                  pb_p[:, 0:512 * n].rearrange("p (i c d) -> p i c d", c=NCH, d=HD), AX.X, ALU.add)\
                    .then_inc(s["qk_red"], 1)
            dve.wait_ge(s["qk_red"], CH)
            for j in range(CH):
                ins = dve.tensor_tensor(QQ[:, j, 0:j + 1, :], QQ[:, j, 0:j + 1, :], G[:, j, 1:j + 2, :], ALU.mult)
            dve.wait_ge(s["kk_step"], 1)
            wn = 0
            for i in range(CH - 1):
                m = CH - 1 - i
                t = pb_d[:, 0:512 * m].rearrange("p (j c d) -> p j c d", c=NCH, d=HD)
                if wn:
                    dve.wait_ge(s["w_step"], wn)
                dve.tensor_tensor(t, LL[:, i + 1:CH, i, :].unsqueeze(3).broadcast_to([P, m, NCH, HD]),
                                  chunked(W, i, 1).broadcast_to([P, m, NCH, HD]), ALU.mult).then_inc(s["w_step"], 1)
                dve.wait_ge(s["w_step"], wn + 1)
                dve.tensor_tensor(chunked(W, i + 1, m), chunked(W, i + 1, m), t, ALU.add).then_inc(s["w_step"], 1)
                wn += 2
            fo = G[:, :, 0, :].rearrange("p j c -> p c j")
            ke = G[:, CH - 1, 1:CH + 1, :].rearrange("p j c -> p c j")
            for d in range(HD):
                qd = Q[:, d, :].rearrange("p (c j) -> p c j", j=CH)
                dve.tensor_tensor(qd, qd, fo, ALU.mult).then_inc(s["w_step"], 1)
                kd = K[:, d, :].rearrange("p (c j) -> p c j", j=CH)
                dve.tensor_tensor(kd, kd, ke, ALU.mult).then_inc(s["w_step"], 1)
            dve.wait_ge(s["w_step"], wn + 2 * HD)
            dve.wait_ge(s["u_pool"], 2 * (CH - 1))

            def reduce_out(r, a):
                c = 4 * r + a
                fo = pb_p[:, 2048 * (a % 2) + 1024:2048 * (a % 2) + 1536].rearrange("p (j v k) -> p j v k", v=HD, k=8)
                dve.tensor_reduce(O[:, :, bass.ds(CH * c, CH)].rearrange("p v j -> p j v"), fo, AX.X, ALU.add)\
                    .then_inc(s["o_red"], 1)

            def chain(r, a, first=False):
                c = 4 * r + a
                cs = bass.ds(CH * c, CH)
                n = 6 * c
                pu = pb_d[:, 0:512].rearrange("p (j v k) -> p j v k", v=HD, k=HD)
                if not first:
                    dve.wait_ge(s["chain"], n + 1)
                dve.tensor_tensor(pu, W[:, :, cs].rearrange("p k j -> p j k").unsqueeze(2)
                                  .broadcast_to([P, CH, HD, HD]),
                                  S[:, a, :, :].unsqueeze(1).broadcast_to([P, CH, HD, HD]), ALU.mult)\
                    .then_inc(s["chain"], 1)
                dve.wait_ge(s["chain"], n + 2)
                dve.tensor_reduce(uw[:, :, :], pu, AX.X, ALU.add).then_inc(s["chain"], 1)
                dve.wait_ge(s["chain"], n + 3)
                u = V[:, :, cs]
                dve.tensor_tensor(u, u, uw[:, :, :].rearrange("p j v -> p v j"), ALU.add).then_inc(s["chain"], 1)
                dve.wait_ge(s["chain"], n + 4)
                if not first:
                    dve.wait_ge(s["po_done"], c)
                ps = pb_d[:, 512:1024].rearrange("p (v k j) -> p v k j", k=HD, j=CH)
                dve.tensor_tensor(ps, K[:, :, cs].unsqueeze(1).broadcast_to([P, HD, HD, CH]),
                                  u.unsqueeze(2).broadcast_to([P, HD, HD, CH]), ALU.mult).then_inc(s["chain"], 1)
                if not first:
                    reduce_out(r if a else r - 1, a - 1 if a else 3)
                dve.wait_ge(s["chain"], n + 5)
                dve.tensor_reduce(sr[:, :, :], ps, AX.X, ALU.add).then_inc(s["chain"], 1)
                dve.wait_ge(s["chain"], n + 6)
                if not (isinstance(r, int) and 4 * r + a < 3):
                    dve.wait_ge(s["po_mul"], 2 * c - 5)
                b = (a + 1) % 4
                dve.scalar_tensor_tensor(S[:, b, :, :].rearrange("p v k -> p (v k)"),
                                         S[:, a, :, :].rearrange("p v k -> p (v k)"),
                                         G[:, CH - 1, 0, bass.ds(c, 1)], sr[:, :, :].rearrange("p v k -> p (v k)"),
                                         ALU.mult, ALU.add).then_inc(s["chain"], 1)

            dve.sem_inc(s["chain"], 1)
            chain(0, 0, first=True)
            for a in range(1, 4):
                chain(0, a)
            with dve.Fori(1, NCH // 4) as r:
                for a in range(4):
                    chain(r, a)
            dve.wait_ge(s["po_done"], NCH)
            reduce_out(NCH // 4 - 1, 3)

            dve.wait_ge(s["cw_in"], 144)
            dve.tensor_scalar(wo[:, :], wo[:, :], nw[:, 0:1], None, ALU.mult).then_inc(s["wo_step"], 1)
            dve.wait_ge(s["cs_ps"], 1)
            dve.tensor_copy(wcol[:, :], c0[:, 0:C]).then_inc(s["wo_step"], 1)
            dve.wait_ge(s["gate_sig"], 1)
            dve.wait_ge(s["wo_step"], 2)

            def gated(b):
                dve.wait_ge(o_in[b % 3], 16 * (b // 3 + 1))
                dve.tensor_tensor(og[:, b % 3, :], og[:, b % 3, :], gate[:, b, :], ALU.mult)\
                    .then_inc(s["og_done"], 1)

            gated(0)
            gated(1)
            for b in range(B):
                tp, yp = ((c1, c2), (c3, c4))[b % 2]
                n = 7 * b
                dve.wait_ge(s["oy_ps"], b + 1)
                for i in range(TT):
                    ins = dve.bn_stats(ost[:, i, :], tp[:, P * i:P * i + P])
                ins.then_inc(s["stat_done"], 1)
                dve.wait_ge(s["stat_done"], 2 * NT + 2 * b + 1)
                for i in range(TT):
                    ins = dve.bn_aggr(omv[:, i, :], ost[:, i, :])
                ins.then_inc(s["stat_done"], 1)
                dve.wait_ge(s["stat_done"], 2 * NT + 2 * b + 2)
                dve.tensor_scalar(ors[:, 0, :], omv[:, :, 1], EPS_LN, None, ALU.add).then_inc(s["ost_step"], 1)
                dve.tensor_scalar(ors[:, 3, :], omv[:, :, 0], -1.0, None, ALU.mult).then_inc(s["ost_step"], 1)
                if b + 2 < B:
                    gated(b + 2)
                dve.wait_ge(s["ost_step"], n + 2)
                for i in range(TT):
                    y = pb_d[:, P * i:P * i + P]
                    ins = dve.scalar_tensor_tensor(y, wcol[:, :], ors[:, 3, i:i + 1], yp[:, P * i:P * i + P],
                                                   ALU.mult, ALU.add)
                ins.then_inc(s["ost_step"], 1)
                dve.wait_ge(s["o_sqrt"], b + 1)
                dve.reciprocal(ors[:, 2, :], ors[:, 1, :]).then_inc(s["ost_step"], 1)
                dve.wait_ge(s["ost_step"], n + 4)
                for i in range(TT):
                    j = TT * b + i
                    ins = dve.scalar_tensor_tensor(x[:, j, :], pb_d[:, P * i:P * i + P], ors[:, 2, i:i + 1],
                                                   x[:, j, :], ALU.mult, ALU.add)
                ins.then_inc(s["ost_done"], 1)
                for _ in range(3):
                    dve.sem_inc(s["ost_step"], 1)

        @block.tensor
        def _(pe):
            pe.wait_ge(s["c_consts"], 1)
            pe.wait_ge(s["cw_in"], 144)
            for b in range(B):
                pe.wait_ge(s["cn_done"], TT * b + TT)
                pe.wait_ge(s["cT_sb"], b)
                for i in range(TT):
                    ins = pe.transpose(c0[:, P * i:P * i + P], cn[:, b % 2, i, :], ident[:, :])
                ins.then_inc(s["cT_ps"], 1)
                pe.wait_ge(s["cT_sb"], b + 1)
                for i in range(3):
                    pe.wait_ge(s["cq_sb"], 3 * (b - 1) + i + 1) if b else None
                    pe.matmul(cqkv[i][:, :], wqkv[:, i, :], cT[:, :], start=True, stop=True).then_inc(s["cq_ps"], 1)
                pe.wait_ge(s["cf_sb"], b)
                pe.matmul(c4[0:2 * H, :], wfg[:, :], cT[:, :], start=True, stop=True).then_inc(s["cf_ps"], 1)
                pe.wait_ge(s["cg1_sb"], b)
                pe.matmul(c5[0:HD, :], wg1[:, :], cT[:, :], start=True, stop=True).then_inc(s["cg1_ps"], 1)
                pe.wait_ge(s["cg1_sb"], b + 1)
                pe.wait_ge(s["cg2_sb"], b)
                pe.matmul(c6[:, :], wg2[:, :], red1[:, :], start=True, stop=True).then_inc(s["cg2_ps"], 1)
            pe.wait_ge(s["wo_step"], 1)
            pe.matmul(c0[:, 0:C], ones[:, :], wo[:, :], start=True, stop=True).then_inc(s["cs_ps"], 1)
            for b in range(B):
                tp, yp = ((c1, c2), (c3, c4))[b % 2]
                pe.wait_ge(s["og_done"], b + 1)
                if b >= 2:
                    pe.wait_ge(s["ost_done"], b - 1)
                for i in range(TT):
                    pe.transpose(tp[:, P * i:P * i + P], og[:, b % 3, P * i:P * i + P], ident[:, :])
                for i in range(TT):
                    ins = pe.matmul(yp[:, P * i:P * i + P], og[:, b % 3, P * i:P * i + P], wo[:, :],
                                    start=True, stop=True)
                ins.then_inc(s["oy_ps"], 1)


def build(nc, xin, W, Wq, Wk, Wv, Wgamma, Wf, Wg1, Wg2, Wo, norm_w, w_red, wg, w1, b1, w2, b2, out):
    with ExitStack() as ctx:
        def sb(name, shape, dt=F32):
            return ctx.enter_context(nc.sbuf_tensor(name, shape, dt))

        def sem(name):
            return ctx.enter_context(nc.semaphore(name))

        xs_dram = nc.dram_tensor("xs_dram", [NS * ST, C], F32, kind="Internal").ap()
        ys_dram = nc.dram_tensor("ys_dram", [NS * ST, C], F32, kind="Internal").ap()
        x = sb("x", [P, NT, C])
        s = {}
        for n in """f_consts fc_step ident_done stat_done rstd_step rstd_ready xnf_done
            rT_ps rT_sb red_ps red_sb lg_ps lg_step lg_exp lg_sum oh_done rank_ps pos_step pos_done texp_done
            zero_done scat_done x_ps x_sb h_ps h_sb y_ps y_sb o_ps o_sb gat_done add_done
            x_out fw_in wg_step wgT_ps wgT_sb""".split():
            s[n] = sem("f_" + n)
        xs_in, ws_in, ys_out = ([sem(f"f_{n}{k}") for k in range(2)] for n in ("xs_in", "ws_in", "ys_out"))
        s["xs_in"], s["ws_in"], s["ys_out"] = xs_in, ws_in, ys_out
        keep = {
            "ident": sb("ident", [P, P]),
            "before": sb("before", [P, P]),
            "ones": sb("ones", [P, P]),
            "zero": sb("zero", [P, 1024]),
            "pref": sb("pref", [P, E]),
            "restart_e": sb("restart_e", [P, E, NT]),
            "tile_at": sb("tile_at", [P, NS]),
            "k_at": sb("k_at", [P, NT * P // ST]),
            "wred_sb": sb("wred_sb", [P, GD]),
            "wgT_s": sb("wgT_s", [GD, E]),
            "b1T": sb("b1T", [P, E, NF]),
            "b2T": sb("b2T", [P, E]),
            "one8": sb("one8", [P, E]),
        }
        attention(nc, x, xin, W)
        experts(nc, x, xs_dram, ys_dram, s, keep, 0, w_red, wg, w1, b1, w2, b2, out)
        delta_rule(nc, x, Wq, Wk, Wv, Wgamma, Wf, Wg1, Wg2, Wo, norm_w)
        experts(nc, x, xs_dram, ys_dram, s, keep, 1, w_red, wg, w1, b1, w2, b2, out)


_INS = ["L0_attn_a_x", "L0_attn_a_W", "L0_attn_b_Wq", "L0_attn_b_Wk", "L0_attn_b_Wv", "L0_attn_b_Wgamma",
        "L0_attn_b_Wf", "L0_attn_b_Wg1", "L0_attn_b_Wg2", "L0_attn_b_Wo", "L0_attn_b_norm_w", "L0_ffn_w_red",
        "L0_ffn_wg", "L0_ffn_w1", "L0_ffn_b1", "L0_ffn_w2", "L0_ffn_b2"]


def kernel(**inputs):
    import numpy as _np
    import concourse.bacc as _bacc
    from concourse import mybir as _mybir
    from concourse.bass_utils import run_bass_kernel_spmd as _run

    nc = _bacc.Bacc("TRN2", target_bir_lowering=False, num_devices=1)
    arrays, args = {}, []
    for name in _INS:
        a = _np.ascontiguousarray(inputs[name])
        arrays[f"in_{name}_dram"] = a
        args.append(nc.dram_tensor(f"in_{name}_dram", a.shape, _mybir.dt.from_np(a.dtype), kind="ExternalInput").ap())
    out = nc.dram_tensor("out_0_dram", (B, T, C), F32, kind="ExternalOutput").ap()
    build(nc, *args, out)
    r = _run(nc, [arrays], core_ids=[0])
    return r.results[0]["out_0_dram"]
```

```python
from contextlib import ExitStack

import concourse.bass as bass
from concourse import mybir

F32 = mybir.dt.float32
BF16 = mybir.dt.bfloat16
I32 = mybir.dt.int32
ALU = mybir.AluOpType
ACT = mybir.ActivationFunctionType
AX = mybir.AxisListType
RMAX = bass.bass_isa.ReduceOp.max

P = 128
B, T, C = 8, 512, 128
H, HD = 16, 8
TT = T // P
NT = B * TT
EPS_LN = 1e-5

NP = H // 2
L = 64
NM = T // L
HU = NM + NM // 2
NU = 2 * HU
EPS_A = 1e-7
NPARTS = 8
Q_PART = [0, 0, 1, 1, 0, 2, 1, 2]
K_PART = [0, 1, 0, 1, 2, 0, 2, 1]
OFF_FIRST = [sum(NM - 1 - j for j in range(m)) for m in range(NM)]
N_OFF = NM * (NM - 1) // 2

E, F, GD = 8, 512, 16
NF = F // P
ST = 256
SLOTS = 4
NS = -(-((B * T + E * (ST - 1)) // ST) // SLOTS) * SLOTS
NR = NS // SLOTS
NC2 = ST // P
EPS_G = 1e-4

CH = 8
NCH = T // CH
EPS_K = 1e-12


def attention(nc, x, xin, W):
    with ExitStack() as ctx:
        def sb(name, shape, dt=F32):
            return ctx.enter_context(nc.sbuf_tensor("a_" + name, shape, dt))

        def psum(name, shape):
            return ctx.enter_context(nc.psum_tensor("a_" + name, shape, F32))

        def sem(name):
            return ctx.enter_context(nc.semaphore(name))

        scratch = nc.dram_tensor("parts_scratch", [2, 2, 3, P, T], BF16, kind="Internal").ap()

        wn = sb("wn", [P, 4, C])
        wT = sb("wT", [P, 3, C])
        wvg = sb("wvg", [P, 2, 72])
        wgT = sb("wgT", [P, H])
        sq = sb("sq", [P, C])
        wss = sb("wss", [P, 2])
        wmx = sb("wmx", [P, 2])
        guard = sb("guard", [P, 4])
        eps_a = sb("eps_a", [P, 1])
        ident = sb("ident", [P, P])
        ident_b = sb("ident_b", [P, P], BF16)
        upto = sb("upto", [P, P])
        after = sb("after", [P, P])
        same = sb("same", [P, P])
        tri = sb("tri", [P, L])
        never = sb("never", [P, L], BF16)
        restart = sb("restart", [P, NP, NM])
        zeros = sb("zeros", [P, 18])
        stats = sb("stats", [P, NT, 6])
        mv = sb("mv", [P, NT, 2])
        rstd = sb("rstd", [P, 4, NT])
        xn = sb("xn", [P, TT, C])
        xnT = sb("xnT", [P, T])
        parts = sb("parts", [P, 2, 3, T], BF16)
        rest = sb("rest", [P, 2, T])
        qf = sb("qf", [P, 2, NP, T], BF16)
        kc = sb("kc", [P, NP, T], BF16)
        kf = sb("kf", [P, 2, NP, NM, 2, L], BF16)
        vd = sb("vd", [P, 2, NM, NP, 18])
        vo = sb("vo", [P, N_OFF, NP, 18])
        gates = sb("gates", [P, P])
        g_low = sb("g_low", [P, P])
        g_abs = sb("g_abs", [P, P])
        logg = sb("logg", [P, P])
        g_cum = sb("g_cum", [P, P])
        b_tot = sb("b_tot", [P, NP, NM])
        b_cum = sb("b_cum", [P, NP, NM])
        tail = sb("tail", [P, NP, NM])
        reach = sb("reach", [P, NP, NM, NM])
        e_tok = sb("e_tok", [P, 2, TT * H])
        ramp = sb("ramp", [P, 2, NP, L])
        decay = sb("decay", [P, 2, NM, NP, L])
        mag = sb("mag", [P, 3, 2 * T])
        pw = sb("pw", [P, 4, 2 * T])
        off_sb = sb("off_sb", [P, 2, T])
        dia_sb = sb("dia_sb", [P, 2, T])
        acc = sb("acc", [P, TT * 4, 2, 9])
        rnorm = sb("rnorm", [P, TT * 4, 2])
        y = sb("y", [P, TT * 4, 2, HD])

        pS = psum("pS", [P, 4, T])
        pOff = psum("pOff", [P, T])
        pDia = psum("pDia", [P, T])
        M0 = psum("M0", [P, T])
        M1 = psum("M1", [P, T])

        names = """x_in w_in consts guard_step w_scaled w_T w_sb stat_done rstd_step rstd_ready
        xn_done xnT_ps xnT_sb qk_ps split_hi split_rest split_mid split_lo parts_out feat_q feat_k
        v_ps v_sb gate_sb tok_ps g_step logg_done cum_ps cum_sb reach_step reach_exp vo_done ramp_done decay_ps decay_sb
        s_ps mag_done sq_done pdg_done pv_done off_done dia_done fin_ps fin_step
        c_step vd_zero kx_done kf_zero w_misc""".split()
        s = {n: sem("a_" + n) for n in names}
        block = ctx.enter_context(nc.Block())

        def vo_at(j, i):
            return OFF_FIRST[j] + i - j - 1

        def width(m):
            return T - L * m

        def unit(n):
            hf, r = divmod(n, HU)
            if r < NM:
                return hf, r // 2, (2 * (r % 2), 2 * (r % 2) + 1)
            return hf, r - NM // 2, (0, 1, 2, 3)

        def last_unit(m):
            return 2 * m + 1 if m < NM // 2 else m + NM // 2

        def pairs_of(hf, qs):
            return slice(2 * qs[0] + hf, 2 * qs[-1] + hf + 1, 2)

        AHEAD_S, AHEAD_MAG, AHEAD_PW = 2, 3, 4
        TURN, QK, VALUES, SUMS, DECAY, EXPAND = 3, 5, 9, 15, 16, 21
        FIN = (1, 12)

        @block.sync
        def _(sp):
            for k in range(B):
                sp.dma_start(x[:, TT * k:TT * (k + 1), :],
                             xin[k].rearrange("(i p) c -> p i c", p=P)).then_inc(s["x_in"], 16)

            def features(bb, k):
                sp.wait_ge(s["split_hi"], 2 * bb + 2)
                sp.wait_ge(s["split_mid"], 2 * bb + 2)
                sp.wait_ge(s["split_lo"], 2 * bb + 2)
                for t in range(2):
                    for c in range(3):
                        sp.dma_start(scratch[k, t, c], parts[:, t, c, :]).then_inc(s["parts_out"], 16)
                sp.wait_ge(s["parts_out"], 96 * bb + 96)
                sp.wait_ge(s["kx_done"], 2 * bb)
                for par in range(2):
                    for c in range(NPARTS):
                        row = 64 * par + HD * c
                        src = [scratch[k, t, part].rearrange("(p x d) t -> x d p t", x=2, d=HD)[par]
                               for t, part in ((0, Q_PART[c]), (1, K_PART[c]))]
                        sp.dma_start(qf[row:row + HD, k, :, :], src[0]).then_inc(s["feat_q"], 16)
                        sp.dma_start(kc[row:row + HD, :, :], src[1]).then_inc(s["feat_k"], 16)

            features(0, 0)

            def batch(b, k, last=False):
                if not last:
                    sp.wait_ge(s["s_ps"], NU * b)
                    features(b + 1, 1 - k)

            batch(0, 0)
            with sp.Fori(1, B - 2, 2) as b:
                batch(b, 1)
                batch(b + 1, 0)

        @block.gpsimd
        def _(pool):
            st = 0

            def step(ins):
                nonlocal st
                st += 1
                ins.then_inc(s["c_step"], 1)
                pool.wait_ge(s["c_step"], st)

            for t, val in ((ident, 0.0), (ident_b, 0.0), (upto, 0.0), (after, 0.0), (same, 0.0), (tri, 1.0),
                           (never, 0.0), (zeros, 0.0)):
                step(pool.memset(t[:, :], val))
            step(pool.memset(restart[:, :, :], 1.0))
            pool.wait_ge(s["c_step"], st)
            step(pool.memset(restart[:, :, 0:1], 0.0))
            for t in (ident, ident_b):
                step(pool.affine_select(out=t[:, :], in_=t[:, :], compare_op=ALU.not_equal, fill=1.0,
                                        base=0, pattern=[[-1, P]], channel_multiplier=1))
            for h in range(2):
                for t in (upto, after, same):
                    step(pool.memset(t[L * h:L * h + L, L * h:L * h + L], 1.0))
            pool.wait_ge(s["c_step"], st)
            for h in range(2):
                lo, hi = L * h, L * h + L
                step(pool.affine_select(out=upto[lo:hi, lo:hi], in_=upto[lo:hi, lo:hi], compare_op=ALU.is_ge,
                                        fill=0.0, base=0, pattern=[[1, L]], channel_multiplier=-1))
                step(pool.affine_select(out=after[lo:hi, lo:hi], in_=after[lo:hi, lo:hi], compare_op=ALU.is_ge,
                                        fill=0.0, base=-1, pattern=[[-1, L]], channel_multiplier=1))
                step(pool.affine_select(out=tri[lo:hi, :], in_=tri[lo:hi, :], compare_op=ALU.is_ge,
                                        fill=0.0, base=0, pattern=[[1, L]], channel_multiplier=-1))
                step(pool.affine_select(out=never[lo:hi, :], in_=never[lo:hi, :], compare_op=ALU.is_ge,
                                        fill=-1e30, base=0, pattern=[[1, L]], channel_multiplier=-1))
            pool.wait_ge(s["c_step"], st)
            pool.memset(guard[:, 3:4], 0.0).then_inc(s["consts"], 1)
            pool.wait_ge(s["guard_step"], 2)
            pool.partition_all_reduce(wmx[:, :], wss[:, :], P, RMAX).then_inc(s["guard_step"], 1)
            pool.wait_ge(s["guard_step"], 3)
            for k in range(2):
                pool.memset(kf[:, k, :, :, :, :].rearrange("p a m x t -> p (a m x t)").bitcast(F32), 0.0)\
                    .then_inc(s["kf_zero"], 1)

            def ramps(bb, m, first=False):
                pool.wait_ge(s["logg_done"], bb + 1)
                if not (first and m < 2):
                    pool.wait_ge(s["decay_ps"], NM * bb + m - 1)
                pool.tensor_tensor(ramp[:, m % 2, :, :],
                                   tri[:, :].unsqueeze(1).broadcast_to([P, NP, L]),
                                   logg[:, 0:64].rearrange("p (a m) -> p a m", m=NM)[:, :, m:m + 1]
                                   .broadcast_to([P, NP, L]), ALU.mult).then_inc(s["ramp_done"], 1)

            def values_off(bb, k, j, first=False):
                if first:
                    pool.wait_ge(s["vd_zero"], 2)
                if j == 0:
                    pool.wait_ge(s["reach_exp"], bb + 1)
                    pool.wait_ge(s["v_sb"], 4 * bb + 4)
                if not first:
                    pool.wait_ge(s["pv_done"], NU * (bb - 1) + HU + last_unit(j) + 1 + AHEAD_PW)
                n = NM - 1 - j
                pool.tensor_tensor(
                    vo[:, vo_at(j, j + 1):vo_at(j, j + 1) + n, :, :],
                    vd[:, k, j, :, :].unsqueeze(1).broadcast_to([P, n, NP, 18]),
                    reach[:, :, j, j:NM - 1].rearrange("p a i -> p i a").unsqueeze(3)
                    .broadcast_to([P, n, NP, 18]), ALU.mult).then_inc(s["vo_done"], 1)

            def diagonal(b, n, k):
                hf, m, qs = unit(n)
                sl = n % 4
                pool.wait_ge(s["sq_done"], NU * b + n + 1 + AHEAD_MAG)
                pool.wait_ge(s["decay_sb"], NM * b + m + 1)
                own = pw[:, sl, 0:len(qs) * width(m)].rearrange("p (l t) -> p l t", l=len(qs))[:, :, 0:L]
                pool.tensor_tensor(own, own, decay[:, k, m, pairs_of(hf, qs), :], ALU.mult)\
                    .then_inc(s["pdg_done"], 1)

            for m in range(NM):
                ramps(0, m, first=True)
            for j in range(NM - 1):
                values_off(0, 0, j, first=True)

            def batch(b, k, last=False):
                for n in range(NU):
                    diagonal(b, n, k)
                    if last:
                        continue
                    if DECAY - 1 <= n < DECAY - 1 + NM:
                        ramps(b + 1, n - DECAY + 1)
                    for j in range(NM - 1):
                        if n == max(HU + last_unit(j) + 1, SUMS + 3 + min(j, 4)):
                            values_off(b + 1, 1 - k, j)
            batch(0, 0)
            with pool.Fori(1, B - 2, 2) as b:
                batch(b, 1)
                batch(b + 1, 0)
            batch(B - 1, 1, last=True)

        @block.scalar
        def _(act):
            act.dma_start(wn[:, 0:3, :], W[0:3 * C, :].rearrange("(j p) c -> p j c", p=P)).then_inc(s["w_in"], 16)
            act.dma_start(wn[0:H, 3, :], W[3 * C:3 * C + H, :]).then_inc(s["w_in"], 16)
            act.wait_ge(s["w_in"], 32)
            act.activation(sq[:, :], wn[:, 0, :], ACT.Square, accum_out=wss[:, 0:1]).then_inc(s["guard_step"], 1)
            act.activation(dia_sb[:, 0, 0:C], wn[:, 1, :], ACT.Square, accum_out=wss[:, 1:2]).then_inc(s["guard_step"], 1)
            act.wait_ge(s["guard_step"], 7)
            act.activation(guard[:, 1:2], guard[:, 0:1], ACT.Sqrt).then_inc(s["guard_step"], 1)
            act.wait_ge(s["rstd_step"], 1)
            act.activation(rstd[:, 2, :], rstd[:, 1, :], ACT.Sqrt).then_inc(s["rstd_step"], 1)

            def turned(bb):
                act.wait_ge(s["xnT_ps"], bb + 1)
                act.wait_ge(s["v_ps"], bb)
                act.activation(xnT[:, :], M0[:, :], ACT.Copy).then_inc(s["xnT_sb"], 1)

            def split_high(bb, t):
                act.wait_ge(s["qk_ps"], 2 * bb + t + 1)
                act.wait_ge(s["parts_out"], 96 * bb)
                act.activation(parts[:, t, 0, :], (M0, M1)[t][:, :], ACT.Copy).then_inc(s["split_hi"], 1)

            def split_mid(bb, t):
                act.wait_ge(s["split_rest"], 2 * bb + t + 1)
                act.activation(parts[:, t, 1, :], rest[:, t, :], ACT.Copy).then_inc(s["split_mid"], 1)

            def values(bb, k, first=False):
                act.wait_ge(s["gate_sb"], 4 * bb + 3)
                if first:
                    act.wait_ge(s["vd_zero"], 2)
                else:
                    act.wait_ge(s["pv_done"], NU * (bb - 1) + AHEAD_PW)
                    act.wait_ge(s["vo_done"], 7 * (bb - 1))
                for q, M in enumerate((M0, M1)):
                    for par in range(2):
                        lo, hi = L * par, L * par + L
                        act.activation(
                            vd[lo:hi, k, 4 * q:4 * q + 4, :, 9 * par:9 * par + HD],
                            M[lo:hi, 0:288].rearrange("p (m c) -> p m c", c=72)[:, :, 0:64]
                            .rearrange("p m (a d) -> p m a d", d=HD), ACT.Copy).then_inc(s["v_sb"], 1)

            def gate_logs(bb):
                act.wait_ge(s["g_step"], 3 * bb + 1)
                act.activation(g_abs[:, :], g_abs[:, :], ACT.Exp).then_inc(s["g_step"], 1)
                act.wait_ge(s["g_step"], 3 * bb + 2)
                act.activation(g_abs[:, :], g_abs[:, :], ACT.Ln, bias=1.0).then_inc(s["g_step"], 1)

            def token_decay(bb, k):
                act.wait_ge(s["cum_sb"], 6 * bb + 2)
                if not isinstance(bb, int) or bb >= 2:
                    act.wait_ge(s["fin_step"], 10 * bb - 14)
                act.activation(e_tok[:, k, :], M0[:, 64:128], ACT.Exp).then_inc(s["tok_ps"], 1)

            def reaches(bb):
                act.wait_ge(s["reach_step"], bb + 1)
                act.activation(reach[:, :, :, :].rearrange("p a j i -> p (a j i)"),
                               reach[:, :, :, :].rearrange("p a j i -> p (a j i)"), ACT.Exp)\
                    .then_inc(s["reach_exp"], 1)

            def decays(bb, k, m, first=False):
                act.wait_ge(s["decay_ps"], NM * bb + m + 1)
                if not first and m == 0:
                    act.wait_ge(s["pdg_done"], NU * (bb - 1))
                act.activation(decay[:, k, m, :, :].rearrange("p a t -> p (a t)"), (M1, M0)[m % 2][:, :],
                               ACT.Exp).then_inc(s["decay_sb"], 1)

            def square(b, n):
                hf, m, qs = unit(n)
                N = len(qs) * width(m)
                act.wait_ge(s["mag_done"], NU * b + n + 1 + AHEAD_S)
                act.wait_ge(s["pv_done"], NU * b + n + 1)
                act.activation(pw[:, n % 4, 0:N], mag[:, n % 3, 0:N], ACT.Square, bias=eps_a[:, 0:1])\
                    .then_inc(s["sq_done"], 1)

            def off_copy(b, hf):
                act.wait_ge(s["pv_done"], NU * b + HU * (hf + 1) + AHEAD_PW)
                if not (isinstance(b, int) and b == 0):
                    act.wait_ge(s["fin_ps"], 2 * b - 1 + hf)
                act.activation(off_sb[:, hf, :], pOff[:, :], ACT.Copy).then_inc(s["off_done"], 1)

            def batch(b, k, first=False, last=False):
                for n in range(NU):
                    square(b, n)
                    if n == 1 and not first:
                        off_copy(b - 1, 1)
                    if n == HU + 1:
                        off_copy(b, 0)
                    if last:
                        continue
                    if n == TURN + 1:
                        turned(b + 1)
                    if n == QK + 1:
                        split_high(b + 1, 0)
                        split_high(b + 1, 1)
                    if n == QK + 3:
                        split_mid(b + 1, 0)
                        split_mid(b + 1, 1)
                    if n == VALUES + 2:
                        values(b + 1, 1 - k)
                    if n == VALUES + 3:
                        gate_logs(b + 1)
                    if n == SUMS + 1:
                        token_decay(b + 1, 1 - k)
                    if n == SUMS + 3:
                        reaches(b + 1)
                    if DECAY <= n < DECAY + NM:
                        decays(b + 1, 1 - k, n - DECAY)

            act.sem_inc(s["sq_done"], AHEAD_MAG)
            turned(0)
            split_high(0, 0)
            split_high(0, 1)
            split_mid(0, 0)
            split_mid(0, 1)
            values(0, 0, first=True)
            gate_logs(0)
            token_decay(0, 0)
            reaches(0)
            for m in range(NM):
                decays(0, 0, m, first=True)
            batch(0, 0, first=True)
            with act.Fori(1, B - 2, 2) as b:
                batch(b, 1)
                batch(b + 1, 0)
            batch(B - 1, 1, last=True)
            off_copy(B - 1, 1)

        @block.vector
        def _(dve):
            dve.sem_inc(s["mag_done"], AHEAD_S)
            dve.memset(vd[:, :, :, :, :].rearrange("p k m a c -> p (k m a c)"), 0.0).then_inc(s["w_misc"], 1)
            dve.memset(pOff[:, :], 0.0).then_inc(s["w_misc"], 1)
            dve.memset(pDia[:, :], 0.0).then_inc(s["w_misc"], 1)
            dve.wait_ge(s["w_misc"], 3)
            for par in range(2):
                lo, hi = L * par, L * par + L
                dve.memset(vd[lo:hi, :, :, :, 9 * par + HD:9 * par + HD + 1]
                           .rearrange("p k m a c -> p (k m a) c"), 1.0).then_inc(s["vd_zero"], 1)
            dve.wait_ge(s["guard_step"], 3)
            dve.tensor_scalar(wss[:, :], wmx[:, :], 1e-30, None, ALU.max).then_inc(s["guard_step"], 1)
            dve.wait_ge(s["guard_step"], 4)
            dve.reciprocal(wmx[:, :], wss[:, :]).then_inc(s["guard_step"], 1)
            dve.wait_ge(s["guard_step"], 5)
            dve.tensor_tensor(guard[:, 2:3], wmx[:, 0:1], wmx[:, 1:2], ALU.mult).then_inc(s["guard_step"], 1)
            dve.wait_ge(s["guard_step"], 6)
            dve.tensor_scalar(guard[:, 0:1], guard[:, 2:3], 1e30 / (HD * HD * C * C), 1.0, ALU.mult, ALU.min)\
                .then_inc(s["guard_step"], 1)
            dve.wait_ge(s["guard_step"], 8)
            dve.tensor_scalar(eps_a[:, :], guard[:, 1:2], EPS_A, None, ALU.mult).then_inc(s["w_scaled"], 1)
            dve.tensor_scalar(wn[:, 0, :], wn[:, 0, :], guard[:, 1:2], None, ALU.mult).then_inc(s["w_scaled"], 1)
            dve.wait_ge(s["w_T"], 1)
            dve.tensor_copy(wT[:, :, :].rearrange("p j o -> p (j o)"), M0[:, 0:384]).then_inc(s["w_sb"], 1)
            dve.tensor_copy(wgT[:, :], M0[:, 384:400]).then_inc(s["w_sb"], 1)
            for par in range(2):
                dve.tensor_copy(wvg[:, par, 0:64].rearrange("p (a d) -> p a d", d=HD),
                                M0[:, 256:384].rearrange("p (a x d) -> p x a d", x=2, d=HD)[:, par])\
                    .then_inc(s["w_sb"], 1)
                dve.tensor_copy(wvg[:, par, 64:72],
                                M0[:, 384:400].rearrange("p (a x) -> p x a", x=2)[:, par]).then_inc(s["w_sb"], 1)
            for k in range(B):
                dve.wait_ge(s["x_in"], 16 * B)
                for i in range(TT):
                    dve.bn_stats(stats[:, TT * k + i, :], x[:, TT * k + i, :]).then_inc(s["stat_done"], 1)
            for k in range(B):
                for i in range(TT):
                    dve.wait_ge(s["stat_done"], TT * k + i + 1)
                    dve.bn_aggr(mv[:, TT * k + i, :], stats[:, TT * k + i, :]).then_inc(s["stat_done"], 1)
            dve.wait_ge(s["stat_done"], 2 * NT)
            dve.tensor_scalar(rstd[:, 1, :], mv[:, :, 1], EPS_LN, None, ALU.add).then_inc(s["rstd_step"], 1)
            dve.wait_ge(s["rstd_step"], 2)
            dve.reciprocal(rstd[:, 3, :], rstd[:, 2, :]).then_inc(s["rstd_step"], 1)
            dve.wait_ge(s["rstd_step"], 3)
            dve.tensor_tensor(rstd[:, 2, :], rstd[:, 3, :], rstd[:, 3, :], ALU.mult).then_inc(s["rstd_step"], 1)
            dve.wait_ge(s["rstd_step"], 4)
            dve.tensor_tensor(rstd[:, 2, :], rstd[:, 2, :], rstd[:, 1, :], ALU.mult).then_inc(s["rstd_step"], 1)
            dve.wait_ge(s["rstd_step"], 5)
            dve.tensor_scalar(rstd[:, 2, :], rstd[:, 2, :], -0.5, 1.5, ALU.mult, ALU.add)\
                .then_inc(s["rstd_step"], 1)
            dve.wait_ge(s["rstd_step"], 6)
            dve.tensor_tensor(rstd[:, 0, :], rstd[:, 2, :], rstd[:, 3, :], ALU.mult).then_inc(s["rstd_ready"], 1)

            def normalize(bb, first=False):
                dve.wait_ge(s["rstd_ready"], 1)
                if not first:
                    dve.wait_ge(s["xnT_ps"], bb)
                for i in range(TT):
                    j = TT * bb + i
                    dve.tensor_scalar(xn[:, i, :], x[:, bass.ds(j, 1), :].rearrange("p a c -> p (a c)"),
                                       mv[:, bass.ds(j, 1), 0:1].rearrange("p a c -> p (a c)"),
                                       rstd[:, 0, bass.ds(j, 1)], ALU.subtract, ALU.mult).then_inc(s["xn_done"], 1)

            def split_rest(bb, t, first=False):
                dve.wait_ge(s["split_hi"], 2 * bb + t + 1)
                if not first:
                    dve.wait_ge(s["split_mid"], 2 * (bb - 1) + t + 1)
                dve.tensor_tensor(rest[:, t, :], (M0, M1)[t][:, :], parts[:, t, 0, :], ALU.subtract)\
                    .then_inc(s["split_rest"], 1)

            def split_low(bb, t):
                dve.wait_ge(s["split_mid"], 2 * bb + t + 1)
                dve.wait_ge(s["parts_out"], 96 * bb)
                dve.tensor_tensor(parts[:, t, 2, :], rest[:, t, :], parts[:, t, 1, :], ALU.subtract)\
                    .then_inc(s["split_lo"], 1)

            def gate_prep(bb):
                dve.wait_ge(s["v_ps"], bb + 1)
                for q, M in enumerate((M0, M1)):
                    dve.tensor_copy(gates[:, 0:64].rearrange("p (a m) -> p m a", m=NM)[:, 4 * q:4 * q + 4, :],
                                    M[:, 0:288].rearrange("p (m c) -> p m c", c=72)[:, :, 64:72])\
                        .then_inc(s["gate_sb"], 1)
                dve.tensor_copy(gates[:, 64:128], M0[:, 288:352]).then_inc(s["gate_sb"], 1)
                dve.wait_ge(s["gate_sb"], 4 * bb + 3)
                dve.tensor_scalar(g_low[:, :], gates[:, :], 0.0, None, ALU.min).then_inc(s["gate_sb"], 1)
                dve.wait_ge(s["gate_sb"], 4 * bb + 4)
                dve.scalar_tensor_tensor(g_abs[:, :], g_low[:, :], 2.0, gates[:, :], ALU.mult, ALU.subtract)\
                    .then_inc(s["g_step"], 1)

            def gate_log(bb):
                dve.wait_ge(s["g_step"], 3 * bb + 3)
                dve.wait_ge(s["ramp_done"], NM * bb)
                dve.tensor_tensor(logg[:, :], g_low[:, :], g_abs[:, :], ALU.subtract).then_inc(s["logg_done"], 1)

            def sums(bb):
                dve.wait_ge(s["cum_ps"], bb + 1)
                dve.tensor_copy(b_tot[:, :, :].rearrange("p a m -> p (a m)"), M0[:, 128:192])\
                    .then_inc(s["cum_sb"], 1)
                dve.wait_ge(s["cum_sb"], 6 * bb + 1)
                dve.tensor_tensor(tail[:, :, :].rearrange("p a m -> p (a m)"),
                                  b_tot[:, :, :].rearrange("p a m -> p (a m)"), M0[:, 0:64], ALU.subtract)\
                    .then_inc(s["cum_sb"], 1)
                dve.tensor_tensor_scan(b_cum[:, :, :].rearrange("p a m -> p (a m)"),
                                       restart[:, :, :].rearrange("p a m -> p (a m)"),
                                       b_tot[:, :, :].rearrange("p a m -> p (a m)"), 0.0, ALU.mult, ALU.add)\
                    .then_inc(s["cum_sb"], 1)

            def reach_sums(bb):
                dve.wait_ge(s["cum_sb"], 6 * bb + 3)
                dve.tensor_tensor(tail[:, :, :], tail[:, :, :], b_cum[:, :, :], ALU.subtract)\
                    .then_inc(s["cum_sb"], 1)
                dve.wait_ge(s["cum_sb"], 6 * bb + 4)
                dve.wait_ge(s["vo_done"], 7 * bb)
                dve.tensor_tensor(reach[:, :, :, :], b_cum[:, :, :].unsqueeze(2).broadcast_to([P, NP, NM, NM]),
                                  tail[:, :, :].unsqueeze(3).broadcast_to([P, NP, NM, NM]), ALU.add)\
                    .then_inc(s["cum_sb"], 1)

            def reach_bound(bb):
                dve.wait_ge(s["cum_sb"], 6 * bb + 5)
                dve.tensor_scalar(reach[:, :, :, :].rearrange("p a j i -> p (a j i)"),
                                  reach[:, :, :, :].rearrange("p a j i -> p (a j i)"), 0.0, None, ALU.min)\
                    .then_inc(s["cum_sb"], 1)
                dve.wait_ge(s["cum_sb"], 6 * bb + 6)
                dve.sem_inc(s["reach_step"], 1)

            def expand(bb, k, first=False):
                dve.wait_ge(s["feat_k"], 256 * bb + 256)
                if first:
                    dve.wait_ge(s["kf_zero"], 2)
                else:
                    dve.wait_ge(s["s_ps"], NU * (bb - 1))
                for par in range(2):
                    lo, hi = L * par, L * par + L
                    dve.tensor_copy(kf[lo:hi, k, :, :, par, :].rearrange("p a m t -> p (a m) t"),
                                    kc[lo:hi, :, :].rearrange("p a (m t) -> p (a m) t", t=L))\
                        .then_inc(s["kx_done"], 1)

            def magnitude(b, n):
                hf, m, qs = unit(n)
                N = len(qs) // 2 * width(m)
                dve.wait_ge(s["s_ps"], NU * b + n + 1)
                dve.wait_ge(s["sq_done"], NU * b + n + 1)
                dve.tensor_scalar(mag[:, n % 3, 0:2 * N].bitcast(I32).rearrange("p (l t) -> p l t", l=2),
                                  pS[:, 2 * (n % 2):2 * (n % 2) + 2, 0:N].bitcast(I32),
                                  0x7fffffff, None, ALU.bitwise_and).then_inc(s["mag_done"], 1)

            def dia_copy(b, hf):
                dve.wait_ge(s["pv_done"], NU * b + HU * (hf + 1) + AHEAD_PW)
                if not (isinstance(b, int) and b == 0):
                    dve.wait_ge(s["fin_ps"], 2 * b - 1 + hf)
                dve.tensor_copy(dia_sb[:, hf, :], pDia[:, :]).then_inc(s["dia_done"], 1)

            def finish(b, k, hf, part):
                step = 5 * (2 * b + hf)
                if part or hf or not isinstance(b, int) or b:
                    dve.wait_ge(s["fin_step"], step + part)
                if part == 0:
                    dve.wait_ge(s["fin_ps"], 2 * b + hf + 1)
                    dve.wait_ge(s["tok_ps"], b + 1)
                if part < 2:
                    view = (M0, M1)[part][:, :].rearrange("p (a c) -> p a c", c=32)[:, :, 0:18]\
                        .rearrange("p a (x d) -> p a x d", x=2)
                if part == 0:
                    et = e_tok[:, k, :].rearrange("p (a x) -> p a x", x=4)[:, :, 2 * hf:2 * hf + 2].unsqueeze(3)\
                        .broadcast_to([P, 16, 2, 9])
                    dve.tensor_tensor(acc[:, :, :, :], view, et, ALU.mult).then_inc(s["fin_step"], 1)
                if part == 1:
                    dve.tensor_tensor(acc[:, :, :, :], view, acc[:, :, :, :], ALU.add).then_inc(s["fin_step"], 1)
                if part == 2:
                    dve.reciprocal(rnorm[:, :, :], acc[:, :, :, HD]).then_inc(s["fin_step"], 1)
                if part == 3:
                    dve.tensor_tensor(y[:, :, :, :], acc[:, :, :, 0:HD],
                                      rnorm[:, :, :].unsqueeze(3).broadcast_to([P, 16, 2, HD]), ALU.mult)\
                        .then_inc(s["fin_step"], 1)
                if part == 4:
                    xs = x[:, bass.ds(TT * b, TT), :].rearrange("p i (a c) -> p (i a) c", c=32)[:, :, 16 * hf:16 * hf + 16]
                    dve.tensor_tensor(xs, xs, y[:, :, :, :].rearrange("p a x d -> p a (x d)"), ALU.add)\
                        .then_inc(s["fin_step"], 1)

            normalize(0, first=True)
            split_rest(0, 0, first=True)
            split_rest(0, 1, first=True)
            split_low(0, 0)
            split_low(0, 1)
            gate_prep(0)
            gate_log(0)
            sums(0)
            reach_sums(0)
            reach_bound(0)
            expand(0, 0, first=True)
            magnitude(0, 0)
            magnitude(0, 1)

            def batch(b, k, first=False, last=False):
                for n in range(NU):
                    if n + 2 < NU:
                        magnitude(b, n + 2)
                    elif not last:
                        magnitude(b + 1, n + 2 - NU)
                    if n == 0 and not first:
                        dia_copy(b - 1, 1)
                    if n == HU:
                        dia_copy(b, 0)
                    for hf in range(2):
                        if FIN[hf] <= n < FIN[hf] + 5 and not first:
                            finish(b - 1, 1 - k, hf, n - FIN[hf])
                    if last:
                        continue
                    if n == TURN - 3:
                        normalize(b + 1)
                    if n == QK + 2:
                        split_rest(b + 1, 0)
                        split_rest(b + 1, 1)
                    if n == QK + 4:
                        split_low(b + 1, 0)
                        split_low(b + 1, 1)
                    if n == VALUES + 2:
                        gate_prep(b + 1)
                    if n == VALUES + 4:
                        gate_log(b + 1)
                    if n == SUMS:
                        sums(b + 1)
                    if n == SUMS + 1:
                        reach_sums(b + 1)
                    if n == SUMS + 2:
                        reach_bound(b + 1)
                    if n == EXPAND:
                        expand(b + 1, 1 - k)

            batch(0, 0, first=True)
            with dve.Fori(1, B - 2, 2) as b:
                batch(b, 1)
                batch(b + 1, 0)
            batch(B - 1, 1, last=True)
            dia_copy(B - 1, 1)
            for hf in range(2):
                for part in range(5):
                    finish(B - 1, 1, hf, part)
            dve.wait_ge(s["fin_step"], 10 * B)

        @block.tensor
        def _(pe):
            pe.sem_inc(s["pv_done"], AHEAD_PW)
            pe.wait_ge(s["consts"], 1)
            pe.wait_ge(s["w_scaled"], 2)
            for j in range(3):
                pe.transpose(M0[:, P * j:P * j + P], wn[:, j, :], ident[:, :])
            pe.transpose(M0[:, 384:400], wn[0:H, 3, :], ident[0:H, 0:H]).then_inc(s["w_T"], 1)
            pe.wait_ge(s["w_sb"], 6)

            def turn(bb, first=False):
                pe.wait_ge(s["xn_done"], TT * bb + TT)
                if not first:
                    pe.wait_ge(s["decay_sb"], NM * bb)
                if not isinstance(bb, int) or bb >= 2:
                    pe.wait_ge(s["fin_step"], 10 * bb - 18)
                for i in range(TT):
                    ins = pe.transpose(M0[:, P * i:P * i + P], xn[:, i, :], ident[:, :])
                ins.then_inc(s["xnT_ps"], 1)

            def project(bb):
                pe.wait_ge(s["xnT_sb"], bb + 1)
                for t, M in enumerate((M0, M1)):
                    pe.matmul(M[:, :], wT[:, t, :], xnT[:, :], start=True, stop=True).then_inc(s["qk_ps"], 1)

            def values(bb):
                pe.wait_ge(s["split_hi"], 2 * bb + 2)
                pe.wait_ge(s["split_rest"], 2 * bb + 2)
                for m in range(NM // 2):
                    value(m)

            def value(m):
                for par in range(2):
                    pe.matmul((M0, M1)[m // 4][L * par:L * par + L, 72 * (m % 4):72 * (m % 4) + 72],
                              xnT[:, L * m:L * m + L], wvg[:, par, :], start=True, stop=True)

            def values_late():
                for m in range(NM // 2, NM):
                    value(m)
                for i in range(TT):
                    ins = pe.matmul(M0[:, 288 + H * i:288 + H * i + H], xnT[:, P * i:P * i + P], wgT[:, :],
                                    start=True, stop=True)
                ins.then_inc(s["v_ps"], 1)

            def sums(bb):
                pe.wait_ge(s["logg_done"], bb + 1)
                pe.wait_ge(s["v_sb"], 4 * bb + 4)
                if not isinstance(bb, int) or bb >= 2:
                    pe.wait_ge(s["fin_step"], 10 * bb - 13)
                pe.matmul(M0[:, 0:128], upto[:, :], logg[:, :], start=True, stop=True)
                pe.matmul(M0[:, 128:192], same[:, :], logg[:, 0:64], start=True, stop=True)\
                    .then_inc(s["cum_ps"], 1)

            def decay_sums(bb, m):
                pe.wait_ge(s["ramp_done"], NM * bb + m + 1)
                if m >= 2:
                    pe.wait_ge(s["decay_sb"], NM * bb + m - 1)
                if m == 1:
                    pe.wait_ge(s["cum_sb"], 6 * bb + 2)
                    pe.wait_ge(s["tok_ps"], bb + 1)
                M = (M1, M0)[m % 2]
                pe.matmul(M[:, :], after[:, :], ramp[:, m % 2, :, :].rearrange("p a t -> p (a t)"),
                          start=True, stop=False)
                pe.matmul(M[:, :].rearrange("p (a t) -> p a t", t=L), ident_b[:, :],
                          never[:, :].unsqueeze(1).broadcast_to([P, NP, L]), start=False, stop=True)\
                    .then_inc(s["decay_ps"], 1)

            def scores(b, k, n):
                hf, m, qs = unit(n)
                if n == 0:
                    pe.wait_ge(s["feat_q"], 256 * b + 256)
                    pe.wait_ge(s["kx_done"], 2 * b + 2)
                pe.wait_ge(s["mag_done"], NU * b + n + 1)
                for l, Q in enumerate(qs):
                    p = 2 * Q + hf
                    half = len(qs) // 2
                    at = width(m) * (l % half)
                    ins = pe.matmul(pS[:, 2 * (n % 2) + l // half, at:at + width(m)], kf[:, k, p, m, :, :].rearrange("p x t -> p (x t)"),
                                    qf[:, k, p, L * m:T], start=True, stop=True)
                ins.then_inc(s["s_ps"], 1)

            def attend(b, k, n):
                hf, m, qs = unit(n)
                if n % HU == 0:
                    pe.wait_ge(s["off_done"], 2 * b + hf)
                    pe.wait_ge(s["dia_done"], 2 * b + hf)
                if n == 0:
                    pe.wait_ge(s["w_misc"], 3)
                pe.wait_ge(s["pdg_done"], NU * b + n + 1)
                if hf == 0 and qs[0] == 0 and m < NM - 1:
                    pe.wait_ge(s["vo_done"], 7 * b + m + 1)
                w = pw[:, n % 4, 0:len(qs) * width(m)].rearrange("p (l t) -> p l t", l=len(qs))
                for i in range(m, NM):
                    for l, Q in enumerate(qs):
                        p = 2 * Q + hf
                        lo, hi = 32 * Q, 32 * Q + 18
                        wi = w[:, l, L * (i - m):L * (i - m) + L]
                        if i == m:
                            if m == 0:
                                pe.matmul(pOff[lo:hi, 0:L], zeros[:, :], wi, start=True, stop=False,
                                          skip_group_check=True)
                            ins = pe.matmul(pDia[lo:hi, L * m:L * m + L], vd[:, k, m, p, :], wi,
                                            start=(m == 0), stop=(m == NM - 1), skip_group_check=True)
                        else:
                            ins = pe.matmul(pOff[lo:hi, L * i:L * i + L], vo[:, vo_at(m, i), p, :], wi,
                                            start=False, stop=(m == NM - 2), skip_group_check=True)
                ins.then_inc(s["pv_done"], 1)

            def turn_back(b, hf, last=False):
                pe.wait_ge(s["off_done"], 2 * b + hf + 1)
                pe.wait_ge(s["dia_done"], 2 * b + hf + 1)
                if last:
                    pe.wait_ge(s["fin_step"], 10 * b + 5 * hf - 3)
                elif hf == 0:
                    pe.wait_ge(s["decay_sb"], NM * (b + 2))
                elif not isinstance(b, int) or b < B - 2:
                    pe.wait_ge(s["v_sb"], 4 * (b + 3))
                    pe.wait_ge(s["gate_sb"], 4 * (b + 2) + 3)
                else:
                    pe.wait_ge(s["fin_step"], 10 * b + 2)
                for src, M in ((off_sb, M0), (dia_sb, M1)):
                    for i in range(TT):
                        ins = pe.transpose(M[:, P * i:P * i + P], src[:, hf, P * i:P * i + P], ident[:, :])
                ins.then_inc(s["fin_ps"], 1)

            turn(0, first=True)
            project(0)
            values(0)
            values_late()
            sums(0)
            for m in range(NM):
                decay_sums(0, m)
            scores(0, 0, 0)
            scores(0, 0, 1)

            def batch(b, k, first=False, last=False):
                for n in range(NU):
                    for hf in range(2):
                        if n == FIN[hf] and not first:
                            turn_back(b - 1, hf)
                    if not last:
                        if n == TURN:
                            turn(b + 1)
                        if n == QK:
                            project(b + 1)
                        if n == VALUES:
                            values(b + 1)
                        if n == VALUES + 1:
                            values_late()
                        if n == SUMS:
                            sums(b + 1)
                        if DECAY <= n < DECAY + NM:
                            decay_sums(b + 1, n - DECAY)
                    if n + 2 < NU:
                        scores(b, k, n + 2)
                    elif not last:
                        scores(b + 1, 1 - k, n + 2 - NU)
                    if n >= 1:
                        attend(b, k, n - 1)
                    elif not first:
                        attend(b - 1, 1 - k, NU - 1)

            batch(0, 0, first=True)
            with pe.Fori(1, B - 2, 2) as b:
                batch(b, 1)
                batch(b + 1, 0)
            batch(B - 1, 1, last=True)
            attend(B - 1, 1, NU - 1)
            turn_back(B - 1, 0, last=True)
            turn_back(B - 1, 1, last=True)


def experts(nc, x, xs_dram, ys_dram, s, keep, f, w_red, wg, w1, b1, w2, b2, out):
    with ExitStack() as ctx:
        def sb(name, shape, dt=F32):
            return ctx.enter_context(nc.sbuf_tensor(f"f{f}_" + name, shape, dt))

        def psum(name, shape):
            return ctx.enter_context(nc.psum_tensor(f"f{f}_" + name, shape, F32))

        def sem(name):
            return ctx.enter_context(nc.semaphore(name))

        xs_in, ws_in, ys_out, gat = s["xs_in"], s["ws_in"], s["ys_out"], s["gat"]

        def before_slot(r, q, n=1):
            return r + (q - n) // SLOTS, (q - n) % SLOTS

        ident = keep["ident"]
        before = keep["before"]
        ones = keep["ones"]
        zero = keep["zero"]
        pref = keep["pref"]
        restart_e = keep["restart_e"]
        tile_at = keep["tile_at"]
        k_at = keep["k_at"]
        stats = sb("stats", [P, NT, 6])
        mv = sb("mv", [P, NT, 2])
        rstd = sb("rstd", [P, 4, NT])
        xa = sb("xa", [P, NT, C])
        rT = sb("rT", [P, 2, T])
        red = sb("red", [GD, 2, T])
        wred_sb = keep["wred_sb"]
        wg_sb = sb("wg_sb", [E, GD])
        wg_sq = sb("wg_sq", [E, GD])
        wg_n = sb("wg_n", [E, 4])
        wgT_s = keep["wgT_s"]
        b_in = sb("b_in", [E * NF + E, P])
        b1T = keep["b1T"]
        b2T = keep["b2T"]
        lg = sb("lg", [P, NT, E])
        lgx = sb("lgx", [P, NT, E])
        hit = sb("hit", [P, NT, E])
        top = sb("top", [P, NT])
        first = sb("first", [P, NT])
        score = sb("score", [P, NT])
        lsum = sb("lsum", [P, NT])
        oh = sb("oh", [P, E, NT])
        tot = sb("tot", [P, E, NT])
        cinc = sb("cinc", [P, E, NT])
        p_at = sb("p_at", [P, E, NT])
        more = sb("more", [P, E, NT * P // ST])
        n_til = sb("n_til", [P, E])
        ends = sb("ends", [P, E])
        base = sb("base", [P, E])
        pos_f = sb("pos_f", [P, NT])
        pos = sb("pos", [P, NT], I32)
        past = sb("past", [P, NS, E])
        texp_f = sb("texp_f", [P, NS])
        texp = sb("texp", [P, NS], I32)
        one8 = keep["one8"]
        xs = sb("xs", [P, SLOTS, NC2, C])
        w1s = sb("w1s", [P, SLOTS, F])
        w2s = sb("w2s", [P, SLOTS, NF, C])
        b1s = sb("b1s", [P, SLOTS, NF])
        b2s = sb("b2s", [P, SLOTS, 1])
        xsT = sb("xsT", [P, 2, ST])
        hs = sb("hs", [P, 2, NF, ST])
        ysT = sb("ysT", [P, 2, ST])
        yo = sb("yo", [P, SLOTS, NC2, C])
        bA = psum("bA", [P, T])
        bB = psum("bB", [P, T])
        bH = psum("bH", [P, 4, T])
        bY = psum("bY", [P, T])
        bO = psum("bO", [P, T])
        block = ctx.enter_context(nc.Block())

        @block.sync
        def _(sp):
            if f == 0:
                sp.dma_start(wred_sb[:, :], w_red).then_inc(s["fw_in"], 16)
                sp.dma_start(wg_sb[:, :], wg).then_inc(s["fw_in"], 16)
                sp.dma_start(b_in[0:E * NF, :], b1.rearrange("e (k p) -> (e k) p", p=P)).then_inc(s["fw_in"], 16)
                sp.dma_start(b_in[E * NF:E * NF + E, :], b2).then_inc(s["fw_in"], 16)
                sp.wait_ge(s["f_consts"], 1)
                for k in range(NS * ST // 1024):
                    n = min(1024, NS * ST - 1024 * k)
                    sp.dma_start(xs_dram[1024 * k:1024 * k + n, :].rearrange("(p a) c -> p (a c)", p=P),
                                 zero[:, 0:n // P * C]).then_inc(s["zero_done"], 16)

                sp.wait_ge(s["wgT_sb"], 3)

            def ffn(f):
                sp.wait_ge(s["texp_done"], f + 1)
                sp.wait_ge(s["scat_done"], 16 * NT * (f + 1))

                def load(r, q):
                    j = SLOTS * r + q
                    g = NS * f + j
                    e = sp.value_load(texp[0:1, bass.ds(j, 1)], min_val=0, max_val=E - 1)
                    late = f > 0 or not isinstance(r, int) or r > 0
                    if late:
                        sp.wait_ge(s["x_ps"], g - SLOTS + 1)
                    sp.dma_start(xs[:, q, :, :], xs_dram[bass.ds(j * ST, ST), :]
                                 .rearrange("(a p) c -> p a c", p=P)).then_inc(xs_in[q], 16)
                    if late:
                        sp.wait_ge(s["h_sb"], g - SLOTS + 1)
                    sp.dma_start(w1s[:, q, :], w1[bass.ds(e, 1), :, :].rearrange("e p f -> p (e f)"))\
                        .then_inc(ws_in[q], 16)
                    sp.dma_start(b1s[:, q, :], b1T[:, bass.ds(e, 1), :].rearrange("p e k -> p (e k)"))\
                        .then_inc(ws_in[q], 16)
                    if late:
                        sp.wait_ge(s["y_sb"], g - SLOTS + 1)
                    sp.dma_start(w2s[:, q, :, :], w2[bass.ds(e, 1), :, :].rearrange("e (k p) d -> p (e k) d", p=P))\
                        .then_inc(ws_in[q], 16)
                    sp.dma_start(b2s[:, q, :], b2T[:, bass.ds(e, 1)]).then_inc(ws_in[q], 16)

                def store(r, q):
                    j = SLOTS * r + q
                    sp.wait_ge(s["o_sb"], NS * f + j + 1)
                    sp.dma_start(ys_dram[bass.ds(j * ST, ST), :].rearrange("(a p) c -> p a c", p=P),
                                 yo[:, q, :, :]).then_inc(ys_out[q], 16)

                for q in range(SLOTS):
                    load(0, q)
                with sp.Fori(0, NR - 1) as r:
                    for q in range(SLOTS):
                        load(r + 1, q)
                        store(r, q)
                for q in range(SLOTS):
                    store(NR - 1, q)

            ffn(f)
            if f == 1:
                sp.wait_ge(s["add_done"], 2 * NT)
                for k in range(B):
                    sp.dma_start(out[k].rearrange("(i p) c -> p i c", p=P),
                                 x[:, TT * k:TT * (k + 1), :]).then_inc(s["x_out"], 16)
                sp.wait_ge(s["x_out"], 16 * B)

        @block.gpsimd
        def _(pool):
            st = 0

            def step(ins):
                nonlocal st
                st += 1
                ins.then_inc(s["fc_step"], 1)
                pool.wait_ge(s["fc_step"], st)

            if f == 0:
                step(pool.memset(ident[:, :], 0.0))
                step(pool.memset(zero[:, :], 0.0))
                step(pool.memset(before[:, :], 1.0))
                step(pool.memset(ones[:, :], 1.0))
                step(pool.memset(one8[:, :], 1.0))
                step(pool.memset(restart_e[:, :, :], 1.0))
                step(pool.memset(restart_e[:, :, 0:1], 0.0))
                step(pool.affine_select(out=ident[:, :], in_=ident[:, :], compare_op=ALU.not_equal, fill=1.0,
                                        base=0, pattern=[[-1, P]], channel_multiplier=1))
                step(pool.affine_select(out=before[:, :], in_=before[:, :], compare_op=ALU.is_ge, fill=0.0,
                                        base=-1, pattern=[[1, P]], channel_multiplier=-1))
                step(pool.iota(pref[:, :], [[-1, E]], base=E, channel_multiplier=0,
                               allow_small_or_imprecise_dtypes=True))
                step(pool.iota(tile_at[:, :], [[1, NS]], base=0, channel_multiplier=0,
                               allow_small_or_imprecise_dtypes=True))
                step(pool.iota(k_at[:, :], [[ST, NT * P // ST]], base=0, channel_multiplier=0,
                               allow_small_or_imprecise_dtypes=True))
                pool.memset(zero[:, 0:1], 0.0).then_inc(s["f_consts"], 1)

            def ffn(f):
                pool.wait_ge(s["zero_done"], 16 * (NS * ST // 1024))
                pool.wait_ge(s["pos_done"], f + 1)
                for i in range(NT):
                    pool.indirect_dma_start(xs_dram[:, :], bass.IndirectOffsetOnAxis(ap=pos[:, i:i + 1], axis=0),
                                            xa[:, i, :], None).then_inc(s["scat_done"], 16)

                for q in range(SLOTS):
                    pool.wait_ge(ys_out[q], 16 * NR * (f + 1))
                pool.wait_ge(s["scat_done"], 16 * NT * (f + 1))
                for i in range(NT):
                    if i >= SLOTS:
                        pool.wait_ge(gat[i % SLOTS], 16 * (NT // SLOTS * f + i // SLOTS))
                    pool.indirect_dma_start(xa[:, i, :], None, ys_dram[:, :],
                                            bass.IndirectOffsetOnAxis(ap=pos[:, i:i + 1], axis=0))\
                        .then_inc(gat[i % SLOTS], 16)

            ffn(f)

        @block.scalar
        def _(act):
            if f == 0:
                act.wait_ge(s["wg_step"], 1)
                act.activation(wg_n[:, 1:2], wg_n[:, 0:1], ACT.Sqrt).then_inc(s["wg_step"], 1)

            def ffn(f):
                act.wait_ge(s["rstd_step"], 6 * f + 1)
                act.activation(rstd[:, 2, :], rstd[:, 1, :], ACT.Sqrt).then_inc(s["rstd_step"], 1)
                for g in range(B):
                    q = B * f + g
                    act.wait_ge(s["rT_ps"], q + 1)
                    if q >= 2:
                        act.wait_ge(s["red_ps"], q - 1)
                    act.activation(rT[:, g % 2, :], bA[:, :], ACT.Copy).then_inc(s["rT_sb"], 1)
                act.wait_ge(s["lg_step"], 4 * f + 3)
                act.activation(lgx[:, :, :].rearrange("p i e -> p (i e)"),
                               lgx[:, :, :].rearrange("p i e -> p (i e)"), ACT.Exp).then_inc(s["lg_exp"], 1)

                def x_copy(r, q, late=True):
                    g = NS * f + SLOTS * r + q
                    act.wait_ge(s["x_ps"], g + 1)
                    if late:
                        act.wait_ge(s["h_ps"], g - 1)
                    act.activation(xsT[:, q % 2, :], bA[:, 0:ST], ACT.Copy).then_inc(s["x_sb"], 1)

                def gelu(r, q, late=True):
                    g = NS * f + SLOTS * r + q
                    act.wait_ge(s["h_ps"], g + 1)
                    act.wait_ge(ws_in[q], 64 * (NR * f + r + 1))
                    if late:
                        act.wait_ge(s["y_ps"], g - 1)
                    for n in range(NF):
                        ins = act.activation(hs[:, q % 2, n, :],
                                             bH[:, 2 * (q % 2) + n // 2, ST * (n % 2):ST * (n % 2) + ST],
                                             ACT.Gelu, bias=b1s[:, q, n:n + 1])
                    ins.then_inc(s["h_sb"], 1)

                def run(r, late=True, last=False):
                    for q in range(SLOTS):
                        if not (last and q == SLOTS - 1):
                            x_copy(*before_slot(r, q, -1), late or q >= 1)
                        gelu(r, q, late or q >= 2)

                x_copy(0, 0, late=f > 0)
                run(0, late=f > 0)
                with act.Fori(1, NR - 1) as r:
                    run(r)
                run(NR - 1, last=True)

            ffn(f)

        @block.vector
        def _(dve):
            if f == 0:
                dve.wait_ge(s["fw_in"], 64)
                dve.tensor_tensor_reduce(wg_sq[:, :], wg_sb[:, :], wg_sb[:, :], 1.0, 0.0, ALU.mult, ALU.add,
                                         wg_n[:, 0:1]).then_inc(s["wg_step"], 1)
                dve.wait_ge(s["wg_step"], 2)
                dve.tensor_scalar(wg_n[:, 2:3], wg_n[:, 1:2], EPS_G, None, ALU.max).then_inc(s["wg_step"], 1)
                dve.wait_ge(s["wg_step"], 3)
                dve.reciprocal(wg_n[:, 3:4], wg_n[:, 2:3]).then_inc(s["wg_step"], 1)
                dve.wait_ge(s["wg_step"], 4)
                dve.tensor_scalar(wg_sq[:, :], wg_sb[:, :], wg_n[:, 3:4], None, ALU.mult).then_inc(s["wg_step"], 1)
                dve.wait_ge(s["wgT_ps"], 1)
                dve.tensor_copy(wgT_s[:, :], bB[0:GD, 0:E]).then_inc(s["wgT_sb"], 1)
                dve.tensor_copy(b1T[:, :, :].rearrange("p e k -> p (e k)"), bB[:, 64:64 + E * NF]).then_inc(s["wgT_sb"], 1)
                dve.tensor_copy(b2T[:, :], bB[:, 64 + E * NF:64 + E * NF + E]).then_inc(s["wgT_sb"], 1)

            def layernorm(f):
                n0 = 2 * NT * f
                for i in range(NT):
                    dve.bn_stats(stats[:, i, :], x[:, i, :]).then_inc(s["stat_done"], 1)
                for i in range(NT):
                    dve.wait_ge(s["stat_done"], n0 + i + 1)
                    dve.bn_aggr(mv[:, i, :], stats[:, i, :]).then_inc(s["stat_done"], 1)
                dve.wait_ge(s["stat_done"], n0 + 2 * NT)
                dve.tensor_scalar(rstd[:, 1, :], mv[:, :, 1], EPS_LN, None, ALU.add).then_inc(s["rstd_step"], 1)
                dve.wait_ge(s["rstd_step"], 6 * f + 2)
                dve.reciprocal(rstd[:, 3, :], rstd[:, 2, :]).then_inc(s["rstd_step"], 1)
                dve.wait_ge(s["rstd_step"], 6 * f + 3)
                dve.tensor_tensor(rstd[:, 2, :], rstd[:, 3, :], rstd[:, 3, :], ALU.mult).then_inc(s["rstd_step"], 1)
                dve.wait_ge(s["rstd_step"], 6 * f + 4)
                dve.tensor_tensor(rstd[:, 2, :], rstd[:, 2, :], rstd[:, 1, :], ALU.mult).then_inc(s["rstd_step"], 1)
                dve.wait_ge(s["rstd_step"], 6 * f + 5)
                dve.tensor_scalar(rstd[:, 2, :], rstd[:, 2, :], -0.5, 1.5, ALU.mult, ALU.add)\
                    .then_inc(s["rstd_step"], 1)
                dve.wait_ge(s["rstd_step"], 6 * f + 6)
                dve.tensor_tensor(rstd[:, 0, :], rstd[:, 2, :], rstd[:, 3, :], ALU.mult).then_inc(s["rstd_ready"], 1)

            def ffn(f):
                layernorm(f)
                dve.wait_ge(s["rstd_ready"], f + 1)
                for i in range(NT):
                    dve.tensor_scalar(xa[:, i, :], x[:, i, :], mv[:, i, 0:1], rstd[:, 0, i:i + 1],
                                      ALU.subtract, ALU.mult).then_inc(s["xnf_done"], 1)
                for g in range(B):
                    q = B * f + g
                    dve.wait_ge(s["red_ps"], q + 1)
                    if q >= 2:
                        dve.wait_ge(s["lg_ps"], q - 1)
                    dve.tensor_copy(red[:, g % 2, :], bB[0:GD, :]).then_inc(s["red_sb"], 1)
                dve.wait_ge(s["lg_ps"], B * (f + 1))
                dve.tensor_copy(lg[:, :, :].rearrange("p i e -> p (i e)"), bY[:, 0:NT * E]).then_inc(s["lg_step"], 1)
                dve.wait_ge(s["lg_step"], 4 * f + 1)
                dve.tensor_reduce(top[:, :], lg[:, :, :], AX.X, ALU.max).then_inc(s["lg_step"], 1)
                dve.wait_ge(s["lg_step"], 4 * f + 2)
                tb = top[:, :].unsqueeze(2).broadcast_to([P, NT, E])
                dve.tensor_tensor(lgx[:, :, :], lg[:, :, :], tb, ALU.subtract).then_inc(s["lg_step"], 1)
                dve.tensor_tensor(hit[:, :, :], lg[:, :, :], tb, ALU.is_equal).then_inc(s["lg_step"], 1)
                dve.wait_ge(s["lg_step"], 4 * f + 4)
                n0 = 5 * f
                dve.tensor_tensor(hit[:, :, :], hit[:, :, :], pref[:, :].unsqueeze(1).broadcast_to([P, NT, E]),
                                  ALU.mult).then_inc(s["oh_done"], 1)
                dve.wait_ge(s["oh_done"], n0 + 1)
                dve.tensor_reduce(first[:, :], hit[:, :, :], AX.X, ALU.max).then_inc(s["oh_done"], 1)
                dve.wait_ge(s["oh_done"], n0 + 2)
                dve.tensor_tensor(oh[:, :, :], pref[:, :].unsqueeze(2).broadcast_to([P, E, NT]),
                                  first[:, :].unsqueeze(1).broadcast_to([P, E, NT]), ALU.is_equal)\
                    .then_inc(s["oh_done"], 1)
                dve.wait_ge(s["lg_exp"], f + 1)
                dve.tensor_reduce(lsum[:, :], lgx[:, :, :], AX.X, ALU.add).then_inc(s["oh_done"], 1)
                dve.wait_ge(s["oh_done"], n0 + 4)
                dve.reciprocal(score[:, :], lsum[:, :]).then_inc(s["oh_done"], 1)
                dve.wait_ge(s["rank_ps"], f + 1)
                at = 12 * f

                def step(ins):
                    nonlocal at
                    at += 1
                    ins.then_inc(s["pos_step"], 1)
                    dve.wait_ge(s["pos_step"], at)

                flat = [t[:, :, :].rearrange("p e i -> p (e i)") for t in (tot, cinc, restart_e)]
                step(dve.tensor_copy(flat[0], bA[:, 256:512]))
                step(dve.tensor_tensor_scan(flat[1], flat[2], flat[0], 0.0, ALU.mult, ALU.add))
                nk = NT * P // ST
                step(dve.tensor_tensor(more[:, :, :], cinc[:, :, NT - 1:NT].broadcast_to([P, E, nk]),
                                       k_at[:, :].unsqueeze(1).broadcast_to([P, E, nk]), ALU.is_gt))
                step(dve.tensor_reduce(n_til[:, :], more[:, :, :], AX.X, ALU.add))
                step(dve.tensor_tensor_scan(ends[:, :], one8[:, :], n_til[:, :], 0.0, ALU.mult, ALU.add))
                step(dve.tensor_tensor(base[:, :], ends[:, :], n_til[:, :], ALU.subtract))
                step(dve.tensor_tensor(p_at[:, :, :], cinc[:, :, :], tot[:, :, :], ALU.subtract))
                step(dve.scalar_tensor_tensor(p_at[:, :, :], base[:, :].unsqueeze(2).broadcast_to([P, E, NT]),
                                              float(ST), p_at[:, :, :], ALU.mult, ALU.add))
                pf = p_at[:, :, :].rearrange("p e i -> p (e i)")
                step(dve.tensor_tensor(pf, bA[:, 0:256], pf, ALU.add))
                step(dve.tensor_tensor(p_at[:, :, :], p_at[:, :, :], oh[:, :, :], ALU.mult))
                step(dve.tensor_reduce(pos_f[:, :], p_at[:, :, :].rearrange("p e i -> p i e"), AX.X, ALU.add))
                dve.tensor_copy(pos[:, :], pos_f[:, :]).then_inc(s["pos_done"], 1)
                step(dve.tensor_tensor(past[:, :, :], tile_at[:, :].unsqueeze(2).broadcast_to([P, NS, E]),
                                       ends[:, :].unsqueeze(1).broadcast_to([P, NS, E]), ALU.is_ge))
                dve.tensor_reduce(texp_f[:, :], past[:, :, :], AX.X, ALU.add).then_inc(s["lg_sum"], 1)
                dve.wait_ge(s["lg_sum"], f + 1)
                dve.tensor_scalar(texp[:, :], texp_f[:, :], float(E - 1), None, ALU.min)\
                    .then_inc(s["texp_done"], 1)

                def y_bias(r, q, late=True):
                    g = NS * f + SLOTS * r + q
                    dve.wait_ge(s["y_ps"], g + 1)
                    dve.wait_ge(ws_in[q], 64 * (NR * f + r + 1))
                    if late:
                        dve.wait_ge(s["o_ps"], g - 1)
                    dve.tensor_scalar(ysT[:, q % 2, :], bY[:, 0:ST], b2s[:, q, 0:1], None, ALU.add)\
                        .then_inc(s["y_sb"], 1)

                def y_out(r, q, late=True):
                    g = NS * f + SLOTS * r + q
                    dve.wait_ge(s["o_ps"], g + 1)
                    if late:
                        dve.wait_ge(ys_out[q], 16 * (NR * f + r))
                    dve.tensor_copy(yo[:, q, :, :].rearrange("p a c -> p (a c)"), bO[:, 0:ST])\
                        .then_inc(s["o_sb"], 1)

                for q in range(SLOTS):
                    y_bias(0, q, late=f > 0 or q >= 2)
                    y_out(0, q, late=f > 0)
                with dve.Fori(1, NR) as r:
                    for q in range(SLOTS):
                        y_bias(r, q)
                        y_out(r, q)
                for i in range(NT):
                    dve.wait_ge(gat[i % SLOTS], 16 * (NT // SLOTS * f + i // SLOTS + 1))
                    dve.scalar_tensor_tensor(x[:, i, :], xa[:, i, :], score[:, i:i + 1], x[:, i, :],
                                             ALU.mult, ALU.add).then_inc(s["add_done"], 1)

            ffn(f)

        @block.tensor
        def _(pe):
            if f == 0:
                pe.wait_ge(s["f_consts"], 1)
                pe.wait_ge(s["wg_step"], 5)
                pe.transpose(bB[:, 64:64 + E * NF + E], b_in[:, :], ident[0:E * NF + E, 0:E * NF + E])
                pe.transpose(bB[0:GD, 0:E], wg_sq[:, :], ident[0:E, 0:E]).then_inc(s["wgT_ps"], 1)
                pe.wait_ge(s["wgT_sb"], 3)

            def ffn(f):
                for g in range(B):
                    q = B * f + g
                    pe.wait_ge(s["xnf_done"], NT * f + TT * g + TT)
                    pe.wait_ge(s["rT_sb"], q)
                    for i in range(TT):
                        ins = pe.transpose(bA[:, P * i:P * i + P], xa[:, TT * g + i, :], ident[:, :])
                    ins.then_inc(s["rT_ps"], 1)
                    pe.wait_ge(s["rT_sb"], q + 1)
                    pe.wait_ge(s["red_sb"], q)
                    pe.matmul(bB[0:GD, :], wred_sb[:, :], rT[:, g % 2, :], start=True, stop=True)\
                        .then_inc(s["red_ps"], 1)
                    pe.wait_ge(s["red_sb"], q + 1)
                    for i in range(TT):
                        c = E * (TT * g + i)
                        ins = pe.matmul(bY[:, c:c + E], red[:, g % 2, P * i:P * i + P], wgT_s[:, :],
                                        start=True, stop=True)
                    ins.then_inc(s["lg_ps"], 1)
                pe.wait_ge(s["oh_done"], 5 * f + 3)
                ohf = oh[:, :, :].rearrange("p e i -> p (e i)")
                pe.matmul(bA[:, 0:256], before[:, :], ohf, start=True, stop=True)
                pe.matmul(bA[:, 256:512], ones[:, :], ohf, start=True, stop=True).then_inc(s["rank_ps"], 1)
                pe.wait_ge(s["pos_done"], f + 1)

                def turn_x(r, q, late=True):
                    g = NS * f + SLOTS * r + q
                    pe.wait_ge(xs_in[q], 16 * (NR * f + r + 1))
                    if late:
                        pe.wait_ge(s["x_sb"], g)
                    for a in range(NC2):
                        ins = pe.transpose(bA[:, P * a:P * a + P], xs[:, q, a, :], ident[:, :])
                    ins.then_inc(s["x_ps"], 1)

                def up(r, q, late=True):
                    g = NS * f + SLOTS * r + q
                    pe.wait_ge(ws_in[q], 64 * (NR * f + r + 1))
                    pe.wait_ge(s["x_sb"], g + 1)
                    if late:
                        pe.wait_ge(s["h_sb"], g - 1)
                    for n in range(NF):
                        ins = pe.matmul(bH[:, 2 * (q % 2) + n // 2, ST * (n % 2):ST * (n % 2) + ST],
                                        w1s[:, q, P * n:P * n + P], xsT[:, q % 2, :], start=True, stop=True)
                    ins.then_inc(s["h_ps"], 1)

                def down(r, q, late=True):
                    g = NS * f + SLOTS * r + q
                    pe.wait_ge(s["h_sb"], g + 1)
                    if late:
                        pe.wait_ge(s["y_sb"], g)
                    for n in range(NF):
                        ins = pe.matmul(bY[:, 0:ST], w2s[:, q, n, :], hs[:, q % 2, n, :], start=(n == 0),
                                        stop=(n == NF - 1))
                    ins.then_inc(s["y_ps"], 1)

                def turn_y(r, q, late=True):
                    g = NS * f + SLOTS * r + q
                    pe.wait_ge(s["y_sb"], g + 1)
                    if late:
                        pe.wait_ge(s["o_sb"], g)
                    for a in range(NC2):
                        ins = pe.transpose(bO[:, P * a:P * a + P], ysT[:, q % 2, P * a:P * a + P], ident[:, :])
                    ins.then_inc(s["o_ps"], 1)

                def run(r, first=False, last=False):
                    for q in range(SLOTS):
                        if not (last and q == SLOTS - 1):
                            turn_x(*before_slot(r, q, -1))
                        late = f > 0 or not first
                        up(r, q, late or q >= 2)
                        if not first or q >= 2:
                            turn_y(*before_slot(r, q, 2), late or q >= 3)
                        if not first or q >= 1:
                            down(*before_slot(r, q, 1), late or q >= 2)

                turn_x(0, 0, late=f > 0)
                run(0, first=True)
                with pe.Fori(1, NR - 1) as r:
                    run(r)
                run(NR - 1, last=True)
                turn_y(NR - 1, SLOTS - 2)
                down(NR - 1, SLOTS - 1)
                turn_y(NR - 1, SLOTS - 1)

            ffn(f)


def delta_rule(nc, x, Wq, Wk, Wv, Wgamma, Wf, Wg1, Wg2, Wo, norm_w):
    with ExitStack() as ctx:
        def sb(name, shape, dt=F32):
            return ctx.enter_context(nc.sbuf_tensor("d_" + name, shape, dt))

        def psum(name, shape):
            return ctx.enter_context(nc.psum_tensor("d_" + name, shape, F32))

        def sem(name):
            return ctx.enter_context(nc.semaphore(name))

        head_dram = nc.dram_tensor("head_dram", [3, B, P, T], F32, kind="Internal").ap()
        fg_dram = nc.dram_tensor("fg_dram", [2, B, H, T], F32, kind="Internal").ap()
        o_dram = nc.dram_tensor("o_dram", [B, P, T], F32, kind="Internal").ap()
        s = {}
        for n in """cc_step c_consts stat_done rstd_step rstd_ready cw_in cn_done cT_ps cT_sb
            cq_ps cq_sb cf_ps cf_sb cg1_ps cg1_sb cg2_ps cg2_sb cq_out cf_out bh_in knorm_step knorm_sq kn_done
            fg_sig decay_step kk_step kk_pool qk_mul qk_red w_step u_pool u_done chain po_mul po_done o_red
            o_out gate_sig og_done wo_step cs_ps oy_ps ost_step o_sqrt ost_done""".split():
            s[n] = sem("d_" + n)
        o_in = [sem(f"o_in{k}") for k in range(3)]
        ident = sb("ident", [P, P])
        ones = sb("ones", [P, P])
        stats = sb("stats", [P, NT, 6])
        mv = sb("mv", [P, NT, 2])
        rstd = sb("rstd", [P, 4, NT])
        wqkv = sb("wqkv", [P, 3, C])
        wfg = sb("wfg", [P, 2 * H])
        wg1 = sb("wg1", [P, HD])
        wg2 = sb("wg2", [HD, C])
        wo = sb("wo", [P, C])
        nw = sb("nw", [P, 1])
        wcol = sb("wcol", [P, C])
        act3 = sb("act3", [P, 3, T])
        gate = sb("gate", [P, B, T])
        Q = sb("Q", [P, HD, T])
        K = sb("K", [P, HD, T])
        V = sb("V", [P, HD, T])
        W = sb("W", [P, HD, T])
        O = W
        fg = sb("fg", [P, 2, T])
        alpha = sb("alpha", [P, T])
        beta = sb("beta", [P, T])
        G = sb("G", [P, CH, CH + 1, NCH])
        LL = sb("LL", [P, CH, CH, NCH])
        QQ = sb("QQ", [P, CH, CH, NCH])
        pb_d = sb("pb_d", [P, CH * HD * NCH])
        pb_p = sb("pb_p", [P, CH * HD * NCH])
        cn = pb_d[:, 0:2 * T].rearrange("p (k i c) -> p k i c", k=2, c=C)
        cT = pb_p[:, 0:T]
        fgl = pb_p[0:2 * H, T:2 * T]
        red1 = pb_p[0:HD, 2 * T:3 * T]
        S = sb("S", [P, 4, HD, HD])
        uw = sb("uw", [P, CH, HD])
        sr = sb("sr", [P, HD, HD])
        og = act3
        ost = sb("ost", [P, TT, 6])
        omv = sb("omv", [P, TT, 2])
        ors = sb("ors", [P, 4, TT])
        c0 = psum("c0", [P, T])
        c1 = psum("c1", [P, T])
        c2 = psum("c2", [P, T])
        c3 = psum("c3", [P, T])
        c4 = psum("c4", [P, T])
        c5 = psum("c5", [P, T])
        c6 = psum("c6", [P, T])
        cqkv = (c1, c2, c3)
        block = ctx.enter_context(nc.Block())

        def chunked(t, first=0, n=CH):
            return t[:, :, :].rearrange("p d (c j) -> p j c d", j=CH)[:, first:first + n]

        @block.sync
        def _(sp):
            for i, w in enumerate((Wq, Wk, Wv)):
                sp.dma_start(wqkv[:, i, :], w).then_inc(s["cw_in"], 16)
            sp.dma_start(wfg[:, 0:H], Wf).then_inc(s["cw_in"], 16)
            sp.dma_start(wfg[:, H:2 * H], Wgamma).then_inc(s["cw_in"], 16)
            sp.dma_start(wg1[:, :], Wg1).then_inc(s["cw_in"], 16)
            sp.dma_start(wg2[:, :], Wg2).then_inc(s["cw_in"], 16)
            sp.dma_start(wo[:, :], Wo).then_inc(s["cw_in"], 16)
            sp.dma_start(nw[:, :], norm_w.rearrange("(p a) -> p a", a=1)).then_inc(s["cw_in"], 16)

            def relayout():
                for b in range(B):
                    sp.wait_ge(s["cq_sb"], 3 * b + 3)
                    for i in range(3):
                        sp.dma_start(head_dram[i, b], act3[:, i, :]).then_inc(s["cq_out"], 16)
                    sp.wait_ge(s["cf_sb"], b + 1)
                    for i in range(2):
                        sp.dma_start(fg_dram[i, b], fgl[H * i:H * i + H, :]).then_inc(s["cf_out"], 16)
                sp.wait_ge(s["cf_out"], 32 * B)
                sp.dma_start(fg[:, 0, :], fg_dram[0].rearrange("b h t -> (b h) t")).then_inc(s["bh_in"], 16)
                sp.dma_start(fg[:, 1, :], fg_dram[1].rearrange("b h t -> (b h) t")).then_inc(s["bh_in"], 16)
                sp.wait_ge(s["cq_out"], 48 * B)
                for i, t in ((1, K), (0, Q), (2, V)):
                    sp.dma_start(t[:, :, :].rearrange("p d t -> p (d t)"),
                                 head_dram[i].rearrange("b (h d) t -> (b h) (d t)", d=HD)).then_inc(s["bh_in"], 16)

            def back():
                sp.wait_ge(s["o_red"], NCH)
                for b in range(B):
                    sp.dma_start(o_dram[b].rearrange("(h d) t -> h (d t)", d=HD),
                                 O[H * b:H * b + H, :, :].rearrange("p d t -> p (d t)")).then_inc(s["o_out"], 16)
                sp.wait_ge(s["o_out"], 16 * B)
                for b in range(B):
                    if b >= 3:
                        sp.wait_ge(s["oy_ps"], b - 2)
                    sp.dma_start(og[:, b % 3, :], o_dram[b]).then_inc(o_in[b % 3], 16)

            relayout()
            back()

        @block.gpsimd
        def _(pool):
            st = 0

            def step(ins):
                nonlocal st
                st += 1
                ins.then_inc(s["cc_step"], 1)
                pool.wait_ge(s["cc_step"], st)

            step(pool.memset(ident[:, :], 0.0))
            step(pool.memset(ones[:, :], 1.0))
            step(pool.memset(QQ[:, :, :, :].rearrange("p j i c -> p (j i c)"), 0.0))
            step(pool.memset(G[:, :, :, :].rearrange("p j i c -> p (j i c)"), 1.0))
            step(pool.memset(S[:, 0, :, :].rearrange("p v k -> p (v k)"), 0.0))
            pool.affine_select(out=ident[:, :], in_=ident[:, :], compare_op=ALU.not_equal, fill=1.0,
                               base=0, pattern=[[-1, P]], channel_multiplier=1).then_inc(s["c_consts"], 1)

            def products():
                pool.wait_ge(s["bh_in"], 80)
                pool.wait_ge(s["kn_done"], 1)
                for j in range(CH):
                    n = j + 1
                    if j:
                        pool.wait_ge(s["qk_red"], j)
                    pool.tensor_tensor(pb_p[:, 0:512 * n].rearrange("p (i c d) -> p i c d", c=NCH, d=HD),
                                       chunked(K, 0, n), chunked(Q, j, 1).broadcast_to([P, n, NCH, HD]), ALU.mult)\
                        .then_inc(s["qk_mul"], 1)
                pool.wait_ge(s["kk_step"], 1)
                pool.wait_ge(s["qk_red"], CH)
                n = 0
                for i in range(CH - 1):
                    m = CH - 1 - i
                    t = pb_p[:, 0:512 * m].rearrange("p (j c d) -> p j c d", c=NCH, d=HD)
                    if n:
                        pool.wait_ge(s["u_pool"], n)
                    pool.tensor_tensor(t, LL[:, i + 1:CH, i, :].unsqueeze(3).broadcast_to([P, m, NCH, HD]),
                                       chunked(V, i, 1).broadcast_to([P, m, NCH, HD]), ALU.mult)\
                        .then_inc(s["u_pool"], 1)
                    pool.wait_ge(s["u_pool"], n + 1)
                    pool.tensor_tensor(chunked(V, i + 1, m), chunked(V, i + 1, m), t, ALU.add)\
                        .then_inc(s["u_pool"], 1)
                    n += 2

            def outputs(r, a):
                c = 4 * r + a
                cs = bass.ds(CH * c, CH)
                po = pb_p[:, 2048 * (a % 2):2048 * (a % 2) + 1024].rearrange("p (j v k) -> p j v k", v=HD, k=16)
                fo = pb_p[:, 2048 * (a % 2) + 1024:2048 * (a % 2) + 1536].rearrange("p (j v k) -> p j v k", v=HD, k=8)
                pool.wait_ge(s["chain"], 6 * c + 1)
                if not (isinstance(r, int) and r == 0 and a < 2):
                    pool.wait_ge(s["o_red"], c - 1)
                pool.tensor_tensor(po[:, :, :, 0:8],
                                   Q[:, :, cs].rearrange("p k j -> p j k").unsqueeze(2).broadcast_to([P, CH, HD, HD]),
                                   S[:, a, :, :].unsqueeze(1).broadcast_to([P, CH, HD, HD]), ALU.mult)\
                    .then_inc(s["po_mul"], 1)
                pool.wait_ge(s["chain"], 6 * c + 4)
                pool.tensor_tensor(po[:, :, :, 8:16],
                                   QQ[:, :, :, bass.ds(c, 1)].rearrange("p j i c -> p j (i c)").unsqueeze(2)
                                   .broadcast_to([P, CH, HD, CH]),
                                   V[:, :, cs].unsqueeze(1).broadcast_to([P, CH, HD, CH]), ALU.mult)\
                    .then_inc(s["po_mul"], 1)
                pool.wait_ge(s["po_mul"], 2 * c + 2)
                pool.tensor_tensor(fo, po[:, :, :, 0:8], po[:, :, :, 8:16], ALU.add).then_inc(s["po_done"], 1)

            products()
            for a in range(4):
                outputs(0, a)
            with pool.Fori(1, NCH // 4) as r:
                for a in range(4):
                    outputs(r, a)

        @block.scalar
        def _(act):
            act.wait_ge(s["rstd_step"], 1)
            act.activation(rstd[:, 2, :], rstd[:, 1, :], ACT.Sqrt).then_inc(s["rstd_step"], 1)

            for b in range(B):
                act.wait_ge(s["cT_ps"], b + 1)
                if b:
                    act.wait_ge(s["cg1_ps"], b)
                act.activation(cT[:, :], c0[:, :], ACT.Copy).then_inc(s["cT_sb"], 1)
                if b:
                    act.wait_ge(s["cf_out"], 32 * b)
                    act.wait_ge(s["cq_out"], 48 * b)
                for i in range(3):
                    act.wait_ge(s["cq_ps"], 3 * b + i + 1)
                    act.activation(act3[:, i, :], cqkv[i][:, :], ACT.Silu).then_inc(s["cq_sb"], 1)
                act.wait_ge(s["cf_ps"], b + 1)
                act.activation(fgl[:, :], c4[0:2 * H, :], ACT.Copy).then_inc(s["cf_sb"], 1)
                act.wait_ge(s["cg1_ps"], b + 1)
                act.activation(red1[:, :], c5[0:HD, :], ACT.Copy).then_inc(s["cg1_sb"], 1)
                act.wait_ge(s["cg2_ps"], b + 1)
                act.activation(gate[:, b, :], c6[:, :], ACT.Copy).then_inc(s["cg2_sb"], 1)
            act.wait_ge(s["bh_in"], 80)
            act.wait_ge(s["knorm_step"], 2)
            act.activation(alpha[:, :], beta[:, :], ACT.Sqrt).then_inc(s["knorm_sq"], 1)
            act.activation(fg[:, :, :].rearrange("p a t -> p (a t)"), fg[:, :, :].rearrange("p a t -> p (a t)"),
                           ACT.Sigmoid).then_inc(s["fg_sig"], 1)
            act.wait_ge(s["cg2_sb"], B)
            act.activation(gate[:, :, :].rearrange("p b t -> p (b t)"), gate[:, :, :].rearrange("p b t -> p (b t)"),
                           ACT.Sigmoid).then_inc(s["gate_sig"], 1)
            for b in range(B):
                act.wait_ge(s["ost_step"], 7 * b + 1)
                act.activation(ors[:, 1, :], ors[:, 0, :], ACT.Sqrt).then_inc(s["o_sqrt"], 1)

        @block.vector
        def _(dve):
            for i in range(NT):
                dve.bn_stats(stats[:, i, :], x[:, i, :]).then_inc(s["stat_done"], 1)
            for i in range(NT):
                dve.wait_ge(s["stat_done"], i + 1)
                dve.bn_aggr(mv[:, i, :], stats[:, i, :]).then_inc(s["stat_done"], 1)
            dve.wait_ge(s["stat_done"], 2 * NT)
            dve.tensor_scalar(rstd[:, 1, :], mv[:, :, 1], EPS_LN, None, ALU.add).then_inc(s["rstd_step"], 1)
            dve.wait_ge(s["rstd_step"], 2)
            dve.reciprocal(rstd[:, 3, :], rstd[:, 2, :]).then_inc(s["rstd_step"], 1)
            dve.wait_ge(s["rstd_step"], 3)
            dve.tensor_tensor(rstd[:, 2, :], rstd[:, 3, :], rstd[:, 3, :], ALU.mult).then_inc(s["rstd_step"], 1)
            dve.wait_ge(s["rstd_step"], 4)
            dve.tensor_tensor(rstd[:, 2, :], rstd[:, 2, :], rstd[:, 1, :], ALU.mult).then_inc(s["rstd_step"], 1)
            dve.wait_ge(s["rstd_step"], 5)
            dve.tensor_scalar(rstd[:, 2, :], rstd[:, 2, :], -0.5, 1.5, ALU.mult, ALU.add).then_inc(s["rstd_step"], 1)
            dve.wait_ge(s["rstd_step"], 6)
            dve.tensor_tensor(rstd[:, 0, :], rstd[:, 2, :], rstd[:, 3, :], ALU.mult).then_inc(s["rstd_ready"], 1)
            dve.wait_ge(s["rstd_ready"], 1)
            for b in range(B):
                if b >= 2:
                    dve.wait_ge(s["cT_ps"], b - 1)
                for i in range(TT):
                    j = TT * b + i
                    dve.tensor_scalar(cn[:, b % 2, i, :], x[:, j, :], mv[:, j, 0:1], rstd[:, 0, j:j + 1],
                                      ALU.subtract, ALU.mult).then_inc(s["cn_done"], 1)

            dve.wait_ge(s["bh_in"], 80)
            dve.tensor_tensor(pb_d[:, 0:HD * T].rearrange("p (d t) -> p d t", d=HD), K[:, :, :], K[:, :, :],
                              ALU.mult).then_inc(s["knorm_step"], 1)
            dve.wait_ge(s["knorm_step"], 1)
            dve.tensor_reduce(beta[:, :], pb_d[:, 0:HD * T].rearrange("p (d t) -> p t d", d=HD), AX.X, ALU.add)\
                .then_inc(s["knorm_step"], 1)
            dve.wait_ge(s["knorm_sq"], 1)
            dve.tensor_scalar(beta[:, :], alpha[:, :], EPS_K, None, ALU.max).then_inc(s["knorm_step"], 1)
            dve.wait_ge(s["knorm_step"], 3)
            dve.reciprocal(alpha[:, :], beta[:, :]).then_inc(s["knorm_step"], 1)
            dve.wait_ge(s["knorm_step"], 4)
            dve.tensor_tensor(K[:, :, :], K[:, :, :], alpha[:, :].unsqueeze(1).broadcast_to([P, HD, T]), ALU.mult)\
                .then_inc(s["kn_done"], 1)
            dve.wait_ge(s["fg_sig"], 1)
            dve.wait_ge(s["c_consts"], 1)
            dn = 0

            def dstep(ins):
                nonlocal dn
                dn += 1
                ins.then_inc(s["decay_step"], 1)
                dve.wait_ge(s["decay_step"], dn)

            f, gm = fg[:, 0, :], fg[:, 1, :]
            fj = f.rearrange("p (c j) -> p j c", j=CH)
            dve.wait_ge(s["kn_done"], 1)
            dstep(dve.scalar_tensor_tensor(alpha[:, :], f, -1.0, f, ALU.mult, ALU.mult))
            dstep(dve.tensor_tensor(alpha[:, :], alpha[:, :], gm, ALU.mult))
            dstep(dve.tensor_copy(G[:, 0, 0, :], fj[:, 0, :]))
            for j in range(1, CH):
                dstep(dve.tensor_tensor(G[:, j, 0:j + 1, :], G[:, j - 1, 0:j + 1, :],
                                        fj[:, j:j + 1, :].broadcast_to([P, j + 1, NCH]), ALU.mult))
            aj = alpha[:, :].rearrange("p (c j) -> p j c", j=CH)
            bj = beta[:, :].rearrange("p (c j) -> p j c", j=CH)
            dstep(dve.tensor_copy(beta[:, :], alpha[:, :]))
            dstep(dve.tensor_tensor(bj[:, 1:CH, :], aj[:, 1:CH, :], G[:, 0:CH - 1, 0, :], ALU.mult))
            dstep(dve.tensor_tensor(W[:, :, :], K[:, :, :], beta[:, :].unsqueeze(1).broadcast_to([P, HD, T]),
                                    ALU.mult))

            kn = 0
            for j in range(CH):
                if j:
                    t = pb_d[:, 0:512 * j].rearrange("p (i c d) -> p i c d", c=NCH, d=HD)
                    dve.tensor_tensor(t, chunked(K, 0, j), chunked(K, j, 1).broadcast_to([P, j, NCH, HD]), ALU.mult)\
                        .then_inc(s["kk_pool"], 1)
                    dve.wait_ge(s["kk_pool"], 3 * j - 2)
                    dve.tensor_reduce(LL[:, j, 0:j, :], t, AX.X, ALU.add).then_inc(s["kk_pool"], 1)
                    dve.wait_ge(s["kk_pool"], 3 * j - 1)
                    dve.tensor_tensor(LL[:, j, 0:j, :], LL[:, j, 0:j, :], G[:, j - 1, 1:j + 1, :], ALU.mult)\
                        .then_inc(s["kk_pool"], 1)
                    dve.wait_ge(s["kk_pool"], 3 * j)
                    ins = dve.tensor_tensor(LL[:, j, 0:j, :], LL[:, j, 0:j, :],
                                            aj[:, j:j + 1, :].broadcast_to([P, j, NCH]), ALU.mult)
                    if j == CH - 1:
                        ins.then_inc(s["kk_step"], 1)
                dve.wait_ge(s["qk_mul"], j + 1)
                n = j + 1
                dve.tensor_reduce(QQ[:, j, 0:n, :],
                                  pb_p[:, 0:512 * n].rearrange("p (i c d) -> p i c d", c=NCH, d=HD), AX.X, ALU.add)\
                    .then_inc(s["qk_red"], 1)
            dve.wait_ge(s["qk_red"], CH)
            for j in range(CH):
                ins = dve.tensor_tensor(QQ[:, j, 0:j + 1, :], QQ[:, j, 0:j + 1, :], G[:, j, 1:j + 2, :], ALU.mult)
            dve.wait_ge(s["kk_step"], 1)
            wn = 0
            for i in range(CH - 1):
                m = CH - 1 - i
                t = pb_d[:, 0:512 * m].rearrange("p (j c d) -> p j c d", c=NCH, d=HD)
                if wn:
                    dve.wait_ge(s["w_step"], wn)
                dve.tensor_tensor(t, LL[:, i + 1:CH, i, :].unsqueeze(3).broadcast_to([P, m, NCH, HD]),
                                  chunked(W, i, 1).broadcast_to([P, m, NCH, HD]), ALU.mult).then_inc(s["w_step"], 1)
                dve.wait_ge(s["w_step"], wn + 1)
                dve.tensor_tensor(chunked(W, i + 1, m), chunked(W, i + 1, m), t, ALU.add).then_inc(s["w_step"], 1)
                wn += 2
            fo = G[:, :, 0, :].rearrange("p j c -> p c j")
            ke = G[:, CH - 1, 1:CH + 1, :].rearrange("p j c -> p c j")
            for d in range(HD):
                qd = Q[:, d, :].rearrange("p (c j) -> p c j", j=CH)
                dve.tensor_tensor(qd, qd, fo, ALU.mult).then_inc(s["w_step"], 1)
                kd = K[:, d, :].rearrange("p (c j) -> p c j", j=CH)
                dve.tensor_tensor(kd, kd, ke, ALU.mult).then_inc(s["w_step"], 1)
            dve.wait_ge(s["w_step"], wn + 2 * HD)
            dve.wait_ge(s["u_pool"], 2 * (CH - 1))

            def reduce_out(r, a):
                c = 4 * r + a
                fo = pb_p[:, 2048 * (a % 2) + 1024:2048 * (a % 2) + 1536].rearrange("p (j v k) -> p j v k", v=HD, k=8)
                dve.tensor_reduce(O[:, :, bass.ds(CH * c, CH)].rearrange("p v j -> p j v"), fo, AX.X, ALU.add)\
                    .then_inc(s["o_red"], 1)

            def chain(r, a, first=False):
                c = 4 * r + a
                cs = bass.ds(CH * c, CH)
                n = 6 * c
                pu = pb_d[:, 0:512].rearrange("p (j v k) -> p j v k", v=HD, k=HD)
                if not first:
                    dve.wait_ge(s["chain"], n + 1)
                dve.tensor_tensor(pu, W[:, :, cs].rearrange("p k j -> p j k").unsqueeze(2)
                                  .broadcast_to([P, CH, HD, HD]),
                                  S[:, a, :, :].unsqueeze(1).broadcast_to([P, CH, HD, HD]), ALU.mult)\
                    .then_inc(s["chain"], 1)
                dve.wait_ge(s["chain"], n + 2)
                dve.tensor_reduce(uw[:, :, :], pu, AX.X, ALU.add).then_inc(s["chain"], 1)
                dve.wait_ge(s["chain"], n + 3)
                u = V[:, :, cs]
                dve.tensor_tensor(u, u, uw[:, :, :].rearrange("p j v -> p v j"), ALU.add).then_inc(s["chain"], 1)
                dve.wait_ge(s["chain"], n + 4)
                if not first:
                    dve.wait_ge(s["po_done"], c)
                ps = pb_d[:, 512:1024].rearrange("p (v k j) -> p v k j", k=HD, j=CH)
                dve.tensor_tensor(ps, K[:, :, cs].unsqueeze(1).broadcast_to([P, HD, HD, CH]),
                                  u.unsqueeze(2).broadcast_to([P, HD, HD, CH]), ALU.mult).then_inc(s["chain"], 1)
                if not first:
                    reduce_out(r if a else r - 1, a - 1 if a else 3)
                dve.wait_ge(s["chain"], n + 5)
                dve.tensor_reduce(sr[:, :, :], ps, AX.X, ALU.add).then_inc(s["chain"], 1)
                dve.wait_ge(s["chain"], n + 6)
                if not (isinstance(r, int) and 4 * r + a < 3):
                    dve.wait_ge(s["po_mul"], 2 * c - 5)
                b = (a + 1) % 4
                dve.scalar_tensor_tensor(S[:, b, :, :].rearrange("p v k -> p (v k)"),
                                         S[:, a, :, :].rearrange("p v k -> p (v k)"),
                                         G[:, CH - 1, 0, bass.ds(c, 1)], sr[:, :, :].rearrange("p v k -> p (v k)"),
                                         ALU.mult, ALU.add).then_inc(s["chain"], 1)

            dve.sem_inc(s["chain"], 1)
            chain(0, 0, first=True)
            for a in range(1, 4):
                chain(0, a)
            with dve.Fori(1, NCH // 4) as r:
                for a in range(4):
                    chain(r, a)
            dve.wait_ge(s["po_done"], NCH)
            reduce_out(NCH // 4 - 1, 3)

            dve.wait_ge(s["cw_in"], 144)
            dve.tensor_scalar(wo[:, :], wo[:, :], nw[:, 0:1], None, ALU.mult).then_inc(s["wo_step"], 1)
            dve.wait_ge(s["cs_ps"], 1)
            dve.tensor_copy(wcol[:, :], c0[:, 0:C]).then_inc(s["wo_step"], 1)
            dve.wait_ge(s["gate_sig"], 1)
            dve.wait_ge(s["wo_step"], 2)

            def gated(b):
                dve.wait_ge(o_in[b % 3], 16 * (b // 3 + 1))
                dve.tensor_tensor(og[:, b % 3, :], og[:, b % 3, :], gate[:, b, :], ALU.mult)\
                    .then_inc(s["og_done"], 1)

            gated(0)
            gated(1)
            for b in range(B):
                tp, yp = ((c1, c2), (c3, c4))[b % 2]
                n = 7 * b
                dve.wait_ge(s["oy_ps"], b + 1)
                for i in range(TT):
                    ins = dve.bn_stats(ost[:, i, :], tp[:, P * i:P * i + P])
                ins.then_inc(s["stat_done"], 1)
                dve.wait_ge(s["stat_done"], 2 * NT + 2 * b + 1)
                for i in range(TT):
                    ins = dve.bn_aggr(omv[:, i, :], ost[:, i, :])
                ins.then_inc(s["stat_done"], 1)
                dve.wait_ge(s["stat_done"], 2 * NT + 2 * b + 2)
                dve.tensor_scalar(ors[:, 0, :], omv[:, :, 1], EPS_LN, None, ALU.add).then_inc(s["ost_step"], 1)
                dve.tensor_scalar(ors[:, 3, :], omv[:, :, 0], -1.0, None, ALU.mult).then_inc(s["ost_step"], 1)
                if b + 2 < B:
                    gated(b + 2)
                dve.wait_ge(s["ost_step"], n + 2)
                for i in range(TT):
                    y = pb_d[:, P * i:P * i + P]
                    ins = dve.scalar_tensor_tensor(y, wcol[:, :], ors[:, 3, i:i + 1], yp[:, P * i:P * i + P],
                                                   ALU.mult, ALU.add)
                ins.then_inc(s["ost_step"], 1)
                dve.wait_ge(s["o_sqrt"], b + 1)
                dve.reciprocal(ors[:, 2, :], ors[:, 1, :]).then_inc(s["ost_step"], 1)
                dve.wait_ge(s["ost_step"], n + 4)
                for i in range(TT):
                    j = TT * b + i
                    ins = dve.scalar_tensor_tensor(x[:, j, :], pb_d[:, P * i:P * i + P], ors[:, 2, i:i + 1],
                                                   x[:, j, :], ALU.mult, ALU.add)
                ins.then_inc(s["ost_done"], 1)
                for _ in range(3):
                    dve.sem_inc(s["ost_step"], 1)

        @block.tensor
        def _(pe):
            pe.wait_ge(s["c_consts"], 1)
            pe.wait_ge(s["cw_in"], 144)
            for b in range(B):
                pe.wait_ge(s["cn_done"], TT * b + TT)
                pe.wait_ge(s["cT_sb"], b)
                for i in range(TT):
                    ins = pe.transpose(c0[:, P * i:P * i + P], cn[:, b % 2, i, :], ident[:, :])
                ins.then_inc(s["cT_ps"], 1)
                pe.wait_ge(s["cT_sb"], b + 1)
                for i in range(3):
                    pe.wait_ge(s["cq_sb"], 3 * (b - 1) + i + 1) if b else None
                    pe.matmul(cqkv[i][:, :], wqkv[:, i, :], cT[:, :], start=True, stop=True).then_inc(s["cq_ps"], 1)
                pe.wait_ge(s["cf_sb"], b)
                pe.matmul(c4[0:2 * H, :], wfg[:, :], cT[:, :], start=True, stop=True).then_inc(s["cf_ps"], 1)
                pe.wait_ge(s["cg1_sb"], b)
                pe.matmul(c5[0:HD, :], wg1[:, :], cT[:, :], start=True, stop=True).then_inc(s["cg1_ps"], 1)
                pe.wait_ge(s["cg1_sb"], b + 1)
                pe.wait_ge(s["cg2_sb"], b)
                pe.matmul(c6[:, :], wg2[:, :], red1[:, :], start=True, stop=True).then_inc(s["cg2_ps"], 1)
            pe.wait_ge(s["wo_step"], 1)
            pe.matmul(c0[:, 0:C], ones[:, :], wo[:, :], start=True, stop=True).then_inc(s["cs_ps"], 1)
            for b in range(B):
                tp, yp = ((c1, c2), (c3, c4))[b % 2]
                pe.wait_ge(s["og_done"], b + 1)
                if b >= 2:
                    pe.wait_ge(s["ost_done"], b - 1)
                for i in range(TT):
                    pe.transpose(tp[:, P * i:P * i + P], og[:, b % 3, P * i:P * i + P], ident[:, :])
                for i in range(TT):
                    ins = pe.matmul(yp[:, P * i:P * i + P], og[:, b % 3, P * i:P * i + P], wo[:, :],
                                    start=True, stop=True)
                ins.then_inc(s["oy_ps"], 1)


def build(nc, xin, W, Wq, Wk, Wv, Wgamma, Wf, Wg1, Wg2, Wo, norm_w, w_red, wg, w1, b1, w2, b2, out):
    with ExitStack() as ctx:
        def sb(name, shape, dt=F32):
            return ctx.enter_context(nc.sbuf_tensor(name, shape, dt))

        def sem(name):
            return ctx.enter_context(nc.semaphore(name))

        xs_dram = nc.dram_tensor("xs_dram", [NS * ST, C], F32, kind="Internal").ap()
        ys_dram = nc.dram_tensor("ys_dram", [NS * ST, C], F32, kind="Internal").ap()
        x = sb("x", [P, NT, C])
        s = {}
        for n in """f_consts fc_step ident_done stat_done rstd_step rstd_ready xnf_done
            rT_ps rT_sb red_ps red_sb lg_ps lg_step lg_exp lg_sum oh_done rank_ps pos_step pos_done texp_done
            zero_done scat_done x_ps x_sb h_ps h_sb y_ps y_sb o_ps o_sb add_done
            x_out fw_in wg_step wgT_ps wgT_sb""".split():
            s[n] = sem("f_" + n)
        xs_in, ws_in, ys_out, gat = ([sem(f"f_{n}{k}") for k in range(SLOTS)]
                                     for n in ("xs_in", "ws_in", "ys_out", "gat"))
        s["xs_in"], s["ws_in"], s["ys_out"], s["gat"] = xs_in, ws_in, ys_out, gat
        keep = {
            "ident": sb("ident", [P, P]),
            "before": sb("before", [P, P]),
            "ones": sb("ones", [P, P]),
            "zero": sb("zero", [P, 1024]),
            "pref": sb("pref", [P, E]),
            "restart_e": sb("restart_e", [P, E, NT]),
            "tile_at": sb("tile_at", [P, NS]),
            "k_at": sb("k_at", [P, NT * P // ST]),
            "wred_sb": sb("wred_sb", [P, GD]),
            "wgT_s": sb("wgT_s", [GD, E]),
            "b1T": sb("b1T", [P, E, NF]),
            "b2T": sb("b2T", [P, E]),
            "one8": sb("one8", [P, E]),
        }
        attention(nc, x, xin, W)
        experts(nc, x, xs_dram, ys_dram, s, keep, 0, w_red, wg, w1, b1, w2, b2, out)
        delta_rule(nc, x, Wq, Wk, Wv, Wgamma, Wf, Wg1, Wg2, Wo, norm_w)
        experts(nc, x, xs_dram, ys_dram, s, keep, 1, w_red, wg, w1, b1, w2, b2, out)


_INS = ["L0_attn_a_x", "L0_attn_a_W", "L0_attn_b_Wq", "L0_attn_b_Wk", "L0_attn_b_Wv", "L0_attn_b_Wgamma",
        "L0_attn_b_Wf", "L0_attn_b_Wg1", "L0_attn_b_Wg2", "L0_attn_b_Wo", "L0_attn_b_norm_w", "L0_ffn_w_red",
        "L0_ffn_wg", "L0_ffn_w1", "L0_ffn_b1", "L0_ffn_w2", "L0_ffn_b2"]


def kernel(**inputs):
    import numpy as _np
    import concourse.bacc as _bacc
    from concourse import mybir as _mybir
    from concourse.bass_utils import run_bass_kernel_spmd as _run

    nc = _bacc.Bacc("TRN2", target_bir_lowering=False, num_devices=1)
    arrays, args = {}, []
    for name in _INS:
        a = _np.ascontiguousarray(inputs[name])
        arrays[f"in_{name}_dram"] = a
        args.append(nc.dram_tensor(f"in_{name}_dram", a.shape, _mybir.dt.from_np(a.dtype), kind="ExternalInput").ap())
    out = nc.dram_tensor("out_0_dram", (B, T, C), F32, kind="ExternalOutput").ap()
    build(nc, *args, out)
    r = _run(nc, [arrays], core_ids=[0])
    return r.results[0]["out_0_dram"]
```

```python
from contextlib import ExitStack

import concourse.bass as bass
from concourse import mybir

F32 = mybir.dt.float32
BF16 = mybir.dt.bfloat16
I32 = mybir.dt.int32
ALU = mybir.AluOpType
ACT = mybir.ActivationFunctionType
AX = mybir.AxisListType
RMAX = bass.bass_isa.ReduceOp.max

P = 128
B, T, C = 8, 512, 128
H, HD = 16, 8
TT = T // P
NT = B * TT
EPS_LN = 1e-5

NP = H // 2
L = 64
NM = T // L
HU = NM + NM // 2
NU = 2 * HU
EPS_A = 1e-7
NPARTS = 8
Q_PART = [0, 0, 1, 1, 0, 2, 1, 2]
K_PART = [0, 1, 0, 1, 2, 0, 2, 1]
OFF_FIRST = [sum(NM - 1 - j for j in range(m)) for m in range(NM)]
N_OFF = NM * (NM - 1) // 2

E, F, GD = 8, 512, 16
NF = F // P
ST = 256
SLOTS = 4
NS = -(-((B * T + E * (ST - 1)) // ST) // SLOTS) * SLOTS
NR = NS // SLOTS
SPAN = SLOTS * ST
NC2 = ST // P
EPS_G = 1e-4

CH = 8
NCH = T // CH
EPS_K = 1e-12


def attention(nc, x, xin, W):
    with ExitStack() as ctx:
        def sb(name, shape, dt=F32):
            return ctx.enter_context(nc.sbuf_tensor("a_" + name, shape, dt))

        def psum(name, shape):
            return ctx.enter_context(nc.psum_tensor("a_" + name, shape, F32))

        def sem(name):
            return ctx.enter_context(nc.semaphore(name))

        scratch = nc.dram_tensor("parts_scratch", [2, 2, 3, P, T], BF16, kind="Internal").ap()

        wn = sb("wn", [P, 4, C])
        wT = sb("wT", [P, 3, C])
        wvg = sb("wvg", [P, 2, 72])
        wgT = sb("wgT", [P, H])
        sq = sb("sq", [P, C])
        wss = sb("wss", [P, 2])
        wmx = sb("wmx", [P, 2])
        guard = sb("guard", [P, 4])
        eps_a = sb("eps_a", [P, 1])
        ident = sb("ident", [P, P])
        ident_b = sb("ident_b", [P, P], BF16)
        upto = sb("upto", [P, P])
        after = sb("after", [P, P])
        same = sb("same", [P, P])
        tri = sb("tri", [P, L])
        never = sb("never", [P, L], BF16)
        restart = sb("restart", [P, NP, NM])
        zeros = sb("zeros", [P, 18])
        stats = sb("stats", [P, NT, 6])
        mv = sb("mv", [P, NT, 2])
        rstd = sb("rstd", [P, 4, NT])
        xn = sb("xn", [P, TT, C])
        xnT = sb("xnT", [P, T])
        parts = sb("parts", [P, 2, 3, T], BF16)
        rest = sb("rest", [P, 2, T])
        qf = sb("qf", [P, 2, NP, T], BF16)
        kc = sb("kc", [P, NP, T], BF16)
        kf = sb("kf", [P, 2, NP, NM, 2, L], BF16)
        vd = sb("vd", [P, 2, NM, NP, 18])
        vo = sb("vo", [P, N_OFF, NP, 18])
        gates = sb("gates", [P, P])
        g_low = sb("g_low", [P, P])
        g_abs = sb("g_abs", [P, P])
        logg = sb("logg", [P, P])
        g_cum = sb("g_cum", [P, P])
        b_tot = sb("b_tot", [P, NP, NM])
        b_cum = sb("b_cum", [P, NP, NM])
        tail = sb("tail", [P, NP, NM])
        reach = sb("reach", [P, NP, NM, NM])
        e_tok = sb("e_tok", [P, 2, TT * H])
        ramp = sb("ramp", [P, 2, NP, L])
        decay = sb("decay", [P, 2, NM, NP, L])
        mag = sb("mag", [P, 3, 2 * T])
        pw = sb("pw", [P, 4, 2 * T])
        off_sb = sb("off_sb", [P, 2, T])
        dia_sb = sb("dia_sb", [P, 2, T])
        acc = sb("acc", [P, TT * 4, 2, 9])
        rnorm = sb("rnorm", [P, TT * 4, 2])
        y = sb("y", [P, TT * 4, 2, HD])

        pS = psum("pS", [P, 4, T])
        pOff = psum("pOff", [P, T])
        pDia = psum("pDia", [P, T])
        M0 = psum("M0", [P, T])
        M1 = psum("M1", [P, T])

        names = """x_in w_in consts guard_step w_scaled w_T w_sb stat_done rstd_step rstd_ready
        xn_done xnT_ps xnT_sb qk_ps split_hi split_rest split_mid split_lo parts_out feat_q feat_k
        v_ps v_sb gate_sb tok_ps g_step logg_done cum_ps cum_sb reach_step reach_exp vo_done ramp_done decay_ps decay_sb
        s_ps mag_done sq_done pdg_done pv_done off_done dia_done fin_ps fin_step
        c_step vd_zero kx_done kf_zero w_misc""".split()
        s = {n: sem("a_" + n) for n in names}
        block = ctx.enter_context(nc.Block())

        def vo_at(j, i):
            return OFF_FIRST[j] + i - j - 1

        def width(m):
            return T - L * m

        def unit(n):
            hf, r = divmod(n, HU)
            if r < NM:
                return hf, r // 2, (2 * (r % 2), 2 * (r % 2) + 1)
            return hf, r - NM // 2, (0, 1, 2, 3)

        def last_unit(m):
            return 2 * m + 1 if m < NM // 2 else m + NM // 2

        def pairs_of(hf, qs):
            return slice(2 * qs[0] + hf, 2 * qs[-1] + hf + 1, 2)

        AHEAD_S, AHEAD_MAG, AHEAD_PW = 2, 3, 4
        TURN, QK, VALUES, SUMS, DECAY, EXPAND = 3, 5, 9, 15, 16, 21
        FIN = (1, 12)

        @block.sync
        def _(sp):
            for k in range(B):
                sp.dma_start(x[:, TT * k:TT * (k + 1), :],
                             xin[k].rearrange("(i p) c -> p i c", p=P)).then_inc(s["x_in"], 16)

            def features(bb, k):
                sp.wait_ge(s["split_hi"], 2 * bb + 2)
                sp.wait_ge(s["split_mid"], 2 * bb + 2)
                sp.wait_ge(s["split_lo"], 2 * bb + 2)
                for t in range(2):
                    for c in range(3):
                        sp.dma_start(scratch[k, t, c], parts[:, t, c, :]).then_inc(s["parts_out"], 16)
                sp.wait_ge(s["parts_out"], 96 * bb + 96)
                sp.wait_ge(s["kx_done"], 2 * bb)
                for par in range(2):
                    for c in range(NPARTS):
                        row = 64 * par + HD * c
                        src = [scratch[k, t, part].rearrange("(p x d) t -> x d p t", x=2, d=HD)[par]
                               for t, part in ((0, Q_PART[c]), (1, K_PART[c]))]
                        sp.dma_start(qf[row:row + HD, k, :, :], src[0]).then_inc(s["feat_q"], 16)
                        sp.dma_start(kc[row:row + HD, :, :], src[1]).then_inc(s["feat_k"], 16)

            features(0, 0)

            def batch(b, k, last=False):
                if not last:
                    sp.wait_ge(s["s_ps"], NU * b)
                    features(b + 1, 1 - k)

            batch(0, 0)
            with sp.Fori(1, B - 2, 2) as b:
                batch(b, 1)
                batch(b + 1, 0)

        @block.gpsimd
        def _(pool):
            st = 0

            def step(ins):
                nonlocal st
                st += 1
                ins.then_inc(s["c_step"], 1)
                pool.wait_ge(s["c_step"], st)

            for t, val in ((ident, 0.0), (ident_b, 0.0), (upto, 0.0), (after, 0.0), (same, 0.0), (tri, 1.0),
                           (never, 0.0), (zeros, 0.0)):
                step(pool.memset(t[:, :], val))
            step(pool.memset(restart[:, :, :], 1.0))
            pool.wait_ge(s["c_step"], st)
            step(pool.memset(restart[:, :, 0:1], 0.0))
            for t in (ident, ident_b):
                step(pool.affine_select(out=t[:, :], in_=t[:, :], compare_op=ALU.not_equal, fill=1.0,
                                        base=0, pattern=[[-1, P]], channel_multiplier=1))
            for h in range(2):
                for t in (upto, after, same):
                    step(pool.memset(t[L * h:L * h + L, L * h:L * h + L], 1.0))
            pool.wait_ge(s["c_step"], st)
            for h in range(2):
                lo, hi = L * h, L * h + L
                step(pool.affine_select(out=upto[lo:hi, lo:hi], in_=upto[lo:hi, lo:hi], compare_op=ALU.is_ge,
                                        fill=0.0, base=0, pattern=[[1, L]], channel_multiplier=-1))
                step(pool.affine_select(out=after[lo:hi, lo:hi], in_=after[lo:hi, lo:hi], compare_op=ALU.is_ge,
                                        fill=0.0, base=-1, pattern=[[-1, L]], channel_multiplier=1))
                step(pool.affine_select(out=tri[lo:hi, :], in_=tri[lo:hi, :], compare_op=ALU.is_ge,
                                        fill=0.0, base=0, pattern=[[1, L]], channel_multiplier=-1))
                step(pool.affine_select(out=never[lo:hi, :], in_=never[lo:hi, :], compare_op=ALU.is_ge,
                                        fill=-1e30, base=0, pattern=[[1, L]], channel_multiplier=-1))
            pool.wait_ge(s["c_step"], st)
            pool.memset(guard[:, 3:4], 0.0).then_inc(s["consts"], 1)
            pool.wait_ge(s["guard_step"], 2)
            pool.partition_all_reduce(wmx[:, :], wss[:, :], P, RMAX).then_inc(s["guard_step"], 1)
            pool.wait_ge(s["guard_step"], 3)
            for k in range(2):
                pool.memset(kf[:, k, :, :, :, :].rearrange("p a m x t -> p (a m x t)").bitcast(F32), 0.0)\
                    .then_inc(s["kf_zero"], 1)

            def ramps(bb, m, first=False):
                pool.wait_ge(s["logg_done"], bb + 1)
                if not (first and m < 2):
                    pool.wait_ge(s["decay_ps"], NM * bb + m - 1)
                pool.tensor_tensor(ramp[:, m % 2, :, :],
                                   tri[:, :].unsqueeze(1).broadcast_to([P, NP, L]),
                                   logg[:, 0:64].rearrange("p (a m) -> p a m", m=NM)[:, :, m:m + 1]
                                   .broadcast_to([P, NP, L]), ALU.mult).then_inc(s["ramp_done"], 1)

            def values_off(bb, k, j, first=False):
                if first:
                    pool.wait_ge(s["vd_zero"], 2)
                if j == 0:
                    pool.wait_ge(s["reach_exp"], bb + 1)
                    pool.wait_ge(s["v_sb"], 4 * bb + 4)
                if not first:
                    pool.wait_ge(s["pv_done"], NU * (bb - 1) + HU + last_unit(j) + 1 + AHEAD_PW)
                n = NM - 1 - j
                pool.tensor_tensor(
                    vo[:, vo_at(j, j + 1):vo_at(j, j + 1) + n, :, :],
                    vd[:, k, j, :, :].unsqueeze(1).broadcast_to([P, n, NP, 18]),
                    reach[:, :, j, j:NM - 1].rearrange("p a i -> p i a").unsqueeze(3)
                    .broadcast_to([P, n, NP, 18]), ALU.mult).then_inc(s["vo_done"], 1)

            def diagonal(b, n, k):
                hf, m, qs = unit(n)
                sl = n % 4
                pool.wait_ge(s["sq_done"], NU * b + n + 1 + AHEAD_MAG)
                pool.wait_ge(s["decay_sb"], NM * b + m + 1)
                own = pw[:, sl, 0:len(qs) * width(m)].rearrange("p (l t) -> p l t", l=len(qs))[:, :, 0:L]
                pool.tensor_tensor(own, own, decay[:, k, m, pairs_of(hf, qs), :], ALU.mult)\
                    .then_inc(s["pdg_done"], 1)

            for m in range(NM):
                ramps(0, m, first=True)
            for j in range(NM - 1):
                values_off(0, 0, j, first=True)

            def batch(b, k, last=False):
                for n in range(NU):
                    diagonal(b, n, k)
                    if last:
                        continue
                    if DECAY - 1 <= n < DECAY - 1 + NM:
                        ramps(b + 1, n - DECAY + 1)
                    for j in range(NM - 1):
                        if n == max(HU + last_unit(j) + 1, SUMS + 3 + min(j, 4)):
                            values_off(b + 1, 1 - k, j)
            batch(0, 0)
            with pool.Fori(1, B - 2, 2) as b:
                batch(b, 1)
                batch(b + 1, 0)
            batch(B - 1, 1, last=True)

        @block.scalar
        def _(act):
            act.dma_start(wn[:, 0:3, :], W[0:3 * C, :].rearrange("(j p) c -> p j c", p=P)).then_inc(s["w_in"], 16)
            act.dma_start(wn[0:H, 3, :], W[3 * C:3 * C + H, :]).then_inc(s["w_in"], 16)
            act.wait_ge(s["w_in"], 32)
            act.activation(sq[:, :], wn[:, 0, :], ACT.Square, accum_out=wss[:, 0:1]).then_inc(s["guard_step"], 1)
            act.activation(dia_sb[:, 0, 0:C], wn[:, 1, :], ACT.Square, accum_out=wss[:, 1:2]).then_inc(s["guard_step"], 1)
            act.wait_ge(s["guard_step"], 7)
            act.activation(guard[:, 1:2], guard[:, 0:1], ACT.Sqrt).then_inc(s["guard_step"], 1)
            act.wait_ge(s["rstd_step"], 1)
            act.activation(rstd[:, 2, :], rstd[:, 1, :], ACT.Sqrt).then_inc(s["rstd_step"], 1)

            def turned(bb):
                act.wait_ge(s["xnT_ps"], bb + 1)
                act.wait_ge(s["v_ps"], bb)
                act.activation(xnT[:, :], M0[:, :], ACT.Copy).then_inc(s["xnT_sb"], 1)

            def split_high(bb, t):
                act.wait_ge(s["qk_ps"], 2 * bb + t + 1)
                act.wait_ge(s["parts_out"], 96 * bb)
                act.activation(parts[:, t, 0, :], (M0, M1)[t][:, :], ACT.Copy).then_inc(s["split_hi"], 1)

            def split_mid(bb, t):
                act.wait_ge(s["split_rest"], 2 * bb + t + 1)
                act.activation(parts[:, t, 1, :], rest[:, t, :], ACT.Copy).then_inc(s["split_mid"], 1)

            def values(bb, k, first=False):
                act.wait_ge(s["gate_sb"], 4 * bb + 3)
                if first:
                    act.wait_ge(s["vd_zero"], 2)
                else:
                    act.wait_ge(s["pv_done"], NU * (bb - 1) + AHEAD_PW)
                    act.wait_ge(s["vo_done"], 7 * (bb - 1))
                for q, M in enumerate((M0, M1)):
                    for par in range(2):
                        lo, hi = L * par, L * par + L
                        act.activation(
                            vd[lo:hi, k, 4 * q:4 * q + 4, :, 9 * par:9 * par + HD],
                            M[lo:hi, 0:288].rearrange("p (m c) -> p m c", c=72)[:, :, 0:64]
                            .rearrange("p m (a d) -> p m a d", d=HD), ACT.Copy).then_inc(s["v_sb"], 1)

            def gate_logs(bb):
                act.wait_ge(s["g_step"], 3 * bb + 1)
                act.activation(g_abs[:, :], g_abs[:, :], ACT.Exp).then_inc(s["g_step"], 1)
                act.wait_ge(s["g_step"], 3 * bb + 2)
                act.activation(g_abs[:, :], g_abs[:, :], ACT.Ln, bias=1.0).then_inc(s["g_step"], 1)

            def token_decay(bb, k):
                act.wait_ge(s["cum_sb"], 6 * bb + 2)
                if not isinstance(bb, int) or bb >= 2:
                    act.wait_ge(s["fin_step"], 10 * bb - 14)
                act.activation(e_tok[:, k, :], M0[:, 64:128], ACT.Exp).then_inc(s["tok_ps"], 1)

            def reaches(bb):
                act.wait_ge(s["reach_step"], bb + 1)
                act.activation(reach[:, :, :, :].rearrange("p a j i -> p (a j i)"),
                               reach[:, :, :, :].rearrange("p a j i -> p (a j i)"), ACT.Exp)\
                    .then_inc(s["reach_exp"], 1)

            def decays(bb, k, m, first=False):
                act.wait_ge(s["decay_ps"], NM * bb + m + 1)
                if not first and m == 0:
                    act.wait_ge(s["pdg_done"], NU * (bb - 1))
                act.activation(decay[:, k, m, :, :].rearrange("p a t -> p (a t)"), (M1, M0)[m % 2][:, :],
                               ACT.Exp).then_inc(s["decay_sb"], 1)

            def square(b, n):
                hf, m, qs = unit(n)
                N = len(qs) * width(m)
                act.wait_ge(s["mag_done"], NU * b + n + 1 + AHEAD_S)
                act.wait_ge(s["pv_done"], NU * b + n + 1)
                act.activation(pw[:, n % 4, 0:N], mag[:, n % 3, 0:N], ACT.Square, bias=eps_a[:, 0:1])\
                    .then_inc(s["sq_done"], 1)

            def off_copy(b, hf):
                act.wait_ge(s["pv_done"], NU * b + HU * (hf + 1) + AHEAD_PW)
                if not (isinstance(b, int) and b == 0):
                    act.wait_ge(s["fin_ps"], 2 * b - 1 + hf)
                act.activation(off_sb[:, hf, :], pOff[:, :], ACT.Copy).then_inc(s["off_done"], 1)

            def batch(b, k, first=False, last=False):
                for n in range(NU):
                    square(b, n)
                    if n == 1 and not first:
                        off_copy(b - 1, 1)
                    if n == HU + 1:
                        off_copy(b, 0)
                    if last:
                        continue
                    if n == TURN + 1:
                        turned(b + 1)
                    if n == QK + 1:
                        split_high(b + 1, 0)
                        split_high(b + 1, 1)
                    if n == QK + 3:
                        split_mid(b + 1, 0)
                        split_mid(b + 1, 1)
                    if n == VALUES + 2:
                        values(b + 1, 1 - k)
                    if n == VALUES + 3:
                        gate_logs(b + 1)
                    if n == SUMS + 1:
                        token_decay(b + 1, 1 - k)
                    if n == SUMS + 3:
                        reaches(b + 1)
                    if DECAY <= n < DECAY + NM:
                        decays(b + 1, 1 - k, n - DECAY)

            act.sem_inc(s["sq_done"], AHEAD_MAG)
            turned(0)
            split_high(0, 0)
            split_high(0, 1)
            split_mid(0, 0)
            split_mid(0, 1)
            values(0, 0, first=True)
            gate_logs(0)
            token_decay(0, 0)
            reaches(0)
            for m in range(NM):
                decays(0, 0, m, first=True)
            batch(0, 0, first=True)
            with act.Fori(1, B - 2, 2) as b:
                batch(b, 1)
                batch(b + 1, 0)
            batch(B - 1, 1, last=True)
            off_copy(B - 1, 1)

        @block.vector
        def _(dve):
            dve.sem_inc(s["mag_done"], AHEAD_S)
            dve.memset(vd[:, :, :, :, :].rearrange("p k m a c -> p (k m a c)"), 0.0).then_inc(s["w_misc"], 1)
            dve.memset(pOff[:, :], 0.0).then_inc(s["w_misc"], 1)
            dve.memset(pDia[:, :], 0.0).then_inc(s["w_misc"], 1)
            dve.wait_ge(s["w_misc"], 3)
            for par in range(2):
                lo, hi = L * par, L * par + L
                dve.memset(vd[lo:hi, :, :, :, 9 * par + HD:9 * par + HD + 1]
                           .rearrange("p k m a c -> p (k m a) c"), 1.0).then_inc(s["vd_zero"], 1)
            dve.wait_ge(s["guard_step"], 3)
            dve.tensor_scalar(wss[:, :], wmx[:, :], 1e-30, None, ALU.max).then_inc(s["guard_step"], 1)
            dve.wait_ge(s["guard_step"], 4)
            dve.reciprocal(wmx[:, :], wss[:, :]).then_inc(s["guard_step"], 1)
            dve.wait_ge(s["guard_step"], 5)
            dve.tensor_tensor(guard[:, 2:3], wmx[:, 0:1], wmx[:, 1:2], ALU.mult).then_inc(s["guard_step"], 1)
            dve.wait_ge(s["guard_step"], 6)
            dve.tensor_scalar(guard[:, 0:1], guard[:, 2:3], 1e30 / (HD * HD * C * C), 1.0, ALU.mult, ALU.min)\
                .then_inc(s["guard_step"], 1)
            dve.wait_ge(s["guard_step"], 8)
            dve.tensor_scalar(eps_a[:, :], guard[:, 1:2], EPS_A, None, ALU.mult).then_inc(s["w_scaled"], 1)
            dve.tensor_scalar(wn[:, 0, :], wn[:, 0, :], guard[:, 1:2], None, ALU.mult).then_inc(s["w_scaled"], 1)
            dve.wait_ge(s["w_T"], 1)
            dve.tensor_copy(wT[:, :, :].rearrange("p j o -> p (j o)"), M0[:, 0:384]).then_inc(s["w_sb"], 1)
            dve.tensor_copy(wgT[:, :], M0[:, 384:400]).then_inc(s["w_sb"], 1)
            for par in range(2):
                dve.tensor_copy(wvg[:, par, 0:64].rearrange("p (a d) -> p a d", d=HD),
                                M0[:, 256:384].rearrange("p (a x d) -> p x a d", x=2, d=HD)[:, par])\
                    .then_inc(s["w_sb"], 1)
                dve.tensor_copy(wvg[:, par, 64:72],
                                M0[:, 384:400].rearrange("p (a x) -> p x a", x=2)[:, par]).then_inc(s["w_sb"], 1)
            for k in range(B):
                dve.wait_ge(s["x_in"], 16 * B)
                for i in range(TT):
                    dve.bn_stats(stats[:, TT * k + i, :], x[:, TT * k + i, :]).then_inc(s["stat_done"], 1)
            for k in range(B):
                for i in range(TT):
                    dve.wait_ge(s["stat_done"], TT * k + i + 1)
                    dve.bn_aggr(mv[:, TT * k + i, :], stats[:, TT * k + i, :]).then_inc(s["stat_done"], 1)
            dve.wait_ge(s["stat_done"], 2 * NT)
            dve.tensor_scalar(rstd[:, 1, :], mv[:, :, 1], EPS_LN, None, ALU.add).then_inc(s["rstd_step"], 1)
            dve.wait_ge(s["rstd_step"], 2)
            dve.reciprocal(rstd[:, 3, :], rstd[:, 2, :]).then_inc(s["rstd_step"], 1)
            dve.wait_ge(s["rstd_step"], 3)
            dve.tensor_tensor(rstd[:, 2, :], rstd[:, 3, :], rstd[:, 3, :], ALU.mult).then_inc(s["rstd_step"], 1)
            dve.wait_ge(s["rstd_step"], 4)
            dve.tensor_tensor(rstd[:, 2, :], rstd[:, 2, :], rstd[:, 1, :], ALU.mult).then_inc(s["rstd_step"], 1)
            dve.wait_ge(s["rstd_step"], 5)
            dve.tensor_scalar(rstd[:, 2, :], rstd[:, 2, :], -0.5, 1.5, ALU.mult, ALU.add)\
                .then_inc(s["rstd_step"], 1)
            dve.wait_ge(s["rstd_step"], 6)
            dve.tensor_tensor(rstd[:, 0, :], rstd[:, 2, :], rstd[:, 3, :], ALU.mult).then_inc(s["rstd_ready"], 1)

            def normalize(bb, first=False):
                dve.wait_ge(s["rstd_ready"], 1)
                if not first:
                    dve.wait_ge(s["xnT_ps"], bb)
                for i in range(TT):
                    j = TT * bb + i
                    dve.tensor_scalar(xn[:, i, :], x[:, bass.ds(j, 1), :].rearrange("p a c -> p (a c)"),
                                       mv[:, bass.ds(j, 1), 0:1].rearrange("p a c -> p (a c)"),
                                       rstd[:, 0, bass.ds(j, 1)], ALU.subtract, ALU.mult).then_inc(s["xn_done"], 1)

            def split_rest(bb, t, first=False):
                dve.wait_ge(s["split_hi"], 2 * bb + t + 1)
                if not first:
                    dve.wait_ge(s["split_mid"], 2 * (bb - 1) + t + 1)
                dve.tensor_tensor(rest[:, t, :], (M0, M1)[t][:, :], parts[:, t, 0, :], ALU.subtract)\
                    .then_inc(s["split_rest"], 1)

            def split_low(bb, t):
                dve.wait_ge(s["split_mid"], 2 * bb + t + 1)
                dve.wait_ge(s["parts_out"], 96 * bb)
                dve.tensor_tensor(parts[:, t, 2, :], rest[:, t, :], parts[:, t, 1, :], ALU.subtract)\
                    .then_inc(s["split_lo"], 1)

            def gate_prep(bb):
                dve.wait_ge(s["v_ps"], bb + 1)
                for q, M in enumerate((M0, M1)):
                    dve.tensor_copy(gates[:, 0:64].rearrange("p (a m) -> p m a", m=NM)[:, 4 * q:4 * q + 4, :],
                                    M[:, 0:288].rearrange("p (m c) -> p m c", c=72)[:, :, 64:72])\
                        .then_inc(s["gate_sb"], 1)
                dve.tensor_copy(gates[:, 64:128], M0[:, 288:352]).then_inc(s["gate_sb"], 1)
                dve.wait_ge(s["gate_sb"], 4 * bb + 3)
                dve.tensor_scalar(g_low[:, :], gates[:, :], 0.0, None, ALU.min).then_inc(s["gate_sb"], 1)
                dve.wait_ge(s["gate_sb"], 4 * bb + 4)
                dve.scalar_tensor_tensor(g_abs[:, :], g_low[:, :], 2.0, gates[:, :], ALU.mult, ALU.subtract)\
                    .then_inc(s["g_step"], 1)

            def gate_log(bb):
                dve.wait_ge(s["g_step"], 3 * bb + 3)
                dve.wait_ge(s["ramp_done"], NM * bb)
                dve.tensor_tensor(logg[:, :], g_low[:, :], g_abs[:, :], ALU.subtract).then_inc(s["logg_done"], 1)

            def sums(bb):
                dve.wait_ge(s["cum_ps"], bb + 1)
                dve.tensor_copy(b_tot[:, :, :].rearrange("p a m -> p (a m)"), M0[:, 128:192])\
                    .then_inc(s["cum_sb"], 1)
                dve.wait_ge(s["cum_sb"], 6 * bb + 1)
                dve.tensor_tensor(tail[:, :, :].rearrange("p a m -> p (a m)"),
                                  b_tot[:, :, :].rearrange("p a m -> p (a m)"), M0[:, 0:64], ALU.subtract)\
                    .then_inc(s["cum_sb"], 1)
                dve.tensor_tensor_scan(b_cum[:, :, :].rearrange("p a m -> p (a m)"),
                                       restart[:, :, :].rearrange("p a m -> p (a m)"),
                                       b_tot[:, :, :].rearrange("p a m -> p (a m)"), 0.0, ALU.mult, ALU.add)\
                    .then_inc(s["cum_sb"], 1)

            def reach_sums(bb):
                dve.wait_ge(s["cum_sb"], 6 * bb + 3)
                dve.tensor_tensor(tail[:, :, :], tail[:, :, :], b_cum[:, :, :], ALU.subtract)\
                    .then_inc(s["cum_sb"], 1)
                dve.wait_ge(s["cum_sb"], 6 * bb + 4)
                dve.wait_ge(s["vo_done"], 7 * bb)
                dve.tensor_tensor(reach[:, :, :, :], b_cum[:, :, :].unsqueeze(2).broadcast_to([P, NP, NM, NM]),
                                  tail[:, :, :].unsqueeze(3).broadcast_to([P, NP, NM, NM]), ALU.add)\
                    .then_inc(s["cum_sb"], 1)

            def reach_bound(bb):
                dve.wait_ge(s["cum_sb"], 6 * bb + 5)
                dve.tensor_scalar(reach[:, :, :, :].rearrange("p a j i -> p (a j i)"),
                                  reach[:, :, :, :].rearrange("p a j i -> p (a j i)"), 0.0, None, ALU.min)\
                    .then_inc(s["cum_sb"], 1)
                dve.wait_ge(s["cum_sb"], 6 * bb + 6)
                dve.sem_inc(s["reach_step"], 1)

            def expand(bb, k, first=False):
                dve.wait_ge(s["feat_k"], 256 * bb + 256)
                if first:
                    dve.wait_ge(s["kf_zero"], 2)
                else:
                    dve.wait_ge(s["s_ps"], NU * (bb - 1))
                for par in range(2):
                    lo, hi = L * par, L * par + L
                    dve.tensor_copy(kf[lo:hi, k, :, :, par, :].rearrange("p a m t -> p (a m) t"),
                                    kc[lo:hi, :, :].rearrange("p a (m t) -> p (a m) t", t=L))\
                        .then_inc(s["kx_done"], 1)

            def magnitude(b, n):
                hf, m, qs = unit(n)
                N = len(qs) // 2 * width(m)
                dve.wait_ge(s["s_ps"], NU * b + n + 1)
                dve.wait_ge(s["sq_done"], NU * b + n + 1)
                dve.tensor_scalar(mag[:, n % 3, 0:2 * N].bitcast(I32).rearrange("p (l t) -> p l t", l=2),
                                  pS[:, 2 * (n % 2):2 * (n % 2) + 2, 0:N].bitcast(I32),
                                  0x7fffffff, None, ALU.bitwise_and).then_inc(s["mag_done"], 1)

            def dia_copy(b, hf):
                dve.wait_ge(s["pv_done"], NU * b + HU * (hf + 1) + AHEAD_PW)
                if not (isinstance(b, int) and b == 0):
                    dve.wait_ge(s["fin_ps"], 2 * b - 1 + hf)
                dve.tensor_copy(dia_sb[:, hf, :], pDia[:, :]).then_inc(s["dia_done"], 1)

            def finish(b, k, hf, part):
                step = 5 * (2 * b + hf)
                if part or hf or not isinstance(b, int) or b:
                    dve.wait_ge(s["fin_step"], step + part)
                if part == 0:
                    dve.wait_ge(s["fin_ps"], 2 * b + hf + 1)
                    dve.wait_ge(s["tok_ps"], b + 1)
                if part < 2:
                    view = (M0, M1)[part][:, :].rearrange("p (a c) -> p a c", c=32)[:, :, 0:18]\
                        .rearrange("p a (x d) -> p a x d", x=2)
                if part == 0:
                    et = e_tok[:, k, :].rearrange("p (a x) -> p a x", x=4)[:, :, 2 * hf:2 * hf + 2].unsqueeze(3)\
                        .broadcast_to([P, 16, 2, 9])
                    dve.tensor_tensor(acc[:, :, :, :], view, et, ALU.mult).then_inc(s["fin_step"], 1)
                if part == 1:
                    dve.tensor_tensor(acc[:, :, :, :], view, acc[:, :, :, :], ALU.add).then_inc(s["fin_step"], 1)
                if part == 2:
                    dve.reciprocal(rnorm[:, :, :], acc[:, :, :, HD]).then_inc(s["fin_step"], 1)
                if part == 3:
                    dve.tensor_tensor(y[:, :, :, :], acc[:, :, :, 0:HD],
                                      rnorm[:, :, :].unsqueeze(3).broadcast_to([P, 16, 2, HD]), ALU.mult)\
                        .then_inc(s["fin_step"], 1)
                if part == 4:
                    xs = x[:, bass.ds(TT * b, TT), :].rearrange("p i (a c) -> p (i a) c", c=32)[:, :, 16 * hf:16 * hf + 16]
                    dve.tensor_tensor(xs, xs, y[:, :, :, :].rearrange("p a x d -> p a (x d)"), ALU.add)\
                        .then_inc(s["fin_step"], 1)

            normalize(0, first=True)
            split_rest(0, 0, first=True)
            split_rest(0, 1, first=True)
            split_low(0, 0)
            split_low(0, 1)
            gate_prep(0)
            gate_log(0)
            sums(0)
            reach_sums(0)
            reach_bound(0)
            expand(0, 0, first=True)
            magnitude(0, 0)
            magnitude(0, 1)

            def batch(b, k, first=False, last=False):
                for n in range(NU):
                    if n + 2 < NU:
                        magnitude(b, n + 2)
                    elif not last:
                        magnitude(b + 1, n + 2 - NU)
                    if n == 0 and not first:
                        dia_copy(b - 1, 1)
                    if n == HU:
                        dia_copy(b, 0)
                    for hf in range(2):
                        if FIN[hf] <= n < FIN[hf] + 5 and not first:
                            finish(b - 1, 1 - k, hf, n - FIN[hf])
                    if last:
                        continue
                    if n == TURN - 3:
                        normalize(b + 1)
                    if n == QK + 2:
                        split_rest(b + 1, 0)
                        split_rest(b + 1, 1)
                    if n == QK + 4:
                        split_low(b + 1, 0)
                        split_low(b + 1, 1)
                    if n == VALUES + 2:
                        gate_prep(b + 1)
                    if n == VALUES + 4:
                        gate_log(b + 1)
                    if n == SUMS:
                        sums(b + 1)
                    if n == SUMS + 1:
                        reach_sums(b + 1)
                    if n == SUMS + 2:
                        reach_bound(b + 1)
                    if n == EXPAND:
                        expand(b + 1, 1 - k)

            batch(0, 0, first=True)
            with dve.Fori(1, B - 2, 2) as b:
                batch(b, 1)
                batch(b + 1, 0)
            batch(B - 1, 1, last=True)
            dia_copy(B - 1, 1)
            for hf in range(2):
                for part in range(5):
                    finish(B - 1, 1, hf, part)
            dve.wait_ge(s["fin_step"], 10 * B)

        @block.tensor
        def _(pe):
            pe.sem_inc(s["pv_done"], AHEAD_PW)
            pe.wait_ge(s["consts"], 1)
            pe.wait_ge(s["w_scaled"], 2)
            for j in range(3):
                pe.transpose(M0[:, P * j:P * j + P], wn[:, j, :], ident[:, :])
            pe.transpose(M0[:, 384:400], wn[0:H, 3, :], ident[0:H, 0:H]).then_inc(s["w_T"], 1)
            pe.wait_ge(s["w_sb"], 6)

            def turn(bb, first=False):
                pe.wait_ge(s["xn_done"], TT * bb + TT)
                if not first:
                    pe.wait_ge(s["decay_sb"], NM * bb)
                if not isinstance(bb, int) or bb >= 2:
                    pe.wait_ge(s["fin_step"], 10 * bb - 18)
                for i in range(TT):
                    ins = pe.transpose(M0[:, P * i:P * i + P], xn[:, i, :], ident[:, :])
                ins.then_inc(s["xnT_ps"], 1)

            def project(bb):
                pe.wait_ge(s["xnT_sb"], bb + 1)
                for t, M in enumerate((M0, M1)):
                    pe.matmul(M[:, :], wT[:, t, :], xnT[:, :], start=True, stop=True).then_inc(s["qk_ps"], 1)

            def values(bb):
                pe.wait_ge(s["split_hi"], 2 * bb + 2)
                pe.wait_ge(s["split_rest"], 2 * bb + 2)
                for m in range(NM // 2):
                    value(m)

            def value(m):
                for par in range(2):
                    pe.matmul((M0, M1)[m // 4][L * par:L * par + L, 72 * (m % 4):72 * (m % 4) + 72],
                              xnT[:, L * m:L * m + L], wvg[:, par, :], start=True, stop=True)

            def values_late():
                for m in range(NM // 2, NM):
                    value(m)
                for i in range(TT):
                    ins = pe.matmul(M0[:, 288 + H * i:288 + H * i + H], xnT[:, P * i:P * i + P], wgT[:, :],
                                    start=True, stop=True)
                ins.then_inc(s["v_ps"], 1)

            def sums(bb):
                pe.wait_ge(s["logg_done"], bb + 1)
                pe.wait_ge(s["v_sb"], 4 * bb + 4)
                if not isinstance(bb, int) or bb >= 2:
                    pe.wait_ge(s["fin_step"], 10 * bb - 13)
                pe.matmul(M0[:, 0:128], upto[:, :], logg[:, :], start=True, stop=True)
                pe.matmul(M0[:, 128:192], same[:, :], logg[:, 0:64], start=True, stop=True)\
                    .then_inc(s["cum_ps"], 1)

            def decay_sums(bb, m):
                pe.wait_ge(s["ramp_done"], NM * bb + m + 1)
                if m >= 2:
                    pe.wait_ge(s["decay_sb"], NM * bb + m - 1)
                if m == 1:
                    pe.wait_ge(s["cum_sb"], 6 * bb + 2)
                    pe.wait_ge(s["tok_ps"], bb + 1)
                M = (M1, M0)[m % 2]
                pe.matmul(M[:, :], after[:, :], ramp[:, m % 2, :, :].rearrange("p a t -> p (a t)"),
                          start=True, stop=False)
                pe.matmul(M[:, :].rearrange("p (a t) -> p a t", t=L), ident_b[:, :],
                          never[:, :].unsqueeze(1).broadcast_to([P, NP, L]), start=False, stop=True)\
                    .then_inc(s["decay_ps"], 1)

            def scores(b, k, n):
                hf, m, qs = unit(n)
                if n == 0:
                    pe.wait_ge(s["feat_q"], 256 * b + 256)
                    pe.wait_ge(s["kx_done"], 2 * b + 2)
                pe.wait_ge(s["mag_done"], NU * b + n + 1)
                for l, Q in enumerate(qs):
                    p = 2 * Q + hf
                    half = len(qs) // 2
                    at = width(m) * (l % half)
                    ins = pe.matmul(pS[:, 2 * (n % 2) + l // half, at:at + width(m)], kf[:, k, p, m, :, :].rearrange("p x t -> p (x t)"),
                                    qf[:, k, p, L * m:T], start=True, stop=True)
                ins.then_inc(s["s_ps"], 1)

            def attend(b, k, n):
                hf, m, qs = unit(n)
                if n % HU == 0:
                    pe.wait_ge(s["off_done"], 2 * b + hf)
                    pe.wait_ge(s["dia_done"], 2 * b + hf)
                if n == 0:
                    pe.wait_ge(s["w_misc"], 3)
                pe.wait_ge(s["pdg_done"], NU * b + n + 1)
                if hf == 0 and qs[0] == 0 and m < NM - 1:
                    pe.wait_ge(s["vo_done"], 7 * b + m + 1)
                w = pw[:, n % 4, 0:len(qs) * width(m)].rearrange("p (l t) -> p l t", l=len(qs))
                for i in range(m, NM):
                    for l, Q in enumerate(qs):
                        p = 2 * Q + hf
                        lo, hi = 32 * Q, 32 * Q + 18
                        wi = w[:, l, L * (i - m):L * (i - m) + L]
                        if i == m:
                            if m == 0:
                                pe.matmul(pOff[lo:hi, 0:L], zeros[:, :], wi, start=True, stop=False,
                                          skip_group_check=True)
                            ins = pe.matmul(pDia[lo:hi, L * m:L * m + L], vd[:, k, m, p, :], wi,
                                            start=(m == 0), stop=(m == NM - 1), skip_group_check=True)
                        else:
                            ins = pe.matmul(pOff[lo:hi, L * i:L * i + L], vo[:, vo_at(m, i), p, :], wi,
                                            start=False, stop=(m == NM - 2), skip_group_check=True)
                ins.then_inc(s["pv_done"], 1)

            def turn_back(b, hf, last=False):
                pe.wait_ge(s["off_done"], 2 * b + hf + 1)
                pe.wait_ge(s["dia_done"], 2 * b + hf + 1)
                if last:
                    pe.wait_ge(s["fin_step"], 10 * b + 5 * hf - 3)
                elif hf == 0:
                    pe.wait_ge(s["decay_sb"], NM * (b + 2))
                elif not isinstance(b, int) or b < B - 2:
                    pe.wait_ge(s["v_sb"], 4 * (b + 3))
                    pe.wait_ge(s["gate_sb"], 4 * (b + 2) + 3)
                else:
                    pe.wait_ge(s["fin_step"], 10 * b + 2)
                for src, M in ((off_sb, M0), (dia_sb, M1)):
                    for i in range(TT):
                        ins = pe.transpose(M[:, P * i:P * i + P], src[:, hf, P * i:P * i + P], ident[:, :])
                ins.then_inc(s["fin_ps"], 1)

            turn(0, first=True)
            project(0)
            values(0)
            values_late()
            sums(0)
            for m in range(NM):
                decay_sums(0, m)
            scores(0, 0, 0)
            scores(0, 0, 1)

            def batch(b, k, first=False, last=False):
                for n in range(NU):
                    for hf in range(2):
                        if n == FIN[hf] and not first:
                            turn_back(b - 1, hf)
                    if not last:
                        if n == TURN:
                            turn(b + 1)
                        if n == QK:
                            project(b + 1)
                        if n == VALUES:
                            values(b + 1)
                        if n == VALUES + 1:
                            values_late()
                        if n == SUMS:
                            sums(b + 1)
                        if DECAY <= n < DECAY + NM:
                            decay_sums(b + 1, n - DECAY)
                    if n + 2 < NU:
                        scores(b, k, n + 2)
                    elif not last:
                        scores(b + 1, 1 - k, n + 2 - NU)
                    if n >= 1:
                        attend(b, k, n - 1)
                    elif not first:
                        attend(b - 1, 1 - k, NU - 1)

            batch(0, 0, first=True)
            with pe.Fori(1, B - 2, 2) as b:
                batch(b, 1)
                batch(b + 1, 0)
            batch(B - 1, 1, last=True)
            attend(B - 1, 1, NU - 1)
            turn_back(B - 1, 0, last=True)
            turn_back(B - 1, 1, last=True)


def experts(nc, x, xs_dram, ys_dram, s, keep, f, w_red, wg, w1, b1, w2, b2, out):
    with ExitStack() as ctx:
        def sb(name, shape, dt=F32):
            return ctx.enter_context(nc.sbuf_tensor(f"f{f}_" + name, shape, dt))

        def psum(name, shape):
            return ctx.enter_context(nc.psum_tensor(f"f{f}_" + name, shape, F32))

        def sem(name):
            return ctx.enter_context(nc.semaphore(name))

        xs_in, ws_in, ys_out, row_in = s["xs_in"], s["ws_in"], s["ys_out"], s["row_in"]

        def before_slot(r, q, n=1):
            return r + (q - n) // SLOTS, (q - n) % SLOTS

        ident = keep["ident"]
        before = keep["before"]
        ones = keep["ones"]
        blank = keep["blank"]
        pref = keep["pref"]
        restart_e = keep["restart_e"]
        tile_at = keep["tile_at"]
        k_at = keep["k_at"]
        stats = sb("stats", [P, NT, 6])
        mv = sb("mv", [P, NT, 2])
        rstd = sb("rstd", [P, 4, NT])
        xa = sb("xa", [P, NT, C + 1])
        rT = sb("rT", [P, 2, T])
        lgT = sb("lgT", [P, 2, T])
        wred_sb = keep["wred_sb"]
        wg_sb = sb("wg_sb", [E, GD])
        wg_sq = sb("wg_sq", [E, GD])
        wg_n = sb("wg_n", [E, 4])
        wgT_s = keep["wgT_s"]
        wredT = sb("wredT", [GD, P])
        w_gate = keep["w_gate"]
        b_in = sb("b_in", [E * NF + E, P])
        b1T = keep["b1T"]
        b2T = keep["b2T"]
        lg = sb("lg", [P, NT, E])
        lgx = sb("lgx", [P, NT, E])
        hit = sb("hit", [P, NT, E])
        top = sb("top", [P, NT])
        first = sb("first", [P, NT])
        score = sb("score", [P, NT])
        lsum = sb("lsum", [P, NT])
        oh = sb("oh", [P, E, NT])
        tot = sb("tot", [P, E, NT])
        cinc = sb("cinc", [P, E, NT])
        p_at = sb("p_at", [P, E, NT])
        more = sb("more", [P, E, NT * P // ST])
        n_til = sb("n_til", [P, E])
        ends = sb("ends", [P, E])
        base = sb("base", [P, E])
        pos_f = sb("pos_f", [P, NT])
        pos = sb("pos", [P, NT], I32)
        past = sb("past", [P, NS, E])
        texp_f = sb("texp_f", [P, NS])
        texp = sb("texp", [P, NS], I32)
        one8 = keep["one8"]
        xs = sb("xs", [P, SLOTS, NC2, C + 1])
        who = sb("who", [P, SLOTS, NC2], I32)
        ya = sb("ya", [P, NT, C])
        w1s = sb("w1s", [P, SLOTS, F])
        w2s = sb("w2s", [P, SLOTS, NF, C])
        b1s = sb("b1s", [P, SLOTS, NF])
        b2s = sb("b2s", [P, SLOTS, 1])
        xsT = sb("xsT", [P, 2, ST])
        hs = sb("hs", [P, 2, NF, ST])
        ysT = sb("ysT", [P, 2, ST])
        yo = sb("yo", [P, SLOTS, NC2, C])
        bA = psum("bA", [P, T])
        bB = psum("bB", [P, T])
        bH = psum("bH", [P, 4, T])
        bY = psum("bY", [P, T])
        bO = psum("bO", [P, T])
        block = ctx.enter_context(nc.Block())

        @block.sync
        def _(sp):
            if f == 0:
                sp.dma_start(wred_sb[:, :], w_red).then_inc(s["fw_in"], 16)
                sp.dma_start(wg_sb[:, :], wg).then_inc(s["fw_in"], 16)
                sp.dma_start(b_in[0:E * NF, :], b1.rearrange("e (k p) -> (e k) p", p=P)).then_inc(s["fw_in"], 16)
                sp.dma_start(b_in[E * NF:E * NF + E, :], b2).then_inc(s["fw_in"], 16)
                sp.wait_ge(s["f_consts"], 1)
                for i in range(2):
                    for k in range(NR):
                        sp.dma_start(xs_dram[i][SPAN * k:SPAN * (k + 1), :].rearrange("(p a) c -> p (a c)", p=P),
                                     blank[:, :, :].rearrange("p a c -> p (a c)")).then_inc(s["zero_done"], 16)
                sp.wait_ge(s["wgT_sb"], 5)

            def ffn(f):
                sp.wait_ge(s["texp_done"], f + 1)
                sp.wait_ge(s["scat_done"], 16 * NT * (f + 1))

                def load(r, q):
                    j = SLOTS * r + q
                    g = NS * f + j
                    e = sp.value_load(texp[0:1, bass.ds(j, 1)], min_val=0, max_val=E - 1)
                    late = f > 0 or not isinstance(r, int) or r > 0
                    if late:
                        sp.wait_ge(s["x_ps"], g - SLOTS + 1)
                        sp.wait_ge(s["who_done"], g - SLOTS + 1)
                    sp.dma_start(xs[:, q, :, :], xs_dram[f][bass.ds(j * ST, ST), :]
                                 .rearrange("(a p) c -> p a c", p=P)).then_inc(xs_in[q], 16)
                    if late:
                        sp.wait_ge(s["h_sb"], g - SLOTS + 1)
                    sp.dma_start(w1s[:, q, :], w1[bass.ds(e, 1), :, :].rearrange("e p f -> p (e f)"))\
                        .then_inc(ws_in[q], 16)
                    sp.dma_start(b1s[:, q, :], b1T[:, bass.ds(e, 1), :].rearrange("p e k -> p (e k)"))\
                        .then_inc(ws_in[q], 16)
                    if late:
                        sp.wait_ge(s["y_sb"], g - SLOTS + 1)
                    sp.dma_start(w2s[:, q, :, :], w2[bass.ds(e, 1), :, :].rearrange("e (k p) d -> p (e k) d", p=P))\
                        .then_inc(ws_in[q], 16)
                    sp.dma_start(b2s[:, q, :], b2T[:, bass.ds(e, 1)]).then_inc(ws_in[q], 16)

                for q in range(SLOTS):
                    load(0, q)
                with sp.Fori(0, NR - 1) as r:
                    for q in range(SLOTS):
                        load(r + 1, q)
                for q in range(SLOTS):
                    sp.wait_ge(ys_out[q], 16 * NC2 * NR * (f + 1))
                for k in range(B):
                    sp.dma_start(ya[:, TT * k:TT * (k + 1), :],
                                 ys_dram[f][T * k:T * (k + 1), :].rearrange("(i p) c -> p i c", p=P))\
                        .then_inc(row_in[k], 16)

            ffn(f)
            if f == 1:
                for k in range(B):
                    sp.wait_ge(s["add_done"], NT + TT * (k + 1))
                    sp.dma_start(out[k].rearrange("(i p) c -> p i c", p=P),
                                 x[:, TT * k:TT * (k + 1), :]).then_inc(s["x_out"], 16)
                sp.wait_ge(s["x_out"], 16 * B)

        @block.gpsimd
        def _(pool):
            st = 0

            def step(ins):
                nonlocal st
                st += 1
                ins.then_inc(s["fc_step"], 1)
                pool.wait_ge(s["fc_step"], st)

            if f == 0:
                step(pool.memset(ident[:, :], 0.0))
                step(pool.memset(blank[:, :, :].rearrange("p a c -> p (a c)"), 0.0))
                step(pool.memset(before[:, :], 1.0))
                step(pool.memset(ones[:, :], 1.0))
                step(pool.memset(one8[:, :], 1.0))
                step(pool.memset(w_gate[:, :], 0.0))
                step(pool.memset(restart_e[:, :, :], 1.0))
                step(pool.memset(restart_e[:, :, 0:1], 0.0))
                step(pool.affine_select(out=ident[:, :], in_=ident[:, :], compare_op=ALU.not_equal, fill=1.0,
                                        base=0, pattern=[[-1, P]], channel_multiplier=1))
                step(pool.affine_select(out=before[:, :], in_=before[:, :], compare_op=ALU.is_ge, fill=0.0,
                                        base=-1, pattern=[[1, P]], channel_multiplier=-1))
                step(pool.iota(pref[:, :], [[-1, E]], base=E, channel_multiplier=0,
                               allow_small_or_imprecise_dtypes=True))
                step(pool.iota(tile_at[:, :], [[1, NS]], base=0, channel_multiplier=0,
                               allow_small_or_imprecise_dtypes=True))
                step(pool.iota(k_at[:, :], [[ST, NT * P // ST]], base=0, channel_multiplier=0,
                               allow_small_or_imprecise_dtypes=True))
                pool.iota(blank[:, :, C], [[1, SPAN // P]], base=B * T, channel_multiplier=SPAN // P,
                          allow_small_or_imprecise_dtypes=True).then_inc(s["f_consts"], 1)

            def ffn(f):
                pool.iota(xa[:, :, C], [[P, NT]], base=0, channel_multiplier=1,
                          allow_small_or_imprecise_dtypes=True).then_inc(s["id_done"], 1)
                pool.wait_ge(s["id_done"], f + 1)
                pool.wait_ge(s["zero_done"], 16 * 2 * NR)
                pool.wait_ge(s["pos_done"], f + 1)
                for i in range(NT):
                    pool.indirect_dma_start(xs_dram[f][:, :], bass.IndirectOffsetOnAxis(ap=pos[:, i:i + 1], axis=0),
                                            xa[:, i, :], None).then_inc(s["scat_done"], 16)

                def give_back(r, q):
                    pool.wait_ge(s["o_sb"], NS * f + SLOTS * r + q + 1)
                    pool.sem_inc(s["give"], 1)
                    for a in range(NC2):
                        pool.indirect_dma_start(ys_dram[f][:, :], bass.IndirectOffsetOnAxis(ap=who[:, q, a:a + 1], axis=0),
                                                yo[:, q, a, :], None).then_inc(ys_out[q], 16)

                with pool.Fori(0, NR) as r:
                    for q in range(SLOTS):
                        give_back(r, q)

            ffn(f)

        @block.scalar
        def _(act):
            if f == 0:
                act.wait_ge(s["wg_step"], 1)
                act.activation(wg_n[:, 1:2], wg_n[:, 0:1], ACT.Sqrt).then_inc(s["wg_step"], 1)

            def ffn(f):
                act.wait_ge(s["rstd_step"], 6 * f + 1)
                act.activation(rstd[:, 2, :], rstd[:, 1, :], ACT.Sqrt).then_inc(s["rstd_step"], 1)
                for g in range(B):
                    q = B * f + g
                    act.wait_ge(s["rT_ps"], q + 1)
                    if q >= 2:
                        act.wait_ge(s["lg_ps"], q - 1)
                    act.activation(rT[:, g % 2, :], (bA, bB)[g % 2][:, :], ACT.Copy).then_inc(s["rT_sb"], 1)
                act.wait_ge(s["lg_step"], 4 * f + 3)
                act.activation(lgx[:, :, :].rearrange("p i e -> p (i e)"),
                               lgx[:, :, :].rearrange("p i e -> p (i e)"), ACT.Exp).then_inc(s["lg_exp"], 1)

                def x_copy(r, q, late=True):
                    g = NS * f + SLOTS * r + q
                    act.wait_ge(s["x_ps"], g + 1)
                    if late:
                        act.wait_ge(s["h_ps"], g - 1)
                    act.activation(xsT[:, q % 2, :], bA[:, 0:ST], ACT.Copy).then_inc(s["x_sb"], 1)

                def gelu(r, q, late=True):
                    g = NS * f + SLOTS * r + q
                    act.wait_ge(s["h_ps"], g + 1)
                    act.wait_ge(ws_in[q], 64 * (NR * f + r + 1))
                    if late:
                        act.wait_ge(s["y_ps"], g - 1)
                    for n in range(NF):
                        ins = act.activation(hs[:, q % 2, n, :],
                                             bH[:, 2 * (q % 2) + n // 2, ST * (n % 2):ST * (n % 2) + ST],
                                             ACT.Gelu, bias=b1s[:, q, n:n + 1])
                    ins.then_inc(s["h_sb"], 1)

                def run(r, late=True, last=False):
                    for q in range(SLOTS):
                        if not (last and q == SLOTS - 1):
                            x_copy(*before_slot(r, q, -1), late or q >= 1)
                        gelu(r, q, late or q >= 2)

                x_copy(0, 0, late=f > 0)
                run(0, late=f > 0)
                with act.Fori(1, NR - 1) as r:
                    run(r)
                run(NR - 1, last=True)

            ffn(f)

        @block.vector
        def _(dve):
            def gate_weights():
                dve.wait_ge(s["fw_in"], 64)
                dve.tensor_tensor_reduce(wg_sq[:, :], wg_sb[:, :], wg_sb[:, :], 1.0, 0.0, ALU.mult, ALU.add,
                                         wg_n[:, 0:1]).then_inc(s["wg_step"], 1)
                dve.wait_ge(s["wg_step"], 2)
                dve.tensor_scalar(wg_n[:, 2:3], wg_n[:, 1:2], EPS_G, None, ALU.max).then_inc(s["wg_step"], 1)
                dve.wait_ge(s["wg_step"], 3)
                dve.reciprocal(wg_n[:, 3:4], wg_n[:, 2:3]).then_inc(s["wg_step"], 1)
                dve.wait_ge(s["wg_step"], 4)
                dve.tensor_scalar(wg_sq[:, :], wg_sb[:, :], wg_n[:, 3:4], None, ALU.mult).then_inc(s["wg_step"], 1)
                dve.wait_ge(s["wgT_ps"], 1)
                dve.tensor_copy(wgT_s[:, :], bB[0:GD, 0:E]).then_inc(s["wgT_sb"], 1)
                dve.tensor_copy(wredT[:, :], bB[0:GD, 128:256]).then_inc(s["wgT_sb"], 1)
                dve.tensor_copy(b1T[:, :, :].rearrange("p e k -> p (e k)"), bB[:, 64:64 + E * NF]).then_inc(s["wgT_sb"], 1)
                dve.tensor_copy(b2T[:, :], bB[:, 64 + E * NF:64 + E * NF + E]).then_inc(s["wgT_sb"], 1)
                dve.wait_ge(s["wgT_ps"], 2)
                dve.wait_ge(s["f_consts"], 1)
                dve.tensor_copy(w_gate[:, 0:E], bA[:, 0:E]).then_inc(s["wgT_sb"], 1)

            def moments(f):
                n0 = 2 * NT * f
                for i in range(NT):
                    dve.bn_stats(stats[:, i, :], x[:, i, :]).then_inc(s["stat_done"], 1)
                for i in range(NT):
                    dve.wait_ge(s["stat_done"], n0 + i + 1)
                    dve.bn_aggr(mv[:, i, :], stats[:, i, :]).then_inc(s["stat_done"], 1)

            def deviations(f):
                n0 = 2 * NT * f
                dve.wait_ge(s["stat_done"], n0 + 2 * NT)
                dve.tensor_scalar(rstd[:, 1, :], mv[:, :, 1], EPS_LN, None, ALU.add).then_inc(s["rstd_step"], 1)
                dve.wait_ge(s["rstd_step"], 6 * f + 2)
                dve.reciprocal(rstd[:, 3, :], rstd[:, 2, :]).then_inc(s["rstd_step"], 1)
                dve.wait_ge(s["rstd_step"], 6 * f + 3)
                dve.tensor_tensor(rstd[:, 2, :], rstd[:, 3, :], rstd[:, 3, :], ALU.mult).then_inc(s["rstd_step"], 1)
                dve.wait_ge(s["rstd_step"], 6 * f + 4)
                dve.tensor_tensor(rstd[:, 2, :], rstd[:, 2, :], rstd[:, 1, :], ALU.mult).then_inc(s["rstd_step"], 1)
                dve.wait_ge(s["rstd_step"], 6 * f + 5)
                dve.tensor_scalar(rstd[:, 2, :], rstd[:, 2, :], -0.5, 1.5, ALU.mult, ALU.add)\
                    .then_inc(s["rstd_step"], 1)
                dve.wait_ge(s["rstd_step"], 6 * f + 6)
                dve.tensor_tensor(rstd[:, 0, :], rstd[:, 2, :], rstd[:, 3, :], ALU.mult).then_inc(s["rstd_ready"], 1)

            def ffn(f):
                moments(f)
                if f == 0:
                    gate_weights()
                deviations(f)
                dve.wait_ge(s["rstd_ready"], f + 1)
                for i in range(NT):
                    dve.tensor_scalar(xa[:, i, 0:C], x[:, i, :], mv[:, i, 0:1], rstd[:, 0, i:i + 1],
                                      ALU.subtract, ALU.mult).then_inc(s["xnf_done"], 1)
                for h in range(2):
                    dve.wait_ge(s["lg_ps"], B * f + TT * (h + 1))
                    dve.tensor_copy(lgT[:, h, :], bH[:, h, :]).then_inc(s["lgT_sb"], 1)
                for h in range(2):
                    dve.wait_ge(s["lgT_ps"], 2 * f + h + 1)
                    ins = dve.tensor_copy(lg[:, 16 * h:16 * h + 16, :].rearrange("p (g i) e -> p i g e", g=4),
                                          bH[:, 2 + h, :].rearrange("p (i g e) -> p i g e", i=TT, g=4)[:, :, :, 0:E])
                ins.then_inc(s["lg_step"], 1)
                dve.wait_ge(s["lg_step"], 4 * f + 1)
                dve.tensor_reduce(top[:, :], lg[:, :, :], AX.X, ALU.max).then_inc(s["lg_step"], 1)
                dve.wait_ge(s["lg_step"], 4 * f + 2)
                tb = top[:, :].unsqueeze(2).broadcast_to([P, NT, E])
                dve.tensor_tensor(lgx[:, :, :], lg[:, :, :], tb, ALU.subtract).then_inc(s["lg_step"], 1)
                dve.tensor_tensor(hit[:, :, :], lg[:, :, :], tb, ALU.is_equal).then_inc(s["lg_step"], 1)
                dve.wait_ge(s["lg_step"], 4 * f + 4)
                n0 = 5 * f
                dve.tensor_tensor(hit[:, :, :], hit[:, :, :], pref[:, :].unsqueeze(1).broadcast_to([P, NT, E]),
                                  ALU.mult).then_inc(s["oh_done"], 1)
                dve.wait_ge(s["oh_done"], n0 + 1)
                dve.tensor_reduce(first[:, :], hit[:, :, :], AX.X, ALU.max).then_inc(s["oh_done"], 1)
                dve.wait_ge(s["oh_done"], n0 + 2)
                dve.tensor_tensor(oh[:, :, :], pref[:, :].unsqueeze(2).broadcast_to([P, E, NT]),
                                  first[:, :].unsqueeze(1).broadcast_to([P, E, NT]), ALU.is_equal)\
                    .then_inc(s["oh_done"], 1)
                dve.wait_ge(s["lg_exp"], f + 1)
                dve.tensor_reduce(lsum[:, :], lgx[:, :, :], AX.X, ALU.add).then_inc(s["oh_done"], 1)
                dve.wait_ge(s["oh_done"], n0 + 4)
                dve.reciprocal(score[:, :], lsum[:, :]).then_inc(s["oh_done"], 1)
                dve.wait_ge(s["rank_ps"], f + 1)
                at = 12 * f

                def step(ins):
                    nonlocal at
                    at += 1
                    ins.then_inc(s["pos_step"], 1)
                    dve.wait_ge(s["pos_step"], at)

                flat = [t[:, :, :].rearrange("p e i -> p (e i)") for t in (tot, cinc, restart_e)]
                step(dve.tensor_copy(flat[0], bA[:, 256:512]))
                step(dve.tensor_tensor_scan(flat[1], flat[2], flat[0], 0.0, ALU.mult, ALU.add))
                nk = NT * P // ST
                step(dve.tensor_tensor(more[:, :, :], cinc[:, :, NT - 1:NT].broadcast_to([P, E, nk]),
                                       k_at[:, :].unsqueeze(1).broadcast_to([P, E, nk]), ALU.is_gt))
                step(dve.tensor_reduce(n_til[:, :], more[:, :, :], AX.X, ALU.add))
                step(dve.tensor_tensor_scan(ends[:, :], one8[:, :], n_til[:, :], 0.0, ALU.mult, ALU.add))
                step(dve.tensor_tensor(base[:, :], ends[:, :], n_til[:, :], ALU.subtract))
                step(dve.tensor_tensor(p_at[:, :, :], cinc[:, :, :], tot[:, :, :], ALU.subtract))
                step(dve.scalar_tensor_tensor(p_at[:, :, :], base[:, :].unsqueeze(2).broadcast_to([P, E, NT]),
                                              float(ST), p_at[:, :, :], ALU.mult, ALU.add))
                pf = p_at[:, :, :].rearrange("p e i -> p (e i)")
                step(dve.tensor_tensor(pf, bA[:, 0:256], pf, ALU.add))
                step(dve.tensor_tensor(p_at[:, :, :], p_at[:, :, :], oh[:, :, :], ALU.mult))
                step(dve.tensor_reduce(pos_f[:, :], p_at[:, :, :].rearrange("p e i -> p i e"), AX.X, ALU.add))
                dve.tensor_copy(pos[:, :], pos_f[:, :]).then_inc(s["pos_done"], 1)
                step(dve.tensor_tensor(past[:, :, :], tile_at[:, :].unsqueeze(2).broadcast_to([P, NS, E]),
                                       ends[:, :].unsqueeze(1).broadcast_to([P, NS, E]), ALU.is_ge))
                dve.tensor_reduce(texp_f[:, :], past[:, :, :], AX.X, ALU.add).then_inc(s["lg_sum"], 1)
                dve.wait_ge(s["lg_sum"], f + 1)
                dve.tensor_scalar(texp[:, :], texp_f[:, :], float(E - 1), None, ALU.min)\
                    .then_inc(s["texp_done"], 1)

                def y_bias(r, q, late=True):
                    g = NS * f + SLOTS * r + q
                    dve.wait_ge(s["y_ps"], g + 1)
                    dve.wait_ge(ws_in[q], 64 * (NR * f + r + 1))
                    if late:
                        dve.wait_ge(s["o_ps"], g - 1)
                    dve.tensor_scalar(ysT[:, q % 2, :], bY[:, 0:ST], b2s[:, q, 0:1], None, ALU.add)\
                        .then_inc(s["y_sb"], 1)

                def y_out(r, q, late=True):
                    g = NS * f + SLOTS * r + q
                    if late:
                        dve.wait_ge(ys_out[q], 16 * NC2 * (NR * f + r))
                    dve.wait_ge(xs_in[q], 16 * (NR * f + r + 1))
                    dve.tensor_copy(who[:, q, :], xs[:, q, :, C]).then_inc(s["who_done"], 1)
                    dve.wait_ge(s["o_ps"], g + 1)
                    dve.wait_ge(s["who_done"], g + 1)
                    dve.tensor_copy(yo[:, q, :, :].rearrange("p a c -> p (a c)"), bO[:, 0:ST])\
                        .then_inc(s["o_sb"], 1)

                for q in range(SLOTS):
                    y_bias(0, q, late=f > 0 or q >= 2)
                    y_out(0, q, late=f > 0)
                with dve.Fori(1, NR) as r:
                    for q in range(SLOTS):
                        y_bias(r, q)
                        y_out(r, q)
                for i in range(NT):
                    if i % TT == 0:
                        k = i // TT
                        dve.wait_ge(row_in[k], 16 * (2 * f + 1))
                    dve.scalar_tensor_tensor(x[:, i, :], ya[:, i, :], score[:, i:i + 1], x[:, i, :],
                                             ALU.mult, ALU.add).then_inc(s["add_done"], 1)

            ffn(f)

        @block.tensor
        def _(pe):
            if f == 0:
                pe.wait_ge(s["f_consts"], 1)
                pe.wait_ge(s["wg_step"], 5)
                pe.transpose(bB[:, 64:64 + E * NF + E], b_in[:, :], ident[0:E * NF + E, 0:E * NF + E])
                pe.transpose(bB[0:GD, 128:256], wred_sb[:, :], ident[:, :])
                pe.transpose(bB[0:GD, 0:E], wg_sq[:, :], ident[0:E, 0:E]).then_inc(s["wgT_ps"], 1)
                pe.wait_ge(s["wgT_sb"], 4)
                pe.matmul(bA[:, 0:E], wredT[:, :], wgT_s[:, :], start=True, stop=True).then_inc(s["wgT_ps"], 1)
                pe.wait_ge(s["wgT_sb"], 5)

            def ffn(f):
                def turn(g):
                    q = B * f + g
                    pe.wait_ge(s["xnf_done"], NT * f + TT * g + TT)
                    if g >= 2:
                        pe.wait_ge(s["rT_sb"], q - 1)
                    for i in range(TT):
                        ins = pe.transpose((bA, bB)[g % 2][:, P * i:P * i + P], xa[:, TT * g + i, 0:C], ident[:, :])
                    ins.then_inc(s["rT_ps"], 1)

                turn(0)
                for g in range(B):
                    if g + 1 < B:
                        turn(g + 1)
                    pe.wait_ge(s["rT_sb"], B * f + g + 1)
                    at = 32 * (g % 4)
                    pe.matmul(bH[at:at + 32, g // 4, :], w_gate[:, :], rT[:, g % 2, :], start=True, stop=True,
                              skip_group_check=True).then_inc(s["lg_ps"], 1)
                for h in range(2):
                    pe.wait_ge(s["lgT_sb"], 2 * f + h + 1)
                    for i in range(TT):
                        ins = pe.transpose(bH[:, 2 + h, P * i:P * i + P], lgT[:, h, P * i:P * i + P], ident[:, :])
                    ins.then_inc(s["lgT_ps"], 1)
                pe.wait_ge(s["oh_done"], 5 * f + 3)
                ohf = oh[:, :, :].rearrange("p e i -> p (e i)")
                pe.matmul(bA[:, 0:256], before[:, :], ohf, start=True, stop=True)
                pe.matmul(bA[:, 256:512], ones[:, :], ohf, start=True, stop=True).then_inc(s["rank_ps"], 1)
                pe.wait_ge(s["pos_done"], f + 1)

                def turn_x(r, q, late=True):
                    g = NS * f + SLOTS * r + q
                    pe.wait_ge(xs_in[q], 16 * (NR * f + r + 1))
                    if late:
                        pe.wait_ge(s["x_sb"], g)
                    for a in range(NC2):
                        ins = pe.transpose(bA[:, P * a:P * a + P], xs[:, q, a, 0:C], ident[:, :])
                    ins.then_inc(s["x_ps"], 1)

                def up(r, q, late=True):
                    g = NS * f + SLOTS * r + q
                    pe.wait_ge(ws_in[q], 64 * (NR * f + r + 1))
                    pe.wait_ge(s["x_sb"], g + 1)
                    if late:
                        pe.wait_ge(s["h_sb"], g - 1)
                    for n in range(NF):
                        ins = pe.matmul(bH[:, 2 * (q % 2) + n // 2, ST * (n % 2):ST * (n % 2) + ST],
                                        w1s[:, q, P * n:P * n + P], xsT[:, q % 2, :], start=True, stop=True)
                    ins.then_inc(s["h_ps"], 1)

                def down(r, q, late=True):
                    g = NS * f + SLOTS * r + q
                    pe.wait_ge(s["h_sb"], g + 1)
                    if late:
                        pe.wait_ge(s["y_sb"], g)
                    for n in range(NF):
                        ins = pe.matmul(bY[:, 0:ST], w2s[:, q, n, :], hs[:, q % 2, n, :], start=(n == 0),
                                        stop=(n == NF - 1))
                    ins.then_inc(s["y_ps"], 1)

                def turn_y(r, q, late=True):
                    g = NS * f + SLOTS * r + q
                    pe.wait_ge(s["y_sb"], g + 1)
                    if late:
                        pe.wait_ge(s["o_sb"], g)
                    for a in range(NC2):
                        ins = pe.transpose(bO[:, P * a:P * a + P], ysT[:, q % 2, P * a:P * a + P], ident[:, :])
                    ins.then_inc(s["o_ps"], 1)

                def run(r, first=False, last=False):
                    for q in range(SLOTS):
                        if not (last and q == SLOTS - 1):
                            turn_x(*before_slot(r, q, -1))
                        late = f > 0 or not first
                        up(r, q, late or q >= 2)
                        if not first or q >= 2:
                            turn_y(*before_slot(r, q, 2), late or q >= 3)
                        if not first or q >= 1:
                            down(*before_slot(r, q, 1), late or q >= 2)

                turn_x(0, 0, late=f > 0)
                run(0, first=True)
                with pe.Fori(1, NR - 1) as r:
                    run(r)
                run(NR - 1, last=True)
                turn_y(NR - 1, SLOTS - 2)
                down(NR - 1, SLOTS - 1)
                turn_y(NR - 1, SLOTS - 1)

            ffn(f)


def delta_rule(nc, x, row_in, counted, Wq, Wk, Wv, Wgamma, Wf, Wg1, Wg2, Wo, norm_w):
    with ExitStack() as ctx:
        def sb(name, shape, dt=F32):
            return ctx.enter_context(nc.sbuf_tensor("d_" + name, shape, dt))

        def psum(name, shape):
            return ctx.enter_context(nc.psum_tensor("d_" + name, shape, F32))

        def sem(name):
            return ctx.enter_context(nc.semaphore(name))

        head_dram = nc.dram_tensor("head_dram", [3, B, P, T], F32, kind="Internal").ap()
        fg_dram = nc.dram_tensor("fg_dram", [2, B, H, T], F32, kind="Internal").ap()
        o_dram = nc.dram_tensor("o_dram", [B, P, T], F32, kind="Internal").ap()
        s = {}
        for n in """cc_step c_consts stat_done rstd_step rstd_ready cw_in cn_done cT_ps cT_sb
            cq_ps cq_sb cf_ps cf_sb cg_ps cg_sb gw_ps fg_in v_in knorm_step knorm_sq kn_done
            fg_sig decay_step kk_step kk_pool qk_mul qk_sum qk_red w_step u_pool chain fetched po_mul sum_ps o_red v_dve
            gate_sig wo_step ot_ps oy_ps ost_step o_rstd o_sqrt ost_done""".split():
            s[n] = sem("d_" + n)
        (k_in, k_in_0), (q_in, q_in_0), (cs_ps, cs_ps_0), (gw_sb, gw_sb_0) = counted
        og_done = [sem(f"og_done{k}") for k in range(2)]
        cq_out, cf_out = ([sem(f"{n}{k}") for k in range(2)] for n in ("cq_out", "cf_out"))
        o_out = [(cq_out[k], 24 * B) for k in range(2)] + [(cf_out[k], 16 * B) for k in range(2)]
        ident = sb("ident", [P, P])
        ones = sb("ones", [P, P])
        stats = sb("stats", [P, NT, 6])
        mv = sb("mv", [P, NT, 2])
        rstd = sb("rstd", [P, 4, NT])
        wqkv = sb("wqkv", [P, 3, C])
        wfg = sb("wfg", [P, 2 * H])
        wg1 = sb("wg1", [P, HD])
        wg2 = sb("wg2", [HD, C])
        wo = sb("wo", [P, C])
        nw = sb("nw", [P, 1])
        wo_c = sb("wo_c", [P, C])
        og = sb("og", [P, 3, T])
        eps_ln = sb("eps_ln", [P, 1])
        gate = sb("gate", [P, B, T])
        Q = sb("Q", [P, HD, T])
        KVW = sb("KVW", [P, 3, HD, T])
        K, V, W = KVW[:, 0, :, :], KVW[:, 1, :, :], KVW[:, 2, :, :]
        O = W
        fg = sb("fg", [P, 2, T])
        alpha = sb("alpha", [P, T])
        beta = sb("beta", [P, T])
        G = sb("G", [P, CH, CH + 1, NCH])
        LL = sb("LL", [P, CH, CH, NCH])
        QQ = sb("QQ", [P, CH, CH, NCH])
        pb_d = sb("pb_d", [P, CH * HD * NCH])
        pb_p = sb("pb_p", [P, CH * HD * NCH])
        cn = pb_d[:, 0:2 * T].rearrange("p (k i c) -> p k i c", k=2, c=C)
        act3 = (og, pb_d[:, 2 * T:5 * T].rearrange("p (i t) -> p i t", t=T))
        cT = (pb_p[:, 0:T], pb_p[:, T:2 * T])
        fgl = (pb_p[0:2 * H, 2 * T:3 * T], pb_p[0:2 * H, 3 * T:4 * T])
        wg1T = pb_p[0:HD, 4 * T:4 * T + C]
        wg12 = pb_p[:, 5 * T:5 * T + C]
        ob = pb_d[:, :].rearrange("p (b t) -> p b t", b=B)
        ahead = og[:, 2, 0:6 * CH * HD].rearrange("p (a i d j) -> p a i d j", a=2, i=3, d=HD)
        g_ahead = sb("g_ahead", [P, 2])
        S = sb("S", [P, 4, HD, HD])
        uw = sb("uw", [P, CH, HD])
        sr = sb("sr", [P, HD, HD])
        ost = sb("ost", [P, NT, 6])
        omv = sb("omv", [P, NT, 2])
        ors = sb("ors", [P, 2, NT])
        c0 = psum("c0", [P, T])
        c1 = psum("c1", [P, T])
        c2 = psum("c2", [P, T])
        c3 = psum("c3", [P, T])
        c4 = psum("c4", [P, T])
        c5 = psum("c5", [P, T])
        c6 = psum("c6", [P, T])
        cqkv = (c1, c2, c3)
        block = ctx.enter_context(nc.Block())

        def chunked(t, first=0, n=CH):
            return t[:, :, :].rearrange("p d (c j) -> p j c d", j=CH)[:, first:first + n]

        PIECES = [(j, lo, min(4, j + 1 - lo)) for j in range(CH) for lo in range(0, j + 1, 4)]
        VP = 4

        def half(k, n):
            at = 2048 * (k % 2)
            return pb_p[:, at:at + 512 * n].rearrange("p (i c d) -> p i c d", c=NCH, d=HD)

        def piece_sum(k, n):
            at = 256 * (k % 2)
            return (c0, c1, c2, c3, c4, c6)[k // 2][:, at:at + NCH * n].rearrange("p (i c) -> p i c", c=NCH)

        def gated(engine, b):
            engine.wait_ge(row_in[b], 32)
            engine.tensor_tensor(ob[:, b, :], ob[:, b, :], gate[:, b, :], ALU.mult).then_inc(og_done[b % 2], 1)

        def products_of(g, a):
            return (pb_p, pb_d)[g % 2][:, 1024 * a:1024 * a + 1024].rearrange("p (k j v) -> p j v k", k=16, v=HD)

        @block.sync
        def _(sp):
            for i, w in enumerate((Wq, Wk, Wv)):
                sp.dma_start(wqkv[:, i, :], w).then_inc(s["cw_in"], 16)
            sp.dma_start(wfg[:, 0:H], Wf).then_inc(s["cw_in"], 16)
            sp.dma_start(wfg[:, H:2 * H], Wgamma).then_inc(s["cw_in"], 16)
            sp.dma_start(wg1[:, :], Wg1).then_inc(s["cw_in"], 16)
            sp.dma_start(wg2[:, :], Wg2).then_inc(s["cw_in"], 16)
            sp.dma_start(wo[:, :], Wo).then_inc(s["cw_in"], 16)
            sp.dma_start(nw[:, :], norm_w.rearrange("(p a) -> p a", a=1)).then_inc(s["cw_in"], 16)

            def relayout():
                for b in range(B):
                    sp.wait_ge(s["cq_sb"], 3 * b + 3)
                    for i in range(3):
                        sp.dma_start(head_dram[i, b], act3[b % 2][:, i, :]).then_inc(cq_out[b % 2], 16)
                    sp.wait_ge(s["cf_sb"], b + 1)
                    for i in range(2):
                        sp.dma_start(fg_dram[i, b], fgl[b % 2][H * i:H * i + H, :]).then_inc(cf_out[b % 2], 16)
                for k in range(2):
                    sp.wait_ge(cf_out[k], 16 * B)
                for i in range(2):
                    sp.dma_start(fg[:, i, :], fg_dram[i].rearrange("b h t -> (b h) t")).then_inc(s["fg_in"], 16)
                for k in range(2):
                    sp.wait_ge(cq_out[k], 24 * B)
                for i, t, loaded in ((1, K, k_in), (0, Q, q_in), (2, V, s["v_in"])):
                    sp.dma_start(t[:, :, :].rearrange("p d t -> p (d t)"),
                                 head_dram[i].rearrange("b (h d) t -> (b h) (d t)", d=HD)).then_inc(loaded, 16)

            def back():
                sp.wait_ge(s["o_red"], NCH // 4)
                for b in range(B):
                    sp.dma_start(o_dram[b].rearrange("(h d) t -> h (d t)", d=HD),
                                 O[H * b:H * b + H, :, :].rearrange("p d t -> p (d t)")).then_inc(o_out[b // 2][0], 16)
                for b in range(B):
                    sp.wait_ge(o_out[b // 2][0], o_out[b // 2][1] + 32)
                    sp.dma_start(ob[:, b, :], o_dram[b]).then_inc(row_in[b], 16)

            relayout()
            back()

        @block.gpsimd
        def _(pool):
            st = 0

            def step(ins):
                nonlocal st
                st += 1
                ins.then_inc(s["cc_step"], 1)
                pool.wait_ge(s["cc_step"], st)

            step(pool.memset(ident[:, :], 0.0))
            step(pool.memset(ones[:, :], 1.0 / C))
            step(pool.memset(eps_ln[:, :], EPS_LN))
            step(pool.memset(QQ[:, :, :, :].rearrange("p j i c -> p (j i c)"), 0.0))
            step(pool.memset(G[:, :, :, :].rearrange("p j i c -> p (j i c)"), 1.0))
            step(pool.memset(S[:, 0, :, :].rearrange("p v k -> p (v k)"), 0.0))
            pool.affine_select(out=ident[:, :], in_=ident[:, :], compare_op=ALU.not_equal, fill=1.0,
                               base=0, pattern=[[-1, P]], channel_multiplier=1).then_inc(s["c_consts"], 1)

            def products():
                pool.wait_ge(q_in, q_in_0 + 16)
                pool.wait_ge(s["kn_done"], 1)
                for k, (j, lo, n) in enumerate(PIECES):
                    if k >= 2:
                        pool.wait_ge(s["qk_sum"], k - 1)
                    pool.tensor_tensor(half(k, n), chunked(K, lo, n), chunked(Q, j, 1).broadcast_to([P, n, NCH, HD]),
                                       ALU.mult).then_inc(s["qk_mul"], 1)
                pool.wait_ge(s["kk_step"], 1)
                pool.wait_ge(s["qk_sum"], len(PIECES))
                pool.wait_ge(s["v_in"], 16)
                n = 0
                for i in range(CH - 1):
                    m = CH - 1 - i
                    t = pb_p[:, 0:NCH * VP * m].rearrange("p (j c d) -> p j c d", c=NCH, d=VP)
                    if n:
                        pool.wait_ge(s["u_pool"], n)
                    pool.tensor_tensor(t, LL[:, i + 1:CH, i, :].unsqueeze(3).broadcast_to([P, m, NCH, VP]),
                                       chunked(V, i, 1)[:, :, :, 0:VP].broadcast_to([P, m, NCH, VP]), ALU.mult)\
                        .then_inc(s["u_pool"], 1)
                    pool.wait_ge(s["u_pool"], n + 1)
                    pool.tensor_tensor(chunked(V, i + 1, m)[:, :, :, 0:VP], chunked(V, i + 1, m)[:, :, :, 0:VP], t,
                                       ALU.add)\
                        .then_inc(s["u_pool"], 1)
                    n += 2

            def outputs(r, a):
                c = 8 * r + a
                cs = bass.ds(CH * c, CH)
                po = products_of(a // 4, a % 4)
                pool.wait_ge(s["chain"], 6 * c + 1)
                if a % 4 == 0 and not (isinstance(r, int) and r == 0):
                    pool.wait_ge(s["sum_ps"], 2 * r + a // 4 - 1)
                pool.tensor_tensor(po[:, :, :, 0:8],
                                   Q[:, :, cs].rearrange("p k j -> p j k").unsqueeze(2).broadcast_to([P, CH, HD, HD]),
                                   S[:, a % 4, :, :].unsqueeze(1).broadcast_to([P, CH, HD, HD]), ALU.mult)\
                    .then_inc(s["po_mul"], 1)
                pool.wait_ge(s["chain"], 6 * c + 4)
                pool.tensor_tensor(po[:, :, :, 8:16],
                                   QQ[:, :, :, bass.ds(c, 1)].rearrange("p j i c -> p j (i c)").unsqueeze(2)
                                   .broadcast_to([P, CH, HD, CH]),
                                   ahead[:, a % 2, 1].unsqueeze(1).broadcast_to([P, CH, HD, CH]), ALU.mult)\
                    .then_inc(s["po_mul"], 1)

            products()
            for a in range(8):
                outputs(0, a)
            with pool.Fori(1, NCH // 8) as r:
                for a in range(8):
                    outputs(r, a)
            pool.wait_ge(s["gate_sig"], 1)
            for b in range(1, B, 2):
                gated(pool, b)

        @block.scalar
        def _(act):
            act.wait_ge(s["rstd_step"], 1)
            act.activation(rstd[:, 2, :], rstd[:, 1, :], ACT.Sqrt).then_inc(s["rstd_step"], 1)

            def turned(b):
                act.wait_ge(s["cT_ps"], b + 1)
                if b >= 2:
                    act.wait_ge(s["cg_ps"], b - 1)
                act.activation(cT[b % 2], (c0, c6)[b % 2][:, :], ACT.Copy).then_inc(s["cT_sb"], 1)

            turned(0)
            for b in range(B):
                if b >= 2:
                    act.wait_ge(cf_out[b % 2], 32 * (b // 2))
                    act.wait_ge(cq_out[b % 2], 48 * (b // 2))
                for i in range(3):
                    act.wait_ge(s["cq_ps"], 3 * b + i + 1)
                    act.activation(act3[b % 2][:, i, :], cqkv[i][:, :], ACT.Silu).then_inc(s["cq_sb"], 1)
                    if i == 0 and b + 1 < B:
                        turned(b + 1)
                act.wait_ge(s["cf_ps"], b + 1)
                act.activation(fgl[b % 2], c4[0:2 * H, :], ACT.Copy).then_inc(s["cf_sb"], 1)
                act.wait_ge(s["cg_ps"], b + 1)
                act.activation(gate[:, b, :], c5[:, :], ACT.Copy).then_inc(s["cg_sb"], 1)
            act.wait_ge(s["fg_in"], 32)
            act.activation(fg[:, :, :].rearrange("p a t -> p (a t)"), fg[:, :, :].rearrange("p a t -> p (a t)"),
                           ACT.Sigmoid).then_inc(s["fg_sig"], 1)
            act.wait_ge(k_in, k_in_0 + 16)
            act.activation(pb_d[:, 0:HD * T], K[:, :, :].rearrange("p d t -> p (d t)"), ACT.Square)\
                .then_inc(s["knorm_step"], 1)
            act.wait_ge(s["knorm_step"], 2)
            act.activation(og[:, 1, :], og[:, 0, :], ACT.Sqrt).then_inc(s["knorm_sq"], 1)
            act.wait_ge(s["cg_sb"], B)
            act.activation(gate[:, :, :].rearrange("p b t -> p (b t)"), gate[:, :, :].rearrange("p b t -> p (b t)"),
                           ACT.Sigmoid).then_inc(s["gate_sig"], 1)

            def keep_out(r, a):
                g = 2 * r + a
                act.wait_ge(s["sum_ps"], g + 1)
                act.activation(O[:, :, bass.ds(4 * CH * g, 4 * CH)],
                               (c5, c6)[a][:, 0:256].rearrange("p (t v) -> p v t", v=HD), ACT.Copy)\
                    .then_inc(s["o_red"], 1)

            def fetch(r, a):
                c = 8 * r + a
                if isinstance(r, int) and a < 2:
                    act.wait_ge(s["chain"], 1)
                else:
                    act.wait_ge(s["chain"], 6 * c - 5)
                    act.wait_ge(s["po_mul"], 2 * c - 2)
                act.activation(g_ahead[:, a % 2:a % 2 + 1], G[:, CH - 1, 0, bass.ds(c, 1)], ACT.Copy)
                act.activation(ahead[:, a % 2], KVW[:, :, :, bass.ds(CH * c, CH)], ACT.Copy).then_inc(s["fetched"], 1)

            def round_of(r, first=False):
                for a in range(8):
                    fetch(r, a)
                    if a % 4 == 0 and not first:
                        keep_out(r - 1, a // 4)

            round_of(0, first=True)
            with act.Fori(1, NCH // 8) as r:
                round_of(r)
            for a in range(2):
                keep_out(NCH // 8 - 1, a)
            for b in range(B):
                act.wait_ge(s["ost_step"], b + 1)
                act.activation(ors[:, 0, TT * b:TT * b + TT], omv[:, TT * b:TT * b + TT, 1], ACT.Sqrt,
                               bias=eps_ln[:, 0:1]).then_inc(s["o_sqrt"], 1)

        @block.vector
        def _(dve):
            for i in range(NT):
                dve.bn_stats(stats[:, i, :], x[:, i, :]).then_inc(s["stat_done"], 1)
            for i in range(NT):
                dve.wait_ge(s["stat_done"], i + 1)
                dve.bn_aggr(mv[:, i, :], stats[:, i, :]).then_inc(s["stat_done"], 1)
            dve.wait_ge(s["stat_done"], 2 * NT)
            dve.tensor_scalar(rstd[:, 1, :], mv[:, :, 1], EPS_LN, None, ALU.add).then_inc(s["rstd_step"], 1)
            dve.wait_ge(s["rstd_step"], 2)
            dve.reciprocal(rstd[:, 3, :], rstd[:, 2, :]).then_inc(s["rstd_step"], 1)
            dve.wait_ge(s["rstd_step"], 3)
            dve.tensor_tensor(rstd[:, 2, :], rstd[:, 3, :], rstd[:, 3, :], ALU.mult).then_inc(s["rstd_step"], 1)
            dve.wait_ge(s["rstd_step"], 4)
            dve.tensor_tensor(rstd[:, 2, :], rstd[:, 2, :], rstd[:, 1, :], ALU.mult).then_inc(s["rstd_step"], 1)
            dve.wait_ge(s["rstd_step"], 5)
            dve.tensor_scalar(rstd[:, 2, :], rstd[:, 2, :], -0.5, 1.5, ALU.mult, ALU.add).then_inc(s["rstd_step"], 1)
            dve.wait_ge(s["rstd_step"], 6)
            dve.tensor_tensor(rstd[:, 0, :], rstd[:, 2, :], rstd[:, 3, :], ALU.mult).then_inc(s["rstd_ready"], 1)
            dve.wait_ge(s["rstd_ready"], 1)
            dve.wait_ge(s["gw_ps"], 1)
            dve.tensor_copy(wg1T, c5[0:HD, 0:C]).then_inc(gw_sb, 1)
            for b in range(B):
                if b == 1:
                    dve.wait_ge(s["gw_ps"], 2)
                    dve.tensor_copy(wg12, c5[:, C:2 * C]).then_inc(gw_sb, 1)
                if b >= 2:
                    dve.wait_ge(s["cT_ps"], b - 1)
                for i in range(TT):
                    j = TT * b + i
                    dve.tensor_scalar(cn[:, b % 2, i, :], x[:, j, :], mv[:, j, 0:1], rstd[:, 0, j:j + 1],
                                      ALU.subtract, ALU.mult).then_inc(s["cn_done"], 1)

            dve.wait_ge(s["fg_sig"], 1)
            dve.wait_ge(s["c_consts"], 1)
            dn = 0

            def dstep(ins):
                nonlocal dn
                dn += 1
                ins.then_inc(s["decay_step"], 1)
                dve.wait_ge(s["decay_step"], dn)

            f, gm = fg[:, 0, :], fg[:, 1, :]
            fj = f.rearrange("p (c j) -> p j c", j=CH)
            dstep(dve.scalar_tensor_tensor(alpha[:, :], f, -1.0, f, ALU.mult, ALU.mult))
            dstep(dve.tensor_tensor(alpha[:, :], alpha[:, :], gm, ALU.mult))
            dstep(dve.tensor_copy(G[:, 0, 0, :], fj[:, 0, :]))
            for j in range(1, CH):
                dstep(dve.tensor_tensor(G[:, j, 0:j + 1, :], G[:, j - 1, 0:j + 1, :],
                                        fj[:, j:j + 1, :].broadcast_to([P, j + 1, NCH]), ALU.mult))
            aj = alpha[:, :].rearrange("p (c j) -> p j c", j=CH)
            bj = beta[:, :].rearrange("p (c j) -> p j c", j=CH)
            dstep(dve.tensor_copy(beta[:, :], alpha[:, :]))
            dstep(dve.tensor_tensor(bj[:, 1:CH, :], aj[:, 1:CH, :], G[:, 0:CH - 1, 0, :], ALU.mult))
            dve.wait_ge(s["knorm_step"], 1)
            dve.tensor_reduce(og[:, 0, :], pb_d[:, 0:HD * T].rearrange("p (d t) -> p t d", d=HD), AX.X, ALU.add)\
                .then_inc(s["knorm_step"], 1)
            dve.wait_ge(s["knorm_sq"], 1)
            dve.tensor_scalar(og[:, 0, :], og[:, 1, :], EPS_K, None, ALU.max).then_inc(s["knorm_step"], 1)
            dve.wait_ge(s["knorm_step"], 3)
            dve.reciprocal(og[:, 1, :], og[:, 0, :]).then_inc(s["knorm_step"], 1)
            dve.wait_ge(s["knorm_step"], 4)
            dve.tensor_tensor(K[:, :, :], K[:, :, :], og[:, 1, :].unsqueeze(1).broadcast_to([P, HD, T]), ALU.mult)\
                .then_inc(s["kn_done"], 1)
            dve.wait_ge(s["kn_done"], 1)
            dstep(dve.tensor_tensor(W[:, :, :], K[:, :, :], beta[:, :].unsqueeze(1).broadcast_to([P, HD, T]),
                                    ALU.mult))

            kn = 0
            for j in range(CH):
                if j:
                    t = pb_d[:, 0:512 * j].rearrange("p (i c d) -> p i c d", c=NCH, d=HD)
                    dve.tensor_tensor(t, chunked(K, 0, j), chunked(K, j, 1).broadcast_to([P, j, NCH, HD]), ALU.mult)\
                        .then_inc(s["kk_pool"], 1)
                    dve.wait_ge(s["kk_pool"], 3 * j - 2)
                    dve.tensor_reduce(LL[:, j, 0:j, :], t, AX.X, ALU.add).then_inc(s["kk_pool"], 1)
                    dve.wait_ge(s["kk_pool"], 3 * j - 1)
                    dve.tensor_tensor(LL[:, j, 0:j, :], LL[:, j, 0:j, :], G[:, j - 1, 1:j + 1, :], ALU.mult)\
                        .then_inc(s["kk_pool"], 1)
                    dve.wait_ge(s["kk_pool"], 3 * j)
                    ins = dve.tensor_tensor(LL[:, j, 0:j, :], LL[:, j, 0:j, :],
                                            aj[:, j:j + 1, :].broadcast_to([P, j, NCH]), ALU.mult)
                    if j == CH - 1:
                        ins.then_inc(s["kk_step"], 1)
            dve.wait_ge(s["kk_step"], 1)
            dve.wait_ge(s["v_in"], 16)
            wn = 0
            for i in range(CH - 1):
                m = CH - 1 - i
                t = pb_d[:, 0:512 * m].rearrange("p (j c d) -> p j c d", c=NCH, d=HD)
                if wn:
                    dve.wait_ge(s["w_step"], wn)
                    dve.wait_ge(s["v_dve"], 2 * i)
                dve.tensor_tensor(t, LL[:, i + 1:CH, i, :].unsqueeze(3).broadcast_to([P, m, NCH, HD]),
                                  chunked(W, i, 1).broadcast_to([P, m, NCH, HD]), ALU.mult).then_inc(s["w_step"], 1)
                dve.wait_ge(s["w_step"], wn + 1)
                dve.tensor_tensor(chunked(W, i + 1, m), chunked(W, i + 1, m), t, ALU.add).then_inc(s["w_step"], 1)
                wn += 2
                nv = HD - VP
                t = pb_d[:, 0:NCH * nv * m].rearrange("p (j c d) -> p j c d", c=NCH, d=nv)
                dve.wait_ge(s["w_step"], wn)
                dve.tensor_tensor(t, LL[:, i + 1:CH, i, :].unsqueeze(3).broadcast_to([P, m, NCH, nv]),
                                  chunked(V, i, 1)[:, :, :, VP:HD].broadcast_to([P, m, NCH, nv]), ALU.mult)\
                    .then_inc(s["v_dve"], 1)
                dve.wait_ge(s["v_dve"], 2 * i + 1)
                dve.tensor_tensor(chunked(V, i + 1, m)[:, :, :, VP:HD], chunked(V, i + 1, m)[:, :, :, VP:HD], t,
                                  ALU.add).then_inc(s["v_dve"], 1)
            dve.wait_ge(s["qk_sum"], len(PIECES))
            for k, (j, lo, n) in enumerate(PIECES):
                dve.tensor_tensor(QQ[:, j, lo:lo + n, :], piece_sum(k, n), G[:, j, lo + 1:lo + n + 1, :], ALU.mult)\
                    .then_inc(s["qk_red"], 1)
            fo = G[:, :, 0, :].rearrange("p j c -> p c j")
            ke = G[:, CH - 1, 1:CH + 1, :].rearrange("p j c -> p c j")
            for d in range(HD):
                qd = Q[:, d, :].rearrange("p (c j) -> p c j", j=CH)
                dve.tensor_tensor(qd, qd, fo, ALU.mult).then_inc(s["w_step"], 1)
                kd = K[:, d, :].rearrange("p (c j) -> p c j", j=CH)
                dve.tensor_tensor(kd, kd, ke, ALU.mult).then_inc(s["w_step"], 1)
            dve.wait_ge(s["w_step"], wn + 2 * HD)
            dve.wait_ge(s["qk_red"], len(PIECES))
            dve.wait_ge(s["u_pool"], 2 * (CH - 1))
            dve.wait_ge(s["v_dve"], 2 * (CH - 1))

            def chain(r, a, first=False):
                c = 4 * r + a
                n = 6 * c
                pu = og[:, 0, :].rearrange("p (j v k) -> p j v k", v=HD, k=HD)
                k_c, u, w_c = (ahead[:, a % 2, i] for i in range(3))
                dve.wait_ge(s["fetched"], c + 1)
                if not first:
                    dve.wait_ge(s["chain"], n + 1)
                dve.tensor_tensor(pu, w_c.rearrange("p k j -> p j k").unsqueeze(2)
                                  .broadcast_to([P, CH, HD, HD]),
                                  S[:, a, :, :].unsqueeze(1).broadcast_to([P, CH, HD, HD]), ALU.mult)\
                    .then_inc(s["chain"], 1)
                if not (isinstance(r, int) and 4 * r + a < 3):
                    dve.wait_ge(s["po_mul"], 2 * c - 5)
                dve.wait_ge(s["chain"], n + 2)
                dve.tensor_reduce(uw[:, :, :], pu, AX.X, ALU.add).then_inc(s["chain"], 1)
                dve.wait_ge(s["chain"], n + 3)
                dve.tensor_tensor(u, u, uw[:, :, :].rearrange("p j v -> p v j"), ALU.add).then_inc(s["chain"], 1)
                dve.wait_ge(s["chain"], n + 4)
                ps = og[:, 1, :].rearrange("p (v k j) -> p v k j", k=HD, j=CH)
                dve.tensor_tensor(ps, k_c.unsqueeze(1).broadcast_to([P, HD, HD, CH]),
                                  u.unsqueeze(2).broadcast_to([P, HD, HD, CH]), ALU.mult).then_inc(s["chain"], 1)
                dve.wait_ge(s["chain"], n + 5)
                dve.tensor_reduce(sr[:, :, :], ps, AX.X, ALU.add).then_inc(s["chain"], 1)
                dve.wait_ge(s["chain"], n + 6)
                b = (a + 1) % 4
                dve.scalar_tensor_tensor(S[:, b, :, :].rearrange("p v k -> p (v k)"),
                                         S[:, a, :, :].rearrange("p v k -> p (v k)"),
                                         g_ahead[:, a % 2:a % 2 + 1], sr[:, :, :].rearrange("p v k -> p (v k)"),
                                         ALU.mult, ALU.add).then_inc(s["chain"], 1)

            dve.sem_inc(s["chain"], 1)
            chain(0, 0, first=True)
            for a in range(1, 4):
                chain(0, a)
            with dve.Fori(1, NCH // 4) as r:
                for a in range(4):
                    chain(r, a)

            dve.wait_ge(s["cw_in"], 144)
            dve.tensor_scalar(wo[:, :], wo[:, :], nw[:, 0:1], None, ALU.mult).then_inc(s["wo_step"], 1)
            dve.wait_ge(cs_ps, cs_ps_0 + 1)
            dve.tensor_tensor(wo_c[:, :], wo[:, :], c0[:, 0:C], ALU.subtract).then_inc(s["wo_step"], 1)
            dve.wait_ge(s["gate_sig"], 1)
            for b in range(0, B, 2):
                gated(dve, b)

            def moments(b):
                tp = (c1, c3)[b % 2]
                dve.wait_ge(s["ot_ps"], b + 1)
                for i in range(TT):
                    ins = dve.bn_stats(ost[:, TT * b + i, :], tp[:, P * i:P * i + P])
                ins.then_inc(s["stat_done"], 1)
                dve.wait_ge(s["stat_done"], 2 * NT + b + 1)
                for i in range(TT):
                    ins = dve.bn_aggr(omv[:, TT * b + i, :], ost[:, TT * b + i, :])
                ins.then_inc(s["ost_step"], 1)

            def add_in(b):
                yp = (c2, c4)[b % 2]
                at = slice(TT * b, TT * b + TT)
                dve.wait_ge(s["o_sqrt"], b + 1)
                dve.reciprocal(ors[:, 1, at], ors[:, 0, at]).then_inc(s["o_rstd"], 1)
                dve.wait_ge(s["oy_ps"], b + 1)
                dve.wait_ge(s["o_rstd"], b + 1)
                for i in range(TT):
                    j = TT * b + i
                    ins = dve.scalar_tensor_tensor(x[:, j, :], yp[:, P * i:P * i + P], ors[:, 1, j:j + 1],
                                                   x[:, j, :], ALU.mult, ALU.add)
                ins.then_inc(s["ost_done"], 1)

            moments(0)
            for b in range(1, B):
                moments(b)
                add_in(b - 1)
            add_in(B - 1)

        @block.tensor
        def _(pe):
            pe.wait_ge(s["c_consts"], 1)
            pe.wait_ge(s["cw_in"], 144)
            pe.transpose(c5[0:HD, 0:C], wg1[:, :], ident[:, :]).then_inc(s["gw_ps"], 1)
            pe.wait_ge(gw_sb, gw_sb_0 + 1)
            pe.matmul(c5[:, C:2 * C], wg1T, wg2[:, :], start=True, stop=True).then_inc(s["gw_ps"], 1)

            def turn(b):
                pe.wait_ge(s["cn_done"], TT * b + TT)
                if b >= 2:
                    pe.wait_ge(s["cT_sb"], b - 1)
                for i in range(TT):
                    ins = pe.transpose((c0, c6)[b % 2][:, P * i:P * i + P], cn[:, b % 2, i, :], ident[:, :])
                ins.then_inc(s["cT_ps"], 1)

            turn(0)
            for b in range(B):
                if b + 1 < B:
                    turn(b + 1)
                pe.wait_ge(s["cT_sb"], b + 1)
                for i in range(3):
                    if b:
                        pe.wait_ge(s["cq_sb"], 3 * (b - 1) + i + 1)
                    pe.matmul(cqkv[i][:, :], wqkv[:, i, :], cT[b % 2], start=True, stop=True).then_inc(s["cq_ps"], 1)
                if b:
                    pe.wait_ge(s["cf_sb"], b)
                pe.matmul(c4[0:2 * H, :], wfg[:, :], cT[b % 2], start=True, stop=True).then_inc(s["cf_ps"], 1)
                if b == 0:
                    pe.wait_ge(gw_sb, gw_sb_0 + 2)
                else:
                    pe.wait_ge(s["cg_sb"], b)
                pe.matmul(c5[:, :], wg12, cT[b % 2], start=True, stop=True).then_inc(s["cg_ps"], 1)
            pe.wait_ge(s["cg_sb"], B)
            pe.wait_ge(s["cq_sb"], 3 * B)
            pe.wait_ge(s["cf_sb"], B)
            for k, (j, lo, n) in enumerate(PIECES):
                pe.wait_ge(s["qk_mul"], k + 1)
                po = half(k, n)
                for d in range(HD):
                    ins = pe.matmul(piece_sum(k, n), ident[:, :],
                                    po[:, :, :, d], start=(d == 0), stop=(d == HD - 1))
                ins.then_inc(s["qk_sum"], 1)

            def add_up(r, a):
                g = 2 * r + a
                pe.wait_ge(s["po_mul"], 8 * g + 8)
                if not (isinstance(r, int) and r == 0):
                    pe.wait_ge(s["o_red"], g - 1)
                po = (pb_p, pb_d)[a][:, :].rearrange("p (c k x) -> p k c x", k=16, x=64)
                for k in range(16):
                    ins = pe.matmul((c5, c6)[a][:, 0:256].rearrange("p (c x) -> p c x", x=64), ident[:, :],
                                    po[:, k], start=(k == 0), stop=(k == 15))
                ins.then_inc(s["sum_ps"], 1)

            for a in range(2):
                add_up(0, a)
            with pe.Fori(1, NCH // 8) as r:
                for a in range(2):
                    add_up(r, a)
            pe.wait_ge(s["wo_step"], 1)
            pe.matmul(c0[:, 0:C], ones[:, :], wo[:, :], start=True, stop=True).then_inc(cs_ps, 1)
            pe.wait_ge(s["wo_step"], 2)
            for b in range(B):
                tp, yp = ((c1, c2), (c3, c4))[b % 2]
                pe.wait_ge(og_done[b % 2], b // 2 + 1)
                if b >= 2:
                    pe.wait_ge(s["ost_step"], b - 1)
                for i in range(TT):
                    ins = pe.transpose(tp[:, P * i:P * i + P], ob[:, b, P * i:P * i + P], ident[:, :])
                ins.then_inc(s["ot_ps"], 1)
                if b >= 2:
                    pe.wait_ge(s["ost_done"], b - 1)
                for i in range(TT):
                    ins = pe.matmul(yp[:, P * i:P * i + P], ob[:, b, P * i:P * i + P], wo_c[:, :],
                                    start=True, stop=True)
                ins.then_inc(s["oy_ps"], 1)


def build(nc, xin, W, Wq, Wk, Wv, Wgamma, Wf, Wg1, Wg2, Wo, norm_w, w_red, wg, w1, b1, w2, b2, out):
    with ExitStack() as ctx:
        def sb(name, shape, dt=F32):
            return ctx.enter_context(nc.sbuf_tensor(name, shape, dt))

        def sem(name):
            return ctx.enter_context(nc.semaphore(name))

        xs_dram = [nc.dram_tensor(f"xs_dram{i}", [NS * ST, C + 1], F32, kind="Internal").ap() for i in range(2)]
        ys_dram = [nc.dram_tensor(f"ys_dram{i}", [B * T + SPAN, C], F32, kind="Internal").ap() for i in range(2)]
        x = sb("x", [P, NT, C])
        s = {}
        for n in """f_consts fc_step stat_done rstd_step rstd_ready xnf_done
            rT_ps rT_sb lgT_ps lgT_sb id_done who_done give lg_ps lg_step lg_exp lg_sum oh_done rank_ps pos_step pos_done texp_done
            zero_done scat_done x_ps x_sb h_ps h_sb y_ps y_sb o_ps o_sb add_done
            x_out fw_in wg_step wgT_ps wgT_sb""".split():
            s[n] = sem("f_" + n)
        for n, m in (("xs_in", SLOTS), ("ws_in", SLOTS), ("ys_out", SLOTS), ("row_in", B)):
            s[n] = [sem(f"f_{n}{k}") for k in range(m)]
        keep = {
            "ident": sb("ident", [P, P]),
            "before": sb("before", [P, P]),
            "ones": sb("ones", [P, P]),
            "blank": sb("blank", [P, SPAN // P, C + 1]),
            "w_gate": sb("w_gate", [P, 32]),
            "pref": sb("pref", [P, E]),
            "restart_e": sb("restart_e", [P, E, NT]),
            "tile_at": sb("tile_at", [P, NS]),
            "k_at": sb("k_at", [P, NT * P // ST]),
            "wred_sb": sb("wred_sb", [P, GD]),
            "wgT_s": sb("wgT_s", [GD, E]),
            "b1T": sb("b1T", [P, E, NF]),
            "b2T": sb("b2T", [P, E]),
            "one8": sb("one8", [P, E]),
        }
        attention(nc, x, xin, W)
        experts(nc, x, xs_dram, ys_dram, s, keep, 0, w_red, wg, w1, b1, w2, b2, out)
        counted = ((s["fw_in"], 64), (s["zero_done"], 32 * NR), (s["wgT_ps"], 2), (s["wgT_sb"], 5))
        delta_rule(nc, x, s["row_in"], counted, Wq, Wk, Wv, Wgamma, Wf, Wg1, Wg2, Wo, norm_w)
        experts(nc, x, xs_dram, ys_dram, s, keep, 1, w_red, wg, w1, b1, w2, b2, out)


_INS = ["L0_attn_a_x", "L0_attn_a_W", "L0_attn_b_Wq", "L0_attn_b_Wk", "L0_attn_b_Wv", "L0_attn_b_Wgamma",
        "L0_attn_b_Wf", "L0_attn_b_Wg1", "L0_attn_b_Wg2", "L0_attn_b_Wo", "L0_attn_b_norm_w", "L0_ffn_w_red",
        "L0_ffn_wg", "L0_ffn_w1", "L0_ffn_b1", "L0_ffn_w2", "L0_ffn_b2"]


def kernel(**inputs):
    import numpy as _np
    import concourse.bacc as _bacc
    from concourse import mybir as _mybir
    from concourse.bass_utils import run_bass_kernel_spmd as _run

    nc = _bacc.Bacc("TRN2", target_bir_lowering=False, num_devices=1)
    arrays, args = {}, []
    for name in _INS:
        a = _np.ascontiguousarray(inputs[name])
        arrays[f"in_{name}_dram"] = a
        args.append(nc.dram_tensor(f"in_{name}_dram", a.shape, _mybir.dt.from_np(a.dtype), kind="ExternalInput").ap())
    out = nc.dram_tensor("out_0_dram", (B, T, C), F32, kind="ExternalOutput").ap()
    build(nc, *args, out)
    r = _run(nc, [arrays], core_ids=[0])
    return r.results[0]["out_0_dram"]
```
